# Optimizing a Trainium2 kernel written in Bass

```python
import numpy as np
import jax
import jax.numpy as jnp

def _softmax(x, axis=-1):
    return jax.nn.softmax(x, axis=axis)

def _gelu(x):
    return jax.nn.gelu(x, approximate=True)

def _silu(x):
    return jax.nn.silu(x)

def _sigmoid(x):
    return jax.nn.sigmoid(x)

def _layernorm(x, axis=-1, eps=1e-05):
    m = jnp.mean(x, axis=axis, keepdims=True)
    v = jnp.var(x, axis=axis, keepdims=True)
    return (x - m) / jnp.sqrt(v + eps)

def _scatter_add(tgt, idx, src, axis=0):
    return tgt.at[idx].add(src)

def _segment_sum(src, seg, n):
    return jax.ops.segment_sum(src, seg, n)
kernel_name = 'mk_flamingo_gated_d1_seqx_r2_f6197a'

def setup_inputs(seed: int=0):
    np.random.seed(seed)
    _w = jnp.asarray

    def _rec_inputs():
        import jax
        import jax.numpy as jnp
        _rk = jax.random.key(seed)
        x = -0.0005207 + 1.001 * jax.random.normal(jax.random.fold_in(_rk, 1), (2, 2048, 512), jnp.float32)
        _lenS = 2048 - jax.random.randint(jax.random.fold_in(_rk, 7), (2,), 0, max(1, 2048 // 4) + 1, jnp.int32)
        _lenS2 = 128 - jax.random.randint(jax.random.fold_in(_rk, 8), (2,), 0, max(1, 128 // 4) + 1, jnp.int32)
        _ctx_1024P = jax.random.normal(jax.random.fold_in(_rk, 11), (2, 16, 512), jnp.float32)
        _ctx_1024c = jax.random.dirichlet(jax.random.fold_in(_rk, 511), 0.3 * jnp.ones((16,), jnp.float32), (2, 128))
        _ctx_1024t = jnp.einsum('bsk,bkd->bsd', _ctx_1024c, _ctx_1024P)
        _ctx_1024t = _ctx_1024t * jax.lax.rsqrt(jnp.mean(jnp.square(_ctx_1024t)) + 1e-12) * 0.953939
        ctx_1024 = -1.52775e-05 + 0.999936 * (_ctx_1024t + 0.3 * jax.random.normal(jax.random.fold_in(_rk, 611), (2, 128, 512), jnp.float32))
        _validS = jnp.arange(2048)[None, :] < _lenS[:, None]
        _validS2 = jnp.arange(128)[None, :] < _lenS2[:, None]
        _causal = jnp.tril(jnp.ones((2048, 2048), dtype=bool))
        mask_BxS2_ik0 = jnp.where(jnp.broadcast_to(_validS2[:, :], (2, 128)), 0, 1).astype(jnp.int32)
        _g = jax.random.normal(jax.random.fold_in(_rk, 9001), (2, 1), jnp.float32)
        _g = jnp.sign(_g) * jnp.maximum(jnp.abs(_g), 1.0) + (_g == 0) * 1.0
        g_xattn = _g[0]
        g_ffn = _g[1]
        return (x, ctx_1024, mask_BxS2_ik0, g_xattn, g_ffn)
    x, ctx_1024, mask_BxS2_ik0, g_xattn, g_ffn = _rec_inputs()

    def _L0_xattn_setup():
        import jax, jax.numpy as jnp
        import numpy as np
        DIM = 512
        HEADS = 16
        HEAD_DIM = DIM // HEADS
        SCALE = HEAD_DIM ** (-0.5)
        MASK_FILL = -1000000000.0

        def layer_norm(x, gamma, beta, eps=1e-05):
            mu = jnp.mean(x, axis=-1, keepdims=True)
            var = jnp.var(x, axis=-1, keepdims=True)
            return (x - mu) * jax.lax.rsqrt(var + eps) * gamma + beta
        key = jax.random.key(seed)
        ks = jax.random.split(key, 10)
        B, N1, N2, C = (8, 128, 2048, DIM)
        s = C ** (-0.5)
        return {'x': jax.random.normal(ks[0], (B, N1, C), jnp.float32), 'kv': jax.random.normal(ks[1], (B, N2, C), jnp.float32), 'padding_mask': jax.random.randint(ks[2], (B, N2), 0, 2, jnp.int32), 'w_q': jax.random.normal(ks[3], (C, C), jnp.float32) * s, 'w_kv': jax.random.normal(ks[4], (C, 2 * C), jnp.float32) * s, 'w_proj': jax.random.normal(ks[5], (C, C), jnp.float32) * s, 'b_proj': jnp.zeros((C,), jnp.float32), 'g_x': jnp.ones((C,), jnp.float32), 'b_x': jnp.zeros((C,), jnp.float32), 'g_kv': jnp.ones((C,), jnp.float32), 'b_kv': jnp.zeros((C,), jnp.float32)}
    _L0_xattn_all = _L0_xattn_setup()
    _L0_xattn_in = {k: v for k, v in _L0_xattn_all.items() if k in ('w_q', 'w_kv', 'w_proj', 'b_proj', 'g_x', 'b_x', 'g_kv', 'b_kv')}
    del _L0_xattn_all

    def _L0_ffn_setup():
        import jax, jax.numpy as jnp
        import numpy as np
        B, S, H, F, G = (8, 1024, 512, 2048, 128)
        EPS = 1e-05

        def _dequant(q, scales, g):
            K, N = q.shape
            w = (q.astype(jnp.float32) - 128.0).reshape(K // g, g, N) * scales[:, None, :]
            return w.reshape(K, N)
        key = jax.random.key(seed)
        ks = jax.random.split(key, 8)
        x = jax.random.normal(ks[0], (B, S, H), dtype=jnp.float32)
        ln_gamma = jnp.ones((H,), jnp.float32)
        ln_beta = jnp.zeros((H,), jnp.float32)
        fc1_q = jax.random.randint(ks[1], (H, F), 0, 128, dtype=jnp.int32)
        fc2_q = jax.random.randint(ks[2], (F, H), 0, 128, dtype=jnp.int32)
        fc1_scales = jax.random.uniform(ks[3], (H // G, F), jnp.float32) * 0.02 + 0.001
        fc2_scales = jax.random.uniform(ks[4], (F // G, H), jnp.float32) * 0.02 + 0.001
        fc1_bias = jax.random.normal(ks[5], (F,), jnp.float32) * 0.02
        fc2_bias = jax.random.normal(ks[6], (H,), jnp.float32) * 0.02
        return {'x': x, 'ln_gamma': ln_gamma, 'ln_beta': ln_beta, 'fc1_q': fc1_q, 'fc1_scales': fc1_scales, 'fc1_bias': fc1_bias, 'fc2_q': fc2_q, 'fc2_scales': fc2_scales, 'fc2_bias': fc2_bias}
    _L0_ffn_all = _L0_ffn_setup()
    _L0_ffn_in = {k: v for k, v in _L0_ffn_all.items() if k in ('ln_gamma', 'ln_beta', 'fc1_q', 'fc1_scales', 'fc1_bias', 'fc2_q', 'fc2_scales', 'fc2_bias')}
    del _L0_ffn_all
    return {'x': x, 'ctx_1024': ctx_1024, 'mask_BxS2_ik0': mask_BxS2_ik0, 'g_xattn': g_xattn, 'g_ffn': g_ffn, 'L0_xattn_w_q': _L0_xattn_in['w_q'], 'L0_xattn_w_kv': _L0_xattn_in['w_kv'], 'L0_xattn_w_proj': _L0_xattn_in['w_proj'], 'L0_xattn_b_proj': _L0_xattn_in['b_proj'], 'L0_xattn_g_x': _L0_xattn_in['g_x'], 'L0_xattn_b_x': _L0_xattn_in['b_x'], 'L0_xattn_g_kv': _L0_xattn_in['g_kv'], 'L0_xattn_b_kv': _L0_xattn_in['b_kv'], 'L0_ffn_ln_gamma': _L0_ffn_in['ln_gamma'], 'L0_ffn_ln_beta': _L0_ffn_in['ln_beta'], 'L0_ffn_fc1_q': _L0_ffn_in['fc1_q'], 'L0_ffn_fc1_scales': _L0_ffn_in['fc1_scales'], 'L0_ffn_fc1_bias': _L0_ffn_in['fc1_bias'], 'L0_ffn_fc2_q': _L0_ffn_in['fc2_q'], 'L0_ffn_fc2_scales': _L0_ffn_in['fc2_scales'], 'L0_ffn_fc2_bias': _L0_ffn_in['fc2_bias']}

def reference(x, ctx_1024, mask_BxS2_ik0, g_xattn, g_ffn, L0_xattn_w_q, L0_xattn_w_kv, L0_xattn_w_proj, L0_xattn_b_proj, L0_xattn_g_x, L0_xattn_b_x, L0_xattn_g_kv, L0_xattn_b_kv, L0_ffn_ln_gamma, L0_ffn_ln_beta, L0_ffn_fc1_q, L0_ffn_fc1_scales, L0_ffn_fc1_bias, L0_ffn_fc2_q, L0_ffn_fc2_scales, L0_ffn_fc2_bias):
    import jax
    import jax.numpy as jnp

    def _L0_xattn_ref(x, kv, padding_mask, w_q, w_kv, w_proj, b_proj, g_x, b_x, g_kv, b_kv):
        import jax, jax.numpy as jnp
        import numpy as np
        DIM = 512
        HEADS = 16
        HEAD_DIM = DIM // HEADS
        SCALE = HEAD_DIM ** (-0.5)
        MASK_FILL = -1000000000.0

        def layer_norm(x, gamma, beta, eps=1e-05):
            mu = jnp.mean(x, axis=-1, keepdims=True)
            var = jnp.var(x, axis=-1, keepdims=True)
            return (x - mu) * jax.lax.rsqrt(var + eps) * gamma + beta
        B, N1, C = x.shape
        N2 = kv.shape[1]
        xn = layer_norm(x, g_x, b_x)
        kvn = layer_norm(kv, g_kv, b_kv)
        q = (xn @ w_q).reshape(B, N1, HEADS, HEAD_DIM).transpose(0, 2, 1, 3)
        kv_proj = (kvn @ w_kv).reshape(B, N2, 2, HEADS, HEAD_DIM).transpose(2, 0, 3, 1, 4)
        k, v = (kv_proj[0], kv_proj[1])
        attn = jnp.einsum('bhqd,bhkd->bhqk', q, k) * SCALE
        mask = padding_mask[:, None, None, :]
        attn = jnp.where(mask == 0, MASK_FILL, attn)
        attn = jax.nn.softmax(attn, axis=-1)
        out = jnp.einsum('bhqk,bhkd->bhqd', attn, v)
        out = out.transpose(0, 2, 1, 3).reshape(B, N1, C)
        return out @ w_proj + b_proj

    def _L0_ffn_ref(x, ln_gamma, ln_beta, fc1_q, fc1_scales, fc1_bias, fc2_q, fc2_scales, fc2_bias):
        import jax, jax.numpy as jnp
        import numpy as np
        B, S, H, F, G = (8, 1024, 512, 2048, 128)
        EPS = 1e-05

        def _dequant(q, scales, g):
            K, N = q.shape
            w = (q.astype(jnp.float32) - 128.0).reshape(K // g, g, N) * scales[:, None, :]
            return w.reshape(K, N)
        residual = x
        mu = jnp.mean(x, axis=-1, keepdims=True)
        var = jnp.mean(jnp.square(x - mu), axis=-1, keepdims=True)
        h = (x - mu) * jax.lax.rsqrt(var + EPS) * ln_gamma + ln_beta
        hf = h.reshape(-1, H)
        w1 = _dequant(fc1_q, fc1_scales, G)
        y = hf @ w1 + fc1_bias
        y = jax.nn.silu(y)
        w2 = _dequant(fc2_q, fc2_scales, G)
        z = y @ w2 + fc2_bias
        return residual + 0.5 * z.reshape(residual.shape)
    x = x + jnp.tanh(g_xattn[0]) * _L0_xattn_ref(_layernorm(x, axis=-1), ctx_1024, mask_BxS2_ik0, L0_xattn_w_q, L0_xattn_w_kv, L0_xattn_w_proj, L0_xattn_b_proj, L0_xattn_g_x, L0_xattn_b_x, L0_xattn_g_kv, L0_xattn_b_kv)
    x = x + jnp.tanh(g_ffn[0]) * _L0_ffn_ref(_layernorm(x, axis=-1), L0_ffn_ln_gamma, L0_ffn_ln_beta, L0_ffn_fc1_q, L0_ffn_fc1_scales, L0_ffn_fc1_bias, L0_ffn_fc2_q, L0_ffn_fc2_scales, L0_ffn_fc2_bias)
    return x

_drawn_inputs = setup_inputs


def setup_inputs(seed=0):
    import zlib

    import numpy as np

    out = dict(_drawn_inputs(seed))
    spreads = {'L0_xattn_b_proj': (0.0, 0.8),
     'L0_xattn_g_x': (1.0, 0.6),
     'L0_xattn_b_x': (0.0, 2.0),
     'L0_xattn_g_kv': (1.0, 0.6),
     'L0_xattn_b_kv': (0.0, 0.8),
     'L0_ffn_ln_gamma': (1.0, 0.2),
     'L0_ffn_ln_beta': (0.0, 0.1)}
    factors = {'L0_ffn_fc1_bias': 64.0, 'L0_ffn_fc2_bias': 64.0}
    for name, (base, spread) in spreads.items():
        noise = np.random.default_rng([zlib.crc32(name.encode()), seed]).standard_normal(out[name].shape)
        drawn = base * np.exp(spread * noise) if base else spread * noise
        out[name] = jnp.asarray(drawn.astype(out[name].dtype))
    for name, factor in factors.items():
        out[name] = (out[name] * factor).astype(out[name].dtype)
    return out
```

```python
from contextlib import ExitStack

import numpy as np

import concourse.bass as bass
from concourse import mybir

F32 = mybir.dt.float32
F32R = mybir.dt.float32r
F16 = mybir.dt.float16
BF16 = mybir.dt.bfloat16
I32 = mybir.dt.int32
ALU = mybir.AluOpType
ACT = mybir.ActivationFunctionType
AX = mybir.AxisListType

P = 128
HEAD = 32
HG = P // HEAD
CHUNK = 512
EPS = 1e-5
FILL = -1e9


def after(eng, semaphore, count):
    if not isinstance(count, int) or count > 0:
        eng.wait_ge(semaphore, count)


def build(nc, x, ctx, mask, g_xattn, g_ffn, w_q, w_kv, w_proj, b_proj, g_x, b_x, g_kv, b_kv,
          ln_gamma, ln_beta, fc1_q, fc1_scales, fc1_bias, fc2_q, fc2_scales, fc2_bias, out):
    B, S, D = x.shape
    KEYS = ctx.shape[1]
    F = fc1_q.shape[1]
    KB = D // P
    FB = F // P
    TT = CHUNK // P
    NCHUNK = B * S // CHUNK
    SCALE = HEAD ** -0.5
    assert B == 2 and KEYS == P and KB == HG and FB % 4 == 0 and NCHUNK % 2 == 0

    rows = "b (c t p) d -> b c t p d"
    x_tiles = x.rearrange(rows, t=TT, p=P)
    out_tiles = out.rearrange(rows, t=TT, p=P)
    x1_dram = nc.dram_tensor("x1_dram", (B, S, D), F32, kind="Internal").ap()
    x1_tiles = x1_dram.rearrange(rows, t=TT, p=P)
    chunk_rows = "b (c t p) d -> b c p t d"
    x_chunks = x.rearrange(chunk_rows, t=TT, p=P)
    x1_chunks = x1_dram.rearrange(chunk_rows, t=TT, p=P)

    def sems(scope, *names):
        return [scope.enter_context(nc.semaphore(n)) for n in names]

    with ExitStack() as whole:
        def sb(name, shape, dt, scope=whole):
            return scope.enter_context(nc.sbuf_tensor(name, shape, dt))

        ident = sb("ident", [P, P], F32)
        cols = sb("cols", [P, 6 * KB + FB], F32)
        gx_c, bx_c, gkv_c, bkv_c, lng_c, lnb_c = (cols[:, KB * n:KB * n + KB] for n in range(6))
        b1_c = cols[:, 6 * KB:6 * KB + FB]
        gates = sb("gates", [P, 2], F32)
        half_gate = sb("half_gate", [P, 1], F32)
        expo = sb("expo", [P, 2, TT], F32)
        eps = sb("eps", [P, TT], F32)
        pause = sb("pause", [P, 1], F32)
        b2_rows = sb("b2_rows", [P, D], F32)

        with ExitStack() as attn:
            def ab(name, shape, dt):
                return sb(name, shape, dt, attn)

            wq_hi, wq_lo = ab("wq_hi", [P, KB, D], F32R), ab("wq_lo", [P, KB, D], F32R)
            wp_hi, wp_lo = ab("wp_hi", [P, KB, D], F32R), ab("wp_lo", [P, KB, D], F32R)
            k_hi, k_lo = (ab(n, [P, B, KB, HG, KEYS], F32R) for n in ("k_hi", "k_lo"))
            v_parts = [ab(f"v{n}", [P, B, D], BF16) for n in range(3)]
            fill_col = ab("fill_col", [P, B], F32)
            minus_row = ab("minus_row", [P, HG, KEYS], F32R)
            ones16 = ab("ones16", [P, HEAD], BF16)
            bp_rows = ab("bp_rows", [P, D], F32)
            max_row = [ab(f"max_row{n}", [P, CHUNK], F32R) for n in range(2)]

            setup(nc, locals())
            attention(nc, locals())

        feed_forward(nc, locals())


def setup(nc, env):
    g = env.get
    (ctx, mask, w_q, w_kv, w_proj, b_proj, ident, cols, gates, half_gate, expo, b2_rows, k_hi, k_lo, v_parts,
     fill_col, minus_row, ones16, bp_rows, max_row) = (g(n) for n in (
         "ctx", "mask", "w_q", "w_kv", "w_proj", "b_proj", "ident", "cols", "gates", "half_gate", "expo",
         "b2_rows", "k_hi", "k_lo", "v_parts", "fill_col", "minus_row", "ones16", "bp_rows", "max_row"))
    B, D, KB, FB, KEYS, TT = (g(n) for n in ("B", "D", "KB", "FB", "KEYS", "TT"))
    gkv_c, bkv_c = g("gkv_c"), g("bkv_c")
    vectors = [g(n) for n in ("g_x", "b_x", "g_kv", "b_kv", "ln_gamma", "ln_beta", "fc1_bias")]
    NV = 6 * KB + FB

    with ExitStack() as scope:
        def sb(name, shape, dt):
            return scope.enter_context(nc.sbuf_tensor(name, shape, dt))

        def sem(name):
            return scope.enter_context(nc.semaphore(name))

        vec_rows = sb("vec_rows", [NV, P], F32)
        ctx_sb = sb("ctx_sb", [P, B, D], F32)
        ctx_n = sb("ctx_n", [P, B, D], F32)
        ctx_t = sb("ctx_t", [P, KB, B * KEYS], F32)
        mask_rows = sb("mask_rows", [P, B * KEYS], I32)
        mask_col = sb("mask_col", [P, B], I32)
        wkv = sb("wkv", [P, KB, 2 * D], F32)
        wq_raw = sb("wq_raw", [P, KB, D], F32)
        wp_raw = sb("wp_raw", [P, KB, D], F32)
        valid = sb("valid", [P, B * KEYS], F32)
        masked = sb("masked", [P, B * KEYS], F32)
        n_valid = sb("n_valid", [P, B], F32)
        some_valid = sb("some_valid", [P, B], F32)
        divisor = sb("divisor", [P, B], F32)
        inv_divisor = sb("inv_divisor", [P, B], F32)
        k_masked = sb("k_masked", [P, KB, B * KEYS], F32)
        k_sum = sb("k_sum", [P, KB, B], F32)
        k_mean = sb("k_mean", [P, KB, B], F32)
        k_full = sb("k_full", [P, KB, B, KEYS], F32)
        v_rest = sb("v_rest", [P, B, D], F32)
        minus_f = sb("minus_f", [P, HG, KEYS], F32)
        fill_a = sb("fill_a", [P, B], F32)
        stats = sb("c_stats", [P, B, 6], F32)
        mean_var = sb("c_mean_var", [P, B, 2], F32)
        var_eps = sb("c_var_eps", [P, B], F32)
        rstd = sb("c_rstd", [P, B], F32)
        ps = [scope.enter_context(nc.psum_tensor(f"sp{n}", [P, 512], F32)) for n in range(8)]
        ps_cols, ps_k, ps_v, ps_t = ps[7], ps[0:4], ps[4:6], ps[6]

        vec_loaded, ctx_loaded, mask_loaded, gate_loaded, wkv_loaded, wq_loaded, wp_loaded, bias_loaded = (
            sem(n) for n in ("vec_loaded", "ctx_loaded", "mask_loaded", "gate_loaded", "wkv_loaded", "wq_loaded",
                             "wp_loaded", "bias_loaded"))
        (ident_ready, pool_step, vec_t, cols_ready, tanh_ready, ctx_stats, ctx_rstd, ctx_normed, ctx_turned,
         ctx_t_ready, k_done, v_done, dve_step, act_step, zeroed) = (
            sem(n) for n in ("ident_ready", "pool_step", "vec_t", "cols_ready", "tanh_ready", "ctx_stats",
                             "ctx_rstd", "ctx_normed", "ctx_turned", "ctx_t_ready", "k_done", "v_done",
                             "dve_step", "act_step", "zeroed"))

        block = scope.enter_context(nc.Block())

        @block.sync
        def _(sp):
            at = 0
            for v in vectors:
                n = v.shape[0] // P
                sp.dma_start(vec_rows[at:at + n, :], v.rearrange("(n p) -> n p", p=P)).then_inc(vec_loaded, 16)
                at += n
            sp.dma_start(ctx_sb[:, :, :], ctx.rearrange("b p d -> p b d")).then_inc(ctx_loaded, 16)
            sp.dma_start(wkv[:, :, :], w_kv.rearrange("(k p) n -> p k n", p=P)).then_inc(wkv_loaded, 16)
            sp.dma_start(wp_raw[:, :, :], w_proj.rearrange("(k p) n -> p k n", p=P)).then_inc(wp_loaded, 16)

        @block.scalar
        def _(act):
            act.dma_start(gates[:, 0:1], g("g_xattn").partition_broadcast(P)).then_inc(gate_loaded, 16)
            act.dma_start(gates[:, 1:2], g("g_ffn").partition_broadcast(P)).then_inc(gate_loaded, 16)
            act.dma_start(mask_rows[:, :], mask.rearrange("b k -> (b k)").partition_broadcast(P)).then_inc(mask_loaded, 16)
            for b in range(B):
                act.dma_start(mask_col[:, b:b + 1], mask[b, :].rearrange("(k a) -> k a", a=1)).then_inc(mask_loaded, 16)
            act.dma_start(wq_raw[:, :, :], w_q.rearrange("(k p) n -> p k n", p=P)).then_inc(wq_loaded, 16)
            act.dma_start(bp_rows[:, :], b_proj.partition_broadcast(P)).then_inc(bias_loaded, 16)
            act.dma_start(b2_rows[:, :], g("fc2_bias").partition_broadcast(P)).then_inc(bias_loaded, 16)
            act.wait_ge(gate_loaded, 32)
            nc.scalar.activation(gates[:, :], gates[:, :], ACT.Tanh).then_inc(tanh_ready, 1)
            act.wait_ge(tanh_ready, 1)
            nc.scalar.mul(half_gate[:, :], gates[:, 1:2], 0.5).then_inc(tanh_ready, 1)
            act.wait_ge(cols_ready, 1)
            for k in range(KB):
                act.wait_ge(ctx_turned, k + 1)
                nc.scalar.activation(ctx_t[:, k, :], ps[k % 2][:, 0:B * KEYS], ACT.Identity,
                                     bias=bkv_c[:, k:k + 1], scale=gkv_c[:, k:k + 1]).then_inc(ctx_t_ready, 1)
            act.wait_ge(wq_loaded, 16)
            nc.scalar.copy(g("wq_hi")[:, :, :], wq_raw[:, :, :]).then_inc(act_step, 1)

        @block.gpsimd
        def _(pool):
            done = [0]

            def link(ins):
                done[0] += 1
                ins.then_inc(pool_step, 1)
                pool.wait_ge(pool_step, done[0])

            link(nc.gpsimd.memset(ident[:, :], 0.0))
            nc.gpsimd.affine_select(out=ident[:, :], in_=ident[:, :], compare_op=ALU.not_equal, fill=1.0, base=0,
                                    pattern=[[-1, P]], channel_multiplier=1).then_inc(ident_ready, 1)
            nc.gpsimd.memset(ones16[:, :], 1.0)
            nc.gpsimd.memset(expo[:, 1, :], 0.5)
            nc.gpsimd.memset(g("eps")[:, :], EPS)
            link(nc.gpsimd.memset(expo[:, 0, :], -0.5))
            pool.wait_ge(ctx_stats, 1)
            link(nc.gpsimd.tensor_scalar(var_eps[:, :], mean_var[:, :, 1], EPS, None, ALU.add))
            nc.gpsimd.tensor_tensor(rstd[:, :], var_eps[:, :], expo[:, 0, 0:B], ALU.pow).then_inc(ctx_rstd, 1)
            nc.gpsimd.memset(max_row[0][:, :].bitcast(F32), 0.0)
            nc.gpsimd.memset(max_row[1][:, :].bitcast(F32), 0.0)
            link(nc.gpsimd.memset(minus_f[:, :, :], 0.0))
            link(nc.gpsimd.affine_select(out=minus_f[:, :, :], in_=minus_f[:, :, :], compare_op=ALU.not_equal,
                                         fill=-1.0, base=0, pattern=[[-1, HG], [0, KEYS]], channel_multiplier=1))
            nc.gpsimd.tensor_copy(minus_row[:, :, :], minus_f[:, :, :])
            pool.wait_ge(act_step, 1)
            for k in range(KB):
                nc.gpsimd.tensor_tensor(g("wq_lo")[:, k, :], wq_raw[:, k, :], g("wq_hi")[:, k, :].bitcast(F32), ALU.subtract)

        @block.tensor
        def _(pe):
            pe.wait_ge(ident_ready, 1)
            pe.wait_ge(vec_loaded, 16 * len(vectors))
            nc.tensor.transpose(ps_cols[:, 0:NV], vec_rows[:, :], ident[0:NV, 0:NV]).then_inc(vec_t, 1)
            pe.wait_ge(ctx_normed, 1)
            for k in range(KB):
                if k >= 2:
                    pe.wait_ge(ctx_t_ready, k - 1)
                for b in range(B):
                    last = nc.tensor.transpose(ps[k % 2][:, b * KEYS:(b + 1) * KEYS], ctx_n[:, b, k * P:(k + 1) * P],
                                               ident[:, :])
                last.then_inc(ctx_turned, 1)
            pe.wait_ge(ctx_t_ready, KB)
            pe.wait_ge(wkv_loaded, 16)
            for m in range(KB):
                for k in range(KB):
                    last = nc.tensor.matmul(ps_k[m][:, 0:B * KEYS], wkv[:, k, m * P:(m + 1) * P], ctx_t[:, k, :],
                                            start=(k == 0), stop=(k == KB - 1))
                last.then_inc(k_done, 1)
            for b in range(B):
                for k in range(KB):
                    last = nc.tensor.matmul(ps_v[b][:, :], ctx_t[:, k, b * KEYS:(b + 1) * KEYS], wkv[:, k, D:2 * D],
                                            start=(k == 0), stop=(k == KB - 1))
                last.then_inc(v_done, 1)

        @block.vector
        def _(dve):
            done = [0]

            def link(ins):
                done[0] += 1
                ins.then_inc(dve_step, 1)
                dve.wait_ge(dve_step, done[0])

            nc.vector.memset(k_hi[:, :, :, :, :].bitcast(F32), 0.0)
            link(nc.vector.memset(k_lo[:, :, :, :, :].bitcast(F32), 0.0))
            dve.wait_ge(ctx_loaded, 16)
            for b in range(B):
                last = nc.vector.bn_stats(stats[:, b, :], ctx_sb[:, b, :])
            link(last)
            for b in range(B):
                last = nc.vector.bn_aggr(mean_var[:, b, :], stats[:, b, :])
            last.then_inc(ctx_stats, 1)
            dve.wait_ge(ctx_rstd, 1)
            for b in range(B):
                last = nc.vector.tensor_scalar(ctx_n[:, b, :], ctx_sb[:, b, :], mean_var[:, b, 0:1], rstd[:, b:b + 1],
                                               ALU.subtract, ALU.mult)
            last.then_inc(ctx_normed, 1)
            dve.wait_ge(vec_t, 1)
            nc.vector.tensor_copy(cols[:, :], ps_cols[:, 0:NV]).then_inc(cols_ready, 1)
            dve.wait_ge(mask_loaded, 16 * (1 + B))
            nc.vector.tensor_scalar(masked[:, :], mask_rows[:, :], 0.0, None, ALU.is_equal)
            link(nc.vector.tensor_scalar(valid[:, :], mask_rows[:, :], 0.0, None, ALU.not_equal))
            link(nc.vector.reduce_sum(n_valid[:, :], valid[:, :].rearrange("p (b k) -> p b k", b=B), AX.X))
            nc.vector.tensor_scalar(some_valid[:, :], n_valid[:, :], 1.0, None, ALU.min)
            link(nc.vector.tensor_scalar(divisor[:, :], n_valid[:, :], 1.0, None, ALU.max))
            link(nc.vector.reciprocal(inv_divisor[:, :], divisor[:, :]))
            link(nc.vector.tensor_scalar(fill_a[:, :], mask_col[:, :], 0.0, FILL, ALU.is_equal, ALU.mult))
            nc.vector.tensor_tensor(fill_col[:, :], fill_a[:, :], some_valid[:, :], ALU.mult)
            dve.wait_ge(tanh_ready, 2)
            dve.wait_ge(wp_loaded, 16)
            link(nc.vector.tensor_scalar(wp_raw[:, :, :], wp_raw[:, :, :], gates[:, 0:1], None, ALU.mult))
            link(nc.vector.tensor_copy(g("wp_hi")[:, :, :], wp_raw[:, :, :]))
            nc.vector.tensor_tensor(g("wp_lo")[:, :, :], wp_raw[:, :, :], g("wp_hi")[:, :, :].bitcast(F32), ALU.subtract)
            dve.wait_ge(bias_loaded, 32)
            nc.vector.tensor_scalar(bp_rows[:, :], bp_rows[:, :], gates[:, 0:1], None, ALU.mult)
            nc.vector.tensor_scalar(b2_rows[:, :], b2_rows[:, :], half_gate[:, :], None, ALU.mult)
            for m in range(KB):
                dve.wait_ge(k_done, m + 1)
                last = nc.vector.tensor_tensor(k_masked[:, m, :], ps_k[m][:, 0:B * KEYS], valid[:, :], ALU.mult)
            link(last)
            link(nc.vector.reduce_sum(k_sum[:, :, :], k_masked[:, :, :].rearrange("p m (b k) -> p m b k", b=B), AX.X))
            for b in range(B):
                last = nc.vector.tensor_scalar(k_mean[:, :, b], k_sum[:, :, b], inv_divisor[:, b:b + 1], None, ALU.mult)
            link(last)
            for m in range(KB):
                for b in range(B):
                    keys = slice(b * KEYS, (b + 1) * KEYS)
                    last = nc.vector.scalar_tensor_tensor(
                        out=k_full[:, m, b, :], in0=masked[:, keys], scalar=k_mean[:, m, b:b + 1],
                        in1=k_masked[:, m, keys], op0=ALU.mult, op1=ALU.add)
            link(last)
            for b in range(B):
                for j in range(HG):
                    at = slice(HEAD * j, HEAD * (j + 1))
                    last = nc.vector.tensor_copy(k_hi[at, b, :, j, :], k_full[at, :, b, :])
            link(last)
            for b in range(B):
                for j in range(HG):
                    at = slice(HEAD * j, HEAD * (j + 1))
                    nc.vector.tensor_tensor(k_lo[at, b, :, j, :], k_full[at, :, b, :], k_hi[at, b, :, j, :].bitcast(F32),
                                            ALU.subtract)
            for b in range(B):
                dve.wait_ge(v_done, b + 1)
                link(nc.vector.tensor_copy(v_parts[0][:, b, :], ps_v[b][:, :]))
                link(nc.vector.tensor_tensor(v_rest[:, b, :], ps_v[b][:, :], v_parts[0][:, b, :], ALU.subtract))
                link(nc.vector.tensor_copy(v_parts[1][:, b, :], v_rest[:, b, :]))
                nc.vector.tensor_tensor(v_parts[2][:, b, :], v_rest[:, b, :], v_parts[1][:, b, :], ALU.subtract)


def split_product(nc, out, stationary, moving):
    n = len(stationary)
    for k, ((s_hi, s_lo), (m_hi, m_lo)) in enumerate(zip(stationary, moving)):
        nc.tensor.matmul(out, s_hi, m_hi, start=(k == 0), stop=False)
        nc.tensor.matmul(out, s_hi, m_lo, start=False, stop=False)
        last = nc.tensor.matmul(out, s_lo, m_hi, start=False, stop=(k == n - 1))
    return last


def attention(nc, env):
    g = env.get
    eps, pause = g("eps"), g("pause")
    (wq_hi, wq_lo, wp_hi, wp_lo, k_hi, k_lo, v_parts, fill_col, minus_row, ones16, bp_rows, max_row, ident, expo,
     gx_c, bx_c, x_chunks, x_tiles, x1_tiles) = (g(n) for n in (
         "wq_hi", "wq_lo", "wp_hi", "wp_lo", "k_hi", "k_lo", "v_parts", "fill_col", "minus_row", "ones16", "bp_rows",
         "max_row", "ident", "expo", "gx_c", "bx_c", "x_chunks", "x_tiles", "x1_tiles"))
    B, D, KB, TT, KEYS, NCHUNK, SCALE = (g(n) for n in ("B", "D", "KB", "TT", "KEYS", "NCHUNK", "SCALE"))
    UNITS = NCHUNK * KB
    PER = 2 * KB
    LOOPS = UNITS // PER
    FIRST, LAST = -6, UNITS + 5

    with ExitStack() as scope:
        def sb(name, shape, dt):
            return scope.enter_context(nc.sbuf_tensor(name, shape, dt))

        def sem(name):
            return scope.enter_context(nc.semaphore(name))

        x_in = sb("x_in", [P, TT, D], F32)
        x_norm = sb("x_norm", [P, TT, D], F32)
        xt_f = [sb(f"xt_f{n}", [P, CHUNK], F32) for n in range(2)]
        xt_hi = [sb(f"xt_hi{n}", [P, KB, CHUNK], F32R) for n in range(2)]
        xt_lo = [sb(f"xt_lo{n}", [P, KB, CHUNK], F32R) for n in range(2)]
        q_f = [sb(f"q_f{n}", [P, CHUNK], F32) for n in range(2)]
        q_hi = [sb(f"q_hi{n}", [P, CHUNK], F32R) for n in range(4)]
        q_lo = [sb(f"q_lo{n}", [P, CHUNK], F32R) for n in range(4)]
        maxima = [sb(f"maxima{n}", [P, TT, HG], F32) for n in range(2)]
        p_f = [sb(f"p_f{n}", [P, CHUNK], F32) for n in range(2)]
        p_hi = [sb(f"p_hi{n}", [P, CHUNK], F16) for n in range(HG)]
        p_lo = [sb(f"p_lo{n}", [P, CHUNK], F16) for n in range(HG)]
        inv_den = sb("inv_den", [P, CHUNK], F32)
        o_f = [sb(f"o_f{n}", [P, CHUNK], F32) for n in range(2)]
        o_hi = [sb(f"o_hi{n}", [P, KB, CHUNK], F32R) for n in range(2)]
        o_lo = [sb(f"o_lo{n}", [P, KB, CHUNK], F32R) for n in range(2)]
        x_res = [sb(f"x_res{n}", [P, D], F32) for n in range(2)]
        x1_out = [sb(f"x1_out{n}", [P, D], F32) for n in range(2)]
        stats = sb("x_stats", [P, TT, 6], F32)
        mean_var = sb("x_mean_var", [P, TT, 2], F32)
        ln_a, ln_r1, ln_b, ln_c, ln_r2, ln_r = (sb(n, [P, TT], F32) for n in
                                                ("ln_a", "ln_r1", "ln_b", "ln_c", "ln_r2", "ln_r"))

        def psum(name):
            return scope.enter_context(nc.psum_tensor(name, [P, 512], F32))

        ps_max = [psum("ps_max0"), psum("ps_max1")]
        ps_s = [psum("ps_s0"), psum("ps_s1")]
        ps_o, ps_den = psum("ps_o"), psum("ps_den")
        ps_qm = psum("ps_qm")
        ps_xp = psum("ps_xp")

        x_loaded = sem("x_loaded")
        res_loaded = [sem("res_loaded0"), sem("res_loaded1")]
        x1_stored = [sem("x1_stored0"), sem("x1_stored1")]
        (stats_some, stats_ready, ln_step, rstd_ready, norm_ready, xt_turned, xt_f_ready, xt_hi_ready, xt_lo_ready,
         q_done, q_f_ready, q_hi_ready, q_lo_ready, max_done, max_taken, max_turned, max_row_ready, s_done,
         p_f_ready, p_hi_ready, p_lo_dve, p_lo_pool, pv_done, den_inv, o_f_ready, o_hi_ready, o_lo_ready,
         proj_done, x1_ready, res_biased) = (sem(n) for n in (
             "stats_some", "stats_ready", "ln_step", "rstd_ready", "norm_ready", "xt_turned", "xt_f_ready",
             "xt_hi_ready", "xt_lo_ready", "q_done", "q_f_ready", "q_hi_ready", "q_lo_ready", "max_done",
             "max_taken", "max_turned", "max_row_ready", "s_done", "p_f_ready", "p_hi_ready", "p_lo_dve",
             "p_lo_pool", "pv_done", "den_inv", "o_f_ready", "o_hi_ready", "o_lo_ready", "proj_done", "x1_ready",
             "res_biased"))

        def real(i, k, n):
            return not isinstance(i, int) or 0 <= PER * i + k < n

        def every_step(eng, step):
            for k in range(FIRST, PER):
                step(0, k)
            with eng.Fori(1, LOOPS - 1) as i:
                for k in range(PER):
                    step(i, k)
            for k in range(LAST - PER * (LOOPS - 1)):
                step(LOOPS - 1, k)


        block = scope.enter_context(nc.Block())

        @block.sync
        def _(sp):
            def load_x(i, c):
                if real(i, KB * c, UNITS):
                    n = 2 * i + c
                    source = x_chunks[c % 2, i + c // 2, :, :, :]
                    sp.lower_val(source.offset * 4)
                    after(sp, norm_ready, TT * n)
                    sp.dma_start(x_in[:, :, :], source).then_inc(x_loaded, 16)

            def step(i, k):
                if k % KB == 0:
                    load_x(i, k // KB + 2)
                tile = k - 4
                if real(i, tile, UNITS):
                    c, t = tile // KB, tile % KB
                    source = x_tiles[c % 2, i + c // 2, t, :, :]
                    sp.lower_val(source.offset * 4)
                    after(sp, x1_ready, PER * i + tile - 1)
                    sp.dma_start(x_res[t % 2][:, :], source).then_inc(res_loaded[t % 2], 16)
                tile = k - 5
                if real(i, tile, UNITS):
                    c, t = tile // KB, tile % KB
                    target = x1_tiles[c % 2, i + c // 2, t, :, :]
                    sp.lower_val(target.offset * 4)
                    after(sp, x1_ready, PER * i + tile + 1)
                    sp.dma_start(target, x1_out[t % 2][:, :]).then_inc(x1_stored[t % 2], 16)

            load_x(0, 0)
            every_step(sp, step)
            for s in x1_stored:
                sp.wait_ge(s, 16 * UNITS // 2)

        @block.tensor
        def _(pe):
            def queries(i, k):
                v, c, m = PER * i + k, (k // KB) % 2, k % KB
                after(pe, xt_hi_ready, KB * (v // KB + 1) if isinstance(i, int) else KB * (2 * i + k // KB + 1))
                after(pe, xt_lo_ready, KB * (v // KB + 1) if isinstance(i, int) else KB * (2 * i + k // KB + 1))
                after(pe, q_f_ready, v)
                after(pe, max_row_ready, v - 1)
                block = slice(m * P, (m + 1) * P)
                split_product(nc, ps_qm[:, :], [(wq_hi[:, n, block], wq_lo[:, n, block]) for n in range(KB)],
                              [(xt_hi[c][:, n, :], xt_lo[c][:, n, :]) for n in range(KB)]).then_inc(q_done, 1)

            def scores_for_max(i, k):
                v, b, m = PER * i + k, (k // KB) % 2, k % KB
                after(pe, q_hi_ready, v + 1)
                for t in range(TT):
                    after(pe, max_taken, TT * v + t - 1)
                    nc.tensor.matmul(ps_max[t % 2][:, :], q_hi[k % 4][:, t * P:(t + 1) * P],
                                     k_hi[:, b, m, :, :].rearrange("p j n -> p (j n)"),
                                     start=True, stop=True).then_inc(max_done, 1)

            def turn_maxima(i, k):
                v = PER * i + k
                after(pe, max_taken, TT * (v + 1))
                after(pe, q_f_ready, v + 2 if real(i, k + 1, UNITS) else v + 1)
                after(pe, max_row_ready, v)
                for t in range(TT):
                    last = nc.tensor.transpose(ps_qm[0:HG, t * P:(t + 1) * P], maxima[k % 2][:, t, :], ident[:, :])
                last.then_inc(max_turned, 1)

            def scores(i, k, j):
                v, b, m = PER * i + k, (k // KB) % 2, k % KB
                if j == 0:
                    after(pe, q_lo_ready, v + 1)
                    after(pe, max_row_ready, v + 1)
                after(pe, p_hi_ready, HG * v + j - 1)
                to = ps_s[j % 2][:, :]
                nc.tensor.matmul(to, k_hi[:, b, m, j, :], q_hi[k % 4][:, :], start=True, stop=False)
                nc.tensor.matmul(to, k_hi[:, b, m, j, :], q_lo[k % 4][:, :], start=False, stop=False)
                nc.tensor.matmul(to, k_lo[:, b, m, j, :], q_hi[k % 4][:, :], start=False, stop=False)
                nc.tensor.matmul(to, minus_row[:, j, :], max_row[k % 2][:, :], start=False, stop=True).then_inc(s_done, 1)

            def weighted_values(i, k):
                v, b, m = PER * i + k, (k // KB) % 2, k % KB
                after(pe, p_hi_ready, HG * (v + 1))
                after(pe, p_lo_dve, (HG - 1) * (v + 1))
                after(pe, p_lo_pool, v + 1)
                after(pe, o_f_ready, v)
                terms = [(v_parts[0], p_hi), (v_parts[1], p_hi), (v_parts[2], p_hi), (v_parts[0], p_lo), (v_parts[1], p_lo)]
                for n, (part, probs) in enumerate(terms):
                    for j in range(HG):
                        h = HG * m + j
                        nc.tensor.matmul(ps_o[HEAD * j:HEAD * (j + 1), :], part[:, b, h * HEAD:(h + 1) * HEAD], probs[j][:, :],
                                         start=(n == 0), stop=(n == len(terms) - 1))
                for n, probs in enumerate((p_hi, p_lo)):
                    for j in range(HG):
                        last = nc.tensor.matmul(ps_den[HEAD * j:HEAD * (j + 1), :], ones16[:, :], probs[j][:, :],
                                                start=(n == 0), stop=(n == 1))
                last.then_inc(pv_done, 1)

            def turn_x(i, c, n):
                if not real(i, KB * c, UNITS):
                    return
                chunk = 2 * i + c
                after(pe, norm_ready, TT * (chunk + 1))
                after(pe, xt_f_ready, KB * chunk + n)
                after(pe, x1_ready, KB * (chunk - 1) + n // 2 - 5 + n % 2)
                for t in range(TT):
                    last = nc.tensor.transpose(ps_xp[:, t * P:(t + 1) * P], x_norm[:, t, n * P:(n + 1) * P], ident[:, :])
                last.then_inc(xt_turned, 1)

            def project(i, k):
                tile, c, t = PER * i + k, (k // KB) % 2, k % KB
                chunk = 2 * i + k // KB
                after(pe, o_hi_ready, KB * (chunk + 1))
                after(pe, o_lo_ready, KB * (chunk + 1))
                after(pe, x1_ready, tile)
                turned = KB * (chunk + 2) + (3, 4, 4, 5)[t]
                after(pe, xt_f_ready, min(turned, KB * NCHUNK) if isinstance(i, int) else turned)
                tokens = slice(t * P, (t + 1) * P)
                split_product(nc, ps_xp[:, :], [(o_hi[c][:, n, tokens], o_lo[c][:, n, tokens]) for n in range(KB)],
                              [(wp_hi[:, n, :], wp_lo[:, n, :]) for n in range(KB)]).then_inc(proj_done, 1)

            def step(i, k):
                if real(i, k + 2, UNITS):
                    queries(i, k + 2)
                if real(i, k + 1, UNITS):
                    scores_for_max(i, k + 1)
                if real(i, k - 1, UNITS):
                    weighted_values(i, k - 1)
                if real(i, k, UNITS):
                    scores(i, k, 0)
                    scores(i, k, 1)
                if k % KB in (0, 1):
                    turn_x(i, k // KB + 1, 2 * (k % KB))
                if real(i, k - 5, UNITS):
                    project(i, k - 5)
                if real(i, k, UNITS):
                    scores(i, k, 2)
                    scores(i, k, 3)
                if k % KB in (0, 1):
                    turn_x(i, k // KB + 1, 2 * (k % KB) + 1)
                if real(i, k + 1, UNITS):
                    turn_maxima(i, k + 1)

            every_step(pe, step)

        @block.scalar
        def _(act):
            def take_queries(i, k):
                v = PER * i + k
                after(act, q_done, v + 1)
                after(act, q_hi_ready, v - 1)
                after(act, q_lo_ready, v - 1)
                nc.scalar.activation(q_f[k % 2][:, :], ps_qm[:, :], ACT.Identity, scale=SCALE).then_inc(q_f_ready, 1)

            def probabilities(i, k, j):
                v, b = PER * i + k, (k // KB) % 2
                after(act, s_done, HG * v + j + 1)
                if j == 1:
                    after(act, p_lo_pool, v)
                else:
                    after(act, p_lo_dve, (HG - 1) * v + {0: 0, 2: 1, 3: 2}[j])
                nc.scalar.activation(p_f[j % 2][:, :], ps_s[j % 2][:, :], ACT.Exp, bias=fill_col[:, b:b + 1]).then_inc(p_f_ready, 1)
                after(act, pv_done, v)
                nc.scalar.activation(p_hi[j][:, :], ps_s[j % 2][:, :], ACT.Exp, bias=fill_col[:, b:b + 1]).then_inc(p_hi_ready, 1)

            def take_x(i, c, n):
                if not real(i, KB * c, UNITS):
                    return
                job = KB * (2 * i + c) + n
                after(act, xt_turned, job + 1)
                after(act, xt_hi_ready, job - 1)
                after(act, xt_lo_ready, job - 1)
                nc.scalar.activation(xt_f[n % 2][:, :], ps_xp[:, :], ACT.Identity, bias=bx_c[:, n:n + 1],
                                     scale=gx_c[:, n:n + 1]).then_inc(xt_f_ready, 1)

            def take_maxima(i, k):
                v = PER * i + k
                after(act, max_turned, v + 1)
                after(act, s_done, HG * (v - 1))
                nc.scalar.copy(max_row[k % 2][0:HG, :], ps_qm[0:HG, :]).then_inc(max_row_ready, 1)

            def outputs_hi(i, k):
                v, c, m = PER * i + k, (k // KB) % 2, k % KB
                after(act, o_f_ready, v + 1)
                after(act, proj_done, KB * (2 * i + k // KB - 1))
                nc.scalar.copy(o_hi[c][:, m, :], o_f[k % 2][:, :]).then_inc(o_hi_ready, 1)

            def step(i, k):
                if real(i, k + 2, UNITS):
                    take_queries(i, k + 2)
                if real(i, k, UNITS):
                    probabilities(i, k, 0)
                    probabilities(i, k, 1)
                if real(i, k - 1, UNITS):
                    outputs_hi(i, k - 1)
                if k % KB in (0, 1):
                    take_x(i, k // KB + 1, 2 * (k % KB))
                if real(i, k, UNITS):
                    probabilities(i, k, 2)
                    probabilities(i, k, 3)
                if k % KB in (0, 1):
                    take_x(i, k // KB + 1, 2 * (k % KB) + 1)
                if real(i, k + 1, UNITS):
                    take_maxima(i, k + 1)

            every_step(act, step)

        @block.vector
        def _(dve):
            def queries_hi(i, k):
                v = PER * i + k
                after(dve, q_f_ready, v + 1)
                after(dve, s_done, HG * (v - 3))
                nc.vector.tensor_copy(q_hi[k % 4][:, :], q_f[k % 2][:, :]).then_inc(q_hi_ready, 1)

            def take_max(i, k):
                v = PER * i + k
                after(dve, max_turned, v - 1)
                for t in range(TT):
                    after(dve, max_done, TT * v + t + 1)
                    nc.vector.reduce_max(maxima[k % 2][:, t, :], ps_max[t % 2][:, :].rearrange("p (j n) -> p j n", j=HG),
                                         AX.X).then_inc(max_taken, 1)

            def normalise(i, k):
                v = PER * i + k
                after(dve, pv_done, v + 1)
                nc.vector.reciprocal(inv_den[:, :], ps_den[:, :]).then_inc(den_inv, 1)
                after(dve, o_hi_ready, v - 1)
                after(dve, o_lo_ready, v - 1)
                after(dve, den_inv, v + 1)
                nc.vector.tensor_tensor(o_f[k % 2][:, :], ps_o[:, :], inv_den[:, :], ALU.mult).then_inc(o_f_ready, 1)

            def probabilities_lo(i, k, j):
                v = PER * i + k
                after(dve, p_f_ready, HG * v + j + 1)
                after(dve, p_hi_ready, HG * v + j + 1)
                nc.vector.tensor_tensor(p_lo[j][:, :], p_f[j % 2][:, :], p_hi[j][:, :], ALU.subtract).then_inc(p_lo_dve, 1)

            def x_hi(i, c, n):
                if not real(i, KB * c, UNITS):
                    return
                chunk = 2 * i + c
                after(dve, xt_f_ready, KB * chunk + n + 1)
                after(dve, q_done, KB * (chunk - 1))
                nc.vector.tensor_copy(xt_hi[c % 2][:, n, :], xt_f[n % 2][:, :]).then_inc(xt_hi_ready, 1)

            def add_residual(i, k):
                tile = PER * i + k
                after(dve, proj_done, tile + 1)
                after(dve, res_biased, tile + 1)
                if real(i, k - 2, UNITS):
                    after(dve, x1_stored[k % 2], 8 * (tile - k % 2))
                nc.vector.tensor_tensor(x1_out[k % 2][:, :], ps_xp[:, :], x_res[k % 2][:, :], ALU.add).then_inc(x1_ready, 1)

            def row_stats(i, c):
                if not real(i, KB * c, UNITS):
                    return
                chunk = 2 * i + c
                after(dve, x_loaded, 16 * (chunk + 1))
                for t in range(TT):
                    nc.vector.bn_stats(stats[:, t, :], x_in[:, t, :]).then_inc(stats_some, 1)
                after(dve, rstd_ready, chunk)
                after(dve, stats_some, TT * (chunk + 1))
                nc.vector.memset(pause[:, :], 0.0)
                for t in range(TT):
                    last = nc.vector.bn_aggr(mean_var[:, t, :], stats[:, t, :])
                last.then_inc(stats_ready, 1)

            def normalise_rows(i, c):
                if not real(i, KB * c, UNITS):
                    return
                chunk = 2 * i + c
                after(dve, rstd_ready, chunk + 1)
                after(dve, stats_ready, chunk + 1)
                after(dve, xt_turned, KB * chunk)
                for t in range(TT):
                    nc.vector.tensor_scalar(x_norm[:, t, :], x_in[:, t, :], mean_var[:, t, 0:1], ln_r[:, t:t + 1],
                                            ALU.subtract, ALU.mult).then_inc(norm_ready, 1)

            def step(i, k):
                if real(i, k + 2, UNITS):
                    queries_hi(i, k + 2)
                if real(i, k + 1, UNITS):
                    take_max(i, k + 1)
                if real(i, k - 1, UNITS):
                    normalise(i, k - 1)
                if real(i, k, UNITS):
                    probabilities_lo(i, k, 0)
                    probabilities_lo(i, k, 1)
                if k % KB in (0, 1):
                    x_hi(i, k // KB + 1, 2 * (k % KB))
                if real(i, k - 5, UNITS):
                    add_residual(i, k - 5)
                if real(i, k, UNITS):
                    probabilities_lo(i, k, 2)
                if k % KB in (0, 1):
                    x_hi(i, k // KB + 1, 2 * (k % KB) + 1)
                if k % KB == 2:
                    row_stats(i, k // KB + 2)
                if k % KB == 3:
                    normalise_rows(i, k // KB + 2)

            every_step(dve, step)

        @block.gpsimd
        def _(pool):
            def queries_lo(i, k):
                v = PER * i + k
                after(pool, q_hi_ready, v + 1)
                after(pool, s_done, HG * (v - 3))
                nc.gpsimd.tensor_tensor(q_lo[k % 4][:, :], q_f[k % 2][:, :], q_hi[k % 4][:, :].bitcast(F32),
                                        ALU.subtract).then_inc(q_lo_ready, 1)

            def bias_residual(i, k):
                tile = PER * i + k
                after(pool, res_loaded[k % 2], 8 * (tile - k % 2) + 16)
                nc.gpsimd.tensor_tensor(x_res[k % 2][:, :], x_res[k % 2][:, :], bp_rows[:, :], ALU.add).then_inc(res_biased, 1)

            def outputs_lo(i, k):
                v, c, m = PER * i + k, (k // KB) % 2, k % KB
                after(pool, o_hi_ready, v + 1)
                after(pool, proj_done, KB * (2 * i + k // KB - 1))
                nc.gpsimd.tensor_tensor(o_lo[c][:, m, :], o_f[k % 2][:, :], o_hi[c][:, m, :].bitcast(F32),
                                        ALU.subtract).then_inc(o_lo_ready, 1)

            def x_lo(i, c, n):
                if not real(i, KB * c, UNITS):
                    return
                chunk = 2 * i + c
                after(pool, xt_hi_ready, KB * chunk + n + 1)
                after(pool, q_done, KB * (chunk - 1))
                nc.gpsimd.tensor_tensor(xt_lo[c % 2][:, n, :], xt_f[n % 2][:, :], xt_hi[c % 2][:, n, :].bitcast(F32),
                                        ALU.subtract).then_inc(xt_lo_ready, 1)

            def probabilities_lo(i, k, j):
                v = PER * i + k
                after(pool, p_f_ready, HG * v + j + 1)
                after(pool, p_hi_ready, HG * v + j + 1)
                nc.gpsimd.tensor_tensor(p_lo[j][:, :], p_f[j % 2][:, :], p_hi[j][:, :], ALU.subtract).then_inc(p_lo_pool, 1)

            def row_scales(i, c):
                if not real(i, KB * c, UNITS):
                    return
                chunk = 2 * i + c
                after(pool, stats_ready, chunk + 1)
                after(pool, norm_ready, TT * chunk)
                var = mean_var[:, :, 1]
                nc.gpsimd.tensor_tensor(ln_a[:, :], var, eps[:, :], ALU.add).then_inc(ln_step, 1)
                after(pool, ln_step, 6 * chunk + 1)
                nc.gpsimd.tensor_tensor(ln_r1[:, :], ln_a[:, :], expo[:, 0, :], ALU.pow).then_inc(ln_step, 1)
                after(pool, ln_step, 6 * chunk + 2)
                nc.gpsimd.tensor_tensor(ln_b[:, :], var, ln_r1[:, :], ALU.mult).then_inc(ln_step, 1)
                after(pool, ln_step, 6 * chunk + 3)
                nc.gpsimd.tensor_tensor(ln_c[:, :], ln_b[:, :], ln_r1[:, :], ALU.mult).then_inc(ln_step, 1)
                after(pool, ln_step, 6 * chunk + 4)
                nc.gpsimd.tensor_tensor(ln_a[:, :], ln_c[:, :], eps[:, :], ALU.add).then_inc(ln_step, 1)
                after(pool, ln_step, 6 * chunk + 5)
                nc.gpsimd.tensor_tensor(ln_r2[:, :], ln_a[:, :], expo[:, 0, :], ALU.pow).then_inc(ln_step, 1)
                after(pool, ln_step, 6 * chunk + 6)
                nc.gpsimd.tensor_tensor(ln_r[:, :], ln_r1[:, :], ln_r2[:, :], ALU.mult).then_inc(rstd_ready, 1)

            def step(i, k):
                if real(i, k + 2, UNITS):
                    queries_lo(i, k + 2)
                if real(i, k - 1, UNITS):
                    outputs_lo(i, k - 1)
                if k % KB in (0, 1):
                    x_lo(i, k // KB + 1, 2 * (k % KB))
                if real(i, k - 5, UNITS):
                    bias_residual(i, k - 5)
                if real(i, k, UNITS):
                    probabilities_lo(i, k, 3)
                if k % KB in (0, 1):
                    x_lo(i, k // KB + 1, 2 * (k % KB) + 1)
                if k % KB == 2:
                    row_scales(i, k // KB + 2)

            every_step(pool, step)


def feed_forward(nc, env):
    g = env.get
    eps, pause = g("eps"), g("pause")
    (gates, half_gate, expo, b2_rows, ident, lng_c, lnb_c, b1_c, x1_chunks, out_tiles, fc1_q, fc1_scales, fc2_q,
     fc2_scales) = (g(n) for n in (
         "gates", "half_gate", "expo", "b2_rows", "ident", "lng_c", "lnb_c", "b1_c", "x1_chunks", "out_tiles",
         "fc1_q", "fc1_scales", "fc2_q", "fc2_scales"))
    B, D, F, KB, FB, TT, NCHUNK = (g(n) for n in ("B", "D", "F", "KB", "FB", "TT", "NCHUNK"))
    LAG = 2
    PER = 2 * FB
    STEPS = NCHUNK * FB
    LOOPS = STEPS // PER

    with ExitStack() as scope:
        def sb(name, shape, dt):
            return scope.enter_context(nc.sbuf_tensor(name, shape, dt))

        def sem(name):
            return scope.enter_context(nc.semaphore(name))

        w1_hi, w1_lo = sb("w1_hi", [P, KB, F], F32R), sb("w1_lo", [P, KB, F], F32R)
        w2_hi, w2_lo = sb("w2_hi", [P, FB, D], F32R), sb("w2_lo", [P, FB, D], F32R)
        dequantise(nc, env, w1_hi, w1_lo, w2_hi, w2_lo)

        x1 = [sb(f"x1_{n}", [P, TT, D], F32) for n in range(2)]
        x1_norm = sb("x1_norm", [P, TT, D], F32)
        ht_f = [sb(f"ht_f{n}", [P, CHUNK], F32) for n in range(2)]
        ht_hi = [sb(f"ht_hi{n}", [P, KB, CHUNK], F32R) for n in range(2)]
        ht_lo = [sb(f"ht_lo{n}", [P, KB, CHUNK], F32R) for n in range(2)]
        y_f = [sb(f"y_f{n}", [P, CHUNK], F32) for n in range(2)]
        y_hi = [sb(f"y_hi{n}", [P, CHUNK], F32R) for n in range(4)]
        y_lo = [sb(f"y_lo{n}", [P, CHUNK], F32R) for n in range(4)]
        out_sb = [sb(f"out_sb{n}", [P, D], F32) for n in range(2)]
        stats = sb("y_stats", [P, TT, 6], F32)
        mean_var = sb("y_mean_var", [P, TT, 2], F32)
        ln_a, ln_r1, ln_b, ln_c, ln_r2, ln_s2, ln_r, u_scale = (
            sb(n, [P, TT], F32) for n in ("fa", "fr1", "fb", "fc", "fr2", "fs2", "fr", "u_scale"))

        def psum(name):
            return scope.enter_context(nc.psum_tensor(name, [P, 512], F32))

        ps_y = [psum("ps_y0"), psum("ps_y1")]
        ps_h = [psum("ps_h0"), psum("ps_h1")]
        ps_z = [psum(f"ps_z{t}") for t in range(TT)]

        x1_loaded = [sem("x1_loaded0"), sem("x1_loaded1")]
        out_stored = [sem("out_stored0"), sem("out_stored1")]
        (stats_some, stats_ready, ln_step, scales_ready, norm_ready, sum_ready, base_ready, h_turned, h_f_ready,
         h_hi_ready, h_lo_ready, y_done, y_f_ready, y_hi_ready, y_lo_ready, z_used, z_done, out_ready) = (
            sem(n) for n in ("f_stats_some", "f_stats_ready", "f_ln_step", "f_scales_ready", "f_norm_ready",
                             "sum_ready", "base_ready", "h_turned", "h_f_ready", "h_hi_ready", "h_lo_ready", "y_done",
                             "y_f_ready", "y_hi_ready", "y_lo_ready", "z_used", "z_done", "out_ready"))

        def every_step(eng, step):
            for k in range(-FB, PER):
                step(0, k)
            with eng.Fori(1, LOOPS - 1) as i:
                for k in range(PER):
                    step(i, k)
            for k in range(PER + LAG + 1):
                step(LOOPS - 1, k)

        def real(i, k):
            return not isinstance(i, int) or 0 <= PER * i + k < STEPS

        LOAD, STATS, SCALES, NORM, TURN, BASE = 3, 5, 6, 7, 10, 14
        EVACUATE = LAG

        block = scope.enter_context(nc.Block())

        @block.sync
        def _(sp):
            def step(i, k):
                c, f = k // FB, k % FB
                if f == LOAD and real(i, FB * (c + 1)):
                    chunk = 2 * i + c + 1
                    source = x1_chunks[(c + 1) % 2, i + (c + 1) // 2, :, :, :]
                    sp.lower_val(source.offset * 4)
                    after(sp, out_ready, TT * (chunk - 1))
                    sp.dma_start(x1[(c + 1) % 2][:, :, :], source)\
                        .then_inc(x1_loaded[(c + 1) % 2], 16)
                if f == EVACUATE and real(i, FB * (c - 1)):
                    for t in range(TT):
                        target = out_tiles[(c - 1) % 2, i + (c - 1) // 2, t, :, :]
                        sp.lower_val(target.offset * 4)
                        after(sp, out_ready, TT * (2 * i + c - 1) + t + 1)
                        sp.dma_start(target, out_sb[t % 2][:, :])\
                            .then_inc(out_stored[t % 2], 16)

            every_step(sp, step)
            for s in out_stored:
                sp.wait_ge(s, 16 * TT // 2 * NCHUNK)

        @block.tensor
        def _(pe):
            def hidden(i, k):
                s, c, f = PER * i + k, (k // FB) % 2, k % FB
                if f == 0:
                    after(pe, h_hi_ready, KB * (2 * i + k // FB + 1))
                    after(pe, h_lo_ready, KB * (2 * i + k // FB + 1))
                after(pe, y_f_ready, s - 1)
                block = slice(f * P, (f + 1) * P)
                split_product(nc, ps_y[f % 2][:, :], [(w1_hi[:, n, block], w1_lo[:, n, block]) for n in range(KB)],
                              [(ht_hi[c][:, n, :], ht_lo[c][:, n, :]) for n in range(KB)]).then_inc(y_done, 1)

            def sums(i, k):
                s, f = PER * i + k, k % FB
                after(pe, y_hi_ready, s + 1)
                after(pe, y_lo_ready, s + 1)
                for t in range(TT):
                    if f == 0:
                        after(pe, out_ready, TT * (2 * i + k // FB - 1) + t + 1)
                    tokens = slice(t * P, (t + 1) * P)
                    hi, lo = y_hi[f % 4][:, tokens], y_lo[f % 4][:, tokens]
                    nc.tensor.matmul(ps_z[t][:, :], hi, w2_hi[:, f, :], start=(f == 0), stop=False)
                    nc.tensor.matmul(ps_z[t][:, :], hi, w2_lo[:, f, :], start=False, stop=False)
                    last = nc.tensor.matmul(ps_z[t][:, :], lo, w2_hi[:, f, :], start=False, stop=(f == FB - 1))
                last.then_inc(z_used, 1)

            def turn_h(i, c, n):
                if not real(i, FB * c):
                    return
                chunk = 2 * i + c
                after(pe, norm_ready, TT * (chunk + 1))
                after(pe, h_f_ready, KB * chunk + n - 1)
                for t in range(TT):
                    last = nc.tensor.transpose(ps_h[n % 2][:, t * P:(t + 1) * P], x1_norm[:, t, n * P:(n + 1) * P], ident[:, :])
                last.then_inc(h_turned, 1)

            def step(i, k):
                if real(i, k):
                    hidden(i, k)
                if TURN <= k % FB < TURN + KB:
                    turn_h(i, k // FB + 1, k % FB - TURN)
                if real(i, k - LAG):
                    sums(i, k - LAG)

            every_step(pe, step)

        @block.scalar
        def _(act):
            def step(i, k):
                if real(i, k):
                    s, f = PER * i + k, k % FB
                    after(act, y_done, s + 1)
                    after(act, y_hi_ready, s - 1)
                    after(act, y_lo_ready, s - 1)
                    nc.scalar.activation(y_f[f % 2][:, :], ps_y[f % 2][:, :], ACT.Silu, bias=b1_c[:, f:f + 1]).then_inc(y_f_ready, 1)
                if TURN <= k % FB < TURN + KB and real(i, FB * (k // FB + 1)):
                    n = k % FB - TURN
                    job = KB * (2 * i + k // FB + 1) + n
                    after(act, h_turned, job + 1)
                    after(act, h_hi_ready, job - 1)
                    after(act, h_lo_ready, job - 1)
                    nc.scalar.activation(ht_f[n % 2][:, :], ps_h[n % 2][:, :], ACT.Identity, bias=lnb_c[:, n:n + 1],
                                         scale=lng_c[:, n:n + 1]).then_inc(h_f_ready, 1)

            every_step(act, step)

        @block.vector
        def _(dve):
            def split_hidden(i, k):
                s, f = PER * i + k, k % FB
                after(dve, y_f_ready, s + 1)
                after(dve, z_used, s - 3)
                nc.vector.tensor_copy(y_hi[f % 4][:, :], y_f[f % 2][:, :]).then_inc(y_hi_ready, 1)
                after(dve, y_hi_ready, s + 1)
                nc.vector.tensor_tensor(y_lo[f % 4][:, :], y_f[f % 2][:, :], y_hi[f % 4][:, :].bitcast(F32),
                                        ALU.subtract).then_inc(y_lo_ready, 1)

            def split_h(i, c, n):
                chunk = 2 * i + c
                after(dve, h_f_ready, KB * chunk + n + 1)
                after(dve, y_done, FB * (chunk - 1))
                nc.vector.tensor_copy(ht_hi[c % 2][:, n, :], ht_f[n % 2][:, :]).then_inc(h_hi_ready, 1)
                after(dve, h_hi_ready, KB * chunk + n + 1)
                nc.vector.tensor_tensor(ht_lo[c % 2][:, n, :], ht_f[n % 2][:, :], ht_hi[c % 2][:, n, :].bitcast(F32),
                                        ALU.subtract).then_inc(h_lo_ready, 1)

            def take_sums(i, c):
                chunk = 2 * i + c
                after(dve, z_used, FB * (chunk + 1))
                after(dve, base_ready, TT * (chunk + 1))
                for t in range(TT):
                    if t >= 2 or real(i, FB * (c - 1)):
                        after(dve, out_stored[t % 2], 16 * (TT // 2 * chunk + t // 2))
                    nc.vector.tensor_tensor(out_sb[t % 2][:, :], ps_z[t][:, :], x1[c % 2][:, t, :], ALU.add).then_inc(out_ready, 1)

            def step(i, k):
                c, f = k // FB, k % FB
                if real(i, k):
                    split_hidden(i, k)
                if f == EVACUATE and real(i, FB * (c - 1)):
                    take_sums(i, c - 1)
                if not real(i, FB * (c + 1)):
                    return
                chunk, b = 2 * i + c + 1, (c + 1) % 2
                if f == STATS:
                    after(dve, x1_loaded[b], 16 * (i + (c + 1) // 2 + 1))
                    after(dve, stats_ready, chunk)
                    for t in range(TT):
                        nc.vector.bn_stats(stats[:, t, :], x1[b][:, t, :]).then_inc(stats_some, 1)
                    after(dve, scales_ready, chunk)
                    after(dve, stats_some, TT * (chunk + 1))
                    nc.vector.memset(pause[:, :], 0.0)
                    for t in range(TT):
                        last = nc.vector.bn_aggr(mean_var[:, t, :], stats[:, t, :])
                    last.then_inc(stats_ready, 1)
                if f == NORM:
                    after(dve, scales_ready, chunk + 1)
                    after(dve, h_turned, KB * chunk)
                    after(dve, sum_ready, TT * chunk)
                    for t in range(TT):
                        nc.vector.tensor_scalar(x1_norm[:, t, :], x1[b][:, t, :], mean_var[:, t, 0:1], ln_r[:, t:t + 1],
                                                ALU.subtract, ALU.mult).then_inc(norm_ready, 1)
                if TURN <= f < TURN + KB:
                    split_h(i, c + 1, f - TURN)
                if f == BASE:
                    for t in range(TT):
                        after(dve, norm_ready, TT * chunk + t + 1)
                        nc.vector.scalar_tensor_tensor(out=x1[b][:, t, :], in0=x1_norm[:, t, :], scalar=u_scale[:, t:t + 1],
                                                       in1=x1[b][:, t, :], op0=ALU.mult, op1=ALU.add).then_inc(sum_ready, 1)

            every_step(dve, step)

        @block.gpsimd
        def _(pool):
            def step(i, k):
                c, f = k // FB, k % FB
                if not real(i, FB * (c + 1)):
                    return
                chunk, b = 2 * i + c + 1, (c + 1) % 2
                if f == SCALES:
                    after(pool, stats_ready, chunk + 1)
                    after(pool, norm_ready, TT * chunk)
                    after(pool, sum_ready, TT * chunk)
                    var = mean_var[:, :, 1]
                    steps = 7 * chunk
                    nc.gpsimd.tensor_tensor(ln_a[:, :], var, eps[:, :], ALU.add).then_inc(ln_step, 1)
                    after(pool, ln_step, steps + 1)
                    nc.gpsimd.tensor_tensor(ln_r1[:, :], ln_a[:, :], expo[:, 0, :], ALU.pow).then_inc(ln_step, 1)
                    after(pool, ln_step, steps + 2)
                    nc.gpsimd.tensor_tensor(ln_b[:, :], var, ln_r1[:, :], ALU.mult).then_inc(ln_step, 1)
                    after(pool, ln_step, steps + 3)
                    nc.gpsimd.tensor_tensor(ln_c[:, :], ln_b[:, :], ln_r1[:, :], ALU.mult).then_inc(ln_step, 1)
                    after(pool, ln_step, steps + 4)
                    nc.gpsimd.tensor_tensor(ln_a[:, :], ln_c[:, :], eps[:, :], ALU.add).then_inc(ln_step, 1)
                    after(pool, ln_step, steps + 5)
                    nc.gpsimd.tensor_tensor(ln_r2[:, :], ln_a[:, :], expo[:, 0, :], ALU.pow).then_inc(ln_step, 1)
                    nc.gpsimd.tensor_tensor(ln_s2[:, :], ln_a[:, :], expo[:, 1, :], ALU.pow).then_inc(ln_step, 1)
                    after(pool, ln_step, steps + 7)
                    nc.gpsimd.tensor_tensor(u_scale[:, :], ln_s2[:, :], gates[:, 1:2].to_broadcast([P, TT]), ALU.mult)
                    nc.gpsimd.tensor_tensor(ln_r[:, :], ln_r1[:, :], ln_r2[:, :], ALU.mult).then_inc(scales_ready, 1)
                if f == BASE:
                    for t in range(TT):
                        after(pool, sum_ready, TT * chunk + t + 1)
                        nc.gpsimd.tensor_tensor(x1[b][:, t, :], x1[b][:, t, :], b2_rows[:, :], ALU.add).then_inc(base_ready, 1)

            every_step(pool, step)


def dequantise(nc, env, w1_hi, w1_lo, w2_hi, w2_lo):
    g = env.get
    fc1_q, fc1_scales, fc2_q, fc2_scales, half_gate = (
        g(n) for n in ("fc1_q", "fc1_scales", "fc2_q", "fc2_scales", "half_gate"))
    D, F, KB, FB = (g(n) for n in ("D", "F", "KB", "FB"))
    NB = FB // 4
    with ExitStack() as scope:
        q_sb = [scope.enter_context(nc.sbuf_tensor(f"q_sb{n}", [P, F], I32)) for n in range(2)]
        s_sb = [scope.enter_context(nc.sbuf_tensor(f"s_sb{n}", [P, F], F32)) for n in range(2)]
        w_f = [scope.enter_context(nc.sbuf_tensor(f"w_f{n}", [P, F], F32)) for n in range(2)]
        piece_loaded = [scope.enter_context(nc.semaphore(f"piece_loaded{n}")) for n in range(2)]
        w_ready, hi_ready, lo_ready = (scope.enter_context(nc.semaphore(n)) for n in ("w_ready", "w_hi_ready", "w_lo_ready"))
        block = scope.enter_context(nc.Block())

        q1 = fc1_q.rearrange("(n p) f -> n p f", p=P)
        q2 = fc2_q.rearrange("(n r p) d -> n p r d", p=P, r=4)
        s2 = fc2_scales.rearrange("(n r) d -> n (r d)", r=4)
        pieces = KB + NB
        hi = [w1_hi[:, n, :] for n in range(KB)] + [w2_hi[:, 4 * n:4 * n + 4, :].rearrange("p r d -> p (r d)") for n in range(NB)]
        lo = [w1_lo[:, n, :] for n in range(KB)] + [w2_lo[:, 4 * n:4 * n + 4, :].rearrange("p r d -> p (r d)") for n in range(NB)]

        @block.sync
        def _(sp):
            for n in range(pieces):
                if n >= 2:
                    sp.wait_ge(w_ready, n - 1)
                if n < KB:
                    sp.dma_start(q_sb[n % 2][:, :], q1[n, :, :]).then_inc(piece_loaded[n % 2], 16)
                    sp.dma_start(s_sb[n % 2][:, :], fc1_scales[n, :].partition_broadcast(P)).then_inc(piece_loaded[n % 2], 16)
                else:
                    sp.dma_start(q_sb[n % 2][:, :].rearrange("p (r d) -> p r d", r=4), q2[n - KB, :, :, :])\
                        .then_inc(piece_loaded[n % 2], 16)
                    sp.dma_start(s_sb[n % 2][:, :], s2[n - KB, :].partition_broadcast(P)).then_inc(piece_loaded[n % 2], 16)

        @block.vector
        def _(dve):
            for n in range(pieces):
                dve.wait_ge(piece_loaded[n % 2], 32 * (n // 2 + 1))
                if n >= 2:
                    dve.wait_ge(hi_ready, n - 1)
                    dve.wait_ge(lo_ready, n - 1)
                nc.vector.scalar_tensor_tensor(out=w_f[n % 2][:, :], in0=q_sb[n % 2][:, :], scalar=-128.0, in1=s_sb[n % 2][:, :],
                                               op0=ALU.add, op1=ALU.mult).then_inc(w_ready, 1)
                dve.wait_ge(hi_ready, n + 1)
                if n < KB:
                    nc.vector.tensor_tensor(lo[n], w_f[n % 2][:, :], hi[n].bitcast(F32), ALU.subtract).then_inc(lo_ready, 1)
                else:
                    nc.vector.scalar_tensor_tensor(out=lo[n], in0=w_f[n % 2][:, :], scalar=half_gate[:, :], in1=hi[n].bitcast(F32),
                                                   op0=ALU.mult, op1=ALU.subtract).then_inc(lo_ready, 1)

        @block.scalar
        def _(act):
            for n in range(pieces):
                act.wait_ge(w_ready, n + 1)
                if n < KB:
                    nc.scalar.copy(hi[n], w_f[n % 2][:, :]).then_inc(hi_ready, 1)
                else:
                    nc.scalar.activation(hi[n], w_f[n % 2][:, :], ACT.Identity, scale=half_gate[:, :]).then_inc(hi_ready, 1)


_INS = ['x', 'ctx_1024', 'mask_BxS2_ik0', 'g_xattn', 'g_ffn', 'L0_xattn_w_q', 'L0_xattn_w_kv', 'L0_xattn_w_proj',
        'L0_xattn_b_proj', 'L0_xattn_g_x', 'L0_xattn_b_x', 'L0_xattn_g_kv', 'L0_xattn_b_kv', 'L0_ffn_ln_gamma',
        'L0_ffn_ln_beta', 'L0_ffn_fc1_q', 'L0_ffn_fc1_scales', 'L0_ffn_fc1_bias', 'L0_ffn_fc2_q', 'L0_ffn_fc2_scales',
        'L0_ffn_fc2_bias']


def kernel(**inputs):
    import concourse.bacc as bacc
    from concourse.bass_utils import run_bass_kernel_spmd

    nc = bacc.Bacc("TRN2", target_bir_lowering=False, num_devices=1, dynamic_dma_scratch_size=1024)
    arrays, args = {}, []
    for name in _INS:
        a = np.ascontiguousarray(inputs[name])
        arrays[f"in_{name}"] = a
        args.append(nc.dram_tensor(f"in_{name}", a.shape, mybir.dt.from_np(a.dtype), kind="ExternalInput").ap())
    out = nc.dram_tensor("out", arrays["in_x"].shape, F32, kind="ExternalOutput").ap()
    build(nc, *args, out)
    r = run_bass_kernel_spmd(nc, [arrays], core_ids=[0])
    return r.results[0]["out"]
```

```python
from contextlib import ExitStack

import numpy as np

import concourse.bass as bass
from concourse import mybir

F32 = mybir.dt.float32
F32R = mybir.dt.float32r
F16 = mybir.dt.float16
BF16 = mybir.dt.bfloat16
I32 = mybir.dt.int32
ALU = mybir.AluOpType
ACT = mybir.ActivationFunctionType
AX = mybir.AxisListType

P = 128
HEAD = 32
HG = P // HEAD
CHUNK = 512
EPS = 1e-5
FILL = -1e9


def after(eng, semaphore, count):
    if not isinstance(count, int) or count > 0:
        eng.wait_ge(semaphore, count)


def build(nc, x, ctx, mask, g_xattn, g_ffn, w_q, w_kv, w_proj, b_proj, g_x, b_x, g_kv, b_kv,
          ln_gamma, ln_beta, fc1_q, fc1_scales, fc1_bias, fc2_q, fc2_scales, fc2_bias, out):
    B, S, D = x.shape
    KEYS = ctx.shape[1]
    F = fc1_q.shape[1]
    KB = D // P
    FB = F // P
    TT = CHUNK // P
    NCHUNK = B * S // CHUNK
    SCALE = HEAD ** -0.5
    assert B == 2 and KEYS == P and KB == HG and FB % 4 == 0 and NCHUNK % 2 == 0

    rows = "b (c t p) d -> b c t p d"
    x_tiles = x.rearrange(rows, t=TT, p=P)
    out_chunks = out.rearrange("b (c t p) d -> b c p t d", t=TT, p=P)
    x1_dram = nc.dram_tensor("x1_dram", (B, S, D), F32, kind="Internal").ap()
    x1_tiles = x1_dram.rearrange(rows, t=TT, p=P)
    chunk_rows = "b (c t p) d -> b c p t d"
    x_chunks = x.rearrange(chunk_rows, t=TT, p=P)
    x1_chunks = x1_dram.rearrange(chunk_rows, t=TT, p=P)

    def sems(scope, *names):
        return [scope.enter_context(nc.semaphore(n)) for n in names]

    with ExitStack() as whole:
        def sb(name, shape, dt, scope=whole):
            return scope.enter_context(nc.sbuf_tensor(name, shape, dt))

        ident = sb("ident", [P, P], F32)
        cols = sb("cols", [P, 6 * KB + FB], F32)
        gx_c, bx_c, gkv_c, bkv_c, lng_c, lnb_c = (cols[:, KB * n:KB * n + KB] for n in range(6))
        b1_c = cols[:, 6 * KB:6 * KB + FB]
        gates = sb("gates", [P, 2], F32)
        half_gate = sb("half_gate", [P, 1], F32)
        expo = sb("expo", [P, 2, TT], F32)
        eps = sb("eps", [P, TT], F32)
        pause = sb("pause", [P, 1], F32)
        b2_rows = sb("b2_rows", [P, D], F32)

        with ExitStack() as attn:
            def ab(name, shape, dt):
                return sb(name, shape, dt, attn)

            wq_hi, wq_lo = ab("wq_hi", [P, KB, D], F32R), ab("wq_lo", [P, KB, D], F32R)
            wp_hi, wp_lo = ab("wp_hi", [P, KB, D], F32R), ab("wp_lo", [P, KB, D], F32R)
            k_hi, k_lo = (ab(n, [P, B, KB, HG, KEYS], F32R) for n in ("k_hi", "k_lo"))
            v_parts = [ab(f"v{n}", [P, B, D], BF16) for n in range(3)]
            fill_col = ab("fill_col", [P, B], F32)
            minus_row = ab("minus_row", [P, HG, KEYS], F32R)
            ones16 = ab("ones16", [P, HEAD], BF16)
            bp_rows = ab("bp_rows", [P, D], F32)
            max_row = [ab(f"max_row{n}", [P, CHUNK], F32R) for n in range(2)]

            setup(nc, locals())
            attention(nc, locals())

        feed_forward(nc, locals())


def setup(nc, env):
    g = env.get
    (ctx, mask, w_q, w_kv, w_proj, b_proj, ident, cols, gates, half_gate, expo, b2_rows, k_hi, k_lo, v_parts,
     fill_col, minus_row, ones16, bp_rows, max_row) = (g(n) for n in (
         "ctx", "mask", "w_q", "w_kv", "w_proj", "b_proj", "ident", "cols", "gates", "half_gate", "expo",
         "b2_rows", "k_hi", "k_lo", "v_parts", "fill_col", "minus_row", "ones16", "bp_rows", "max_row"))
    B, D, KB, FB, KEYS, TT = (g(n) for n in ("B", "D", "KB", "FB", "KEYS", "TT"))
    gkv_c, bkv_c = g("gkv_c"), g("bkv_c")
    vectors = [g(n) for n in ("g_x", "b_x", "g_kv", "b_kv", "ln_gamma", "ln_beta", "fc1_bias")]
    NV = 6 * KB + FB

    with ExitStack() as scope:
        def sb(name, shape, dt):
            return scope.enter_context(nc.sbuf_tensor(name, shape, dt))

        def sem(name):
            return scope.enter_context(nc.semaphore(name))

        vec_rows = sb("vec_rows", [NV, P], F32)
        ctx_sb = sb("ctx_sb", [P, B, D], F32)
        ctx_n = sb("ctx_n", [P, B, D], F32)
        ctx_t = sb("ctx_t", [P, KB, B * KEYS], F32)
        mask_rows = sb("mask_rows", [P, B * KEYS], I32)
        mask_col = sb("mask_col", [P, B], I32)
        wkv = sb("wkv", [P, KB, 2 * D], F32)
        wq_raw = sb("wq_raw", [P, KB, D], F32)
        wp_raw = sb("wp_raw", [P, KB, D], F32)
        valid = sb("valid", [P, B * KEYS], F32)
        masked = sb("masked", [P, B * KEYS], F32)
        n_valid = sb("n_valid", [P, B], F32)
        some_valid = sb("some_valid", [P, B], F32)
        divisor = sb("divisor", [P, B], F32)
        inv_divisor = sb("inv_divisor", [P, B], F32)
        k_masked = sb("k_masked", [P, KB, B * KEYS], F32)
        k_sum = sb("k_sum", [P, KB, B], F32)
        k_mean = sb("k_mean", [P, KB, B], F32)
        k_full = sb("k_full", [P, KB, B, KEYS], F32)
        v_rest = sb("v_rest", [P, B, D], F32)
        minus_f = sb("minus_f", [P, HG, KEYS], F32)
        fill_a = sb("fill_a", [P, B], F32)
        stats = sb("c_stats", [P, B, 6], F32)
        mean_var = sb("c_mean_var", [P, B, 2], F32)
        var_eps = sb("c_var_eps", [P, B], F32)
        rstd = sb("c_rstd", [P, B], F32)
        ps = [scope.enter_context(nc.psum_tensor(f"sp{n}", [P, 512], F32)) for n in range(8)]
        ps_cols, ps_k, ps_v, ps_t = ps[7], ps[0:4], ps[4:6], ps[6]

        vec_loaded, ctx_loaded, mask_loaded, gate_loaded, wkv_loaded, wq_loaded, wp_loaded, bias_loaded = (
            sem(n) for n in ("vec_loaded", "ctx_loaded", "mask_loaded", "gate_loaded", "wkv_loaded", "wq_loaded",
                             "wp_loaded", "bias_loaded"))
        (ident_ready, pool_step, vec_t, cols_ready, tanh_ready, ctx_stats, ctx_rstd, ctx_normed, ctx_turned,
         ctx_t_ready, k_done, v_done, dve_step, act_step, zeroed) = (
            sem(n) for n in ("ident_ready", "pool_step", "vec_t", "cols_ready", "tanh_ready", "ctx_stats",
                             "ctx_rstd", "ctx_normed", "ctx_turned", "ctx_t_ready", "k_done", "v_done",
                             "dve_step", "act_step", "zeroed"))

        block = scope.enter_context(nc.Block())

        @block.sync
        def _(sp):
            at = 0
            for v in vectors:
                n = v.shape[0] // P
                sp.dma_start(vec_rows[at:at + n, :], v.rearrange("(n p) -> n p", p=P)).then_inc(vec_loaded, 16)
                at += n
            sp.dma_start(ctx_sb[:, :, :], ctx.rearrange("b p d -> p b d")).then_inc(ctx_loaded, 16)
            sp.dma_start(wkv[:, :, :], w_kv.rearrange("(k p) n -> p k n", p=P)).then_inc(wkv_loaded, 16)
            sp.dma_start(wp_raw[:, :, :], w_proj.rearrange("(k p) n -> p k n", p=P)).then_inc(wp_loaded, 16)

        @block.scalar
        def _(act):
            act.dma_start(gates[:, 0:1], g("g_xattn").partition_broadcast(P)).then_inc(gate_loaded, 16)
            act.dma_start(gates[:, 1:2], g("g_ffn").partition_broadcast(P)).then_inc(gate_loaded, 16)
            act.dma_start(mask_rows[:, :], mask.rearrange("b k -> (b k)").partition_broadcast(P)).then_inc(mask_loaded, 16)
            for b in range(B):
                act.dma_start(mask_col[:, b:b + 1], mask[b, :].rearrange("(k a) -> k a", a=1)).then_inc(mask_loaded, 16)
            act.dma_start(wq_raw[:, :, :], w_q.rearrange("(k p) n -> p k n", p=P)).then_inc(wq_loaded, 16)
            act.dma_start(bp_rows[:, :], b_proj.partition_broadcast(P)).then_inc(bias_loaded, 16)
            act.dma_start(b2_rows[:, :], g("fc2_bias").partition_broadcast(P)).then_inc(bias_loaded, 16)
            act.wait_ge(gate_loaded, 32)
            nc.scalar.activation(gates[:, :], gates[:, :], ACT.Tanh).then_inc(tanh_ready, 1)
            act.wait_ge(tanh_ready, 1)
            nc.scalar.mul(half_gate[:, :], gates[:, 1:2], 0.5).then_inc(tanh_ready, 1)
            act.wait_ge(cols_ready, 1)
            for k in range(KB):
                act.wait_ge(ctx_turned, k + 1)
                nc.scalar.activation(ctx_t[:, k, :], ps[k % 2][:, 0:B * KEYS], ACT.Identity,
                                     bias=bkv_c[:, k:k + 1], scale=gkv_c[:, k:k + 1]).then_inc(ctx_t_ready, 1)
            act.wait_ge(wq_loaded, 16)
            nc.scalar.copy(g("wq_hi")[:, :, :], wq_raw[:, :, :]).then_inc(act_step, 1)

        @block.gpsimd
        def _(pool):
            done = [0]

            def link(ins):
                done[0] += 1
                ins.then_inc(pool_step, 1)
                pool.wait_ge(pool_step, done[0])

            link(nc.gpsimd.memset(ident[:, :], 0.0))
            nc.gpsimd.affine_select(out=ident[:, :], in_=ident[:, :], compare_op=ALU.not_equal, fill=1.0, base=0,
                                    pattern=[[-1, P]], channel_multiplier=1).then_inc(ident_ready, 1)
            nc.gpsimd.memset(ones16[:, :], 1.0)
            nc.gpsimd.memset(expo[:, 1, :], 0.5)
            nc.gpsimd.memset(g("eps")[:, :], EPS)
            link(nc.gpsimd.memset(expo[:, 0, :], -0.5))
            pool.wait_ge(ctx_stats, 1)
            link(nc.gpsimd.tensor_scalar(var_eps[:, :], mean_var[:, :, 1], EPS, None, ALU.add))
            nc.gpsimd.tensor_tensor(rstd[:, :], var_eps[:, :], expo[:, 0, 0:B], ALU.pow).then_inc(ctx_rstd, 1)
            nc.gpsimd.memset(max_row[0][:, :].bitcast(F32), 0.0)
            nc.gpsimd.memset(max_row[1][:, :].bitcast(F32), 0.0)
            link(nc.gpsimd.memset(minus_f[:, :, :], 0.0))
            link(nc.gpsimd.affine_select(out=minus_f[:, :, :], in_=minus_f[:, :, :], compare_op=ALU.not_equal,
                                         fill=-1.0, base=0, pattern=[[-1, HG], [0, KEYS]], channel_multiplier=1))
            nc.gpsimd.tensor_copy(minus_row[:, :, :], minus_f[:, :, :])
            pool.wait_ge(act_step, 1)
            for k in range(KB):
                nc.gpsimd.tensor_tensor(g("wq_lo")[:, k, :], wq_raw[:, k, :], g("wq_hi")[:, k, :].bitcast(F32), ALU.subtract)

        @block.tensor
        def _(pe):
            pe.wait_ge(ident_ready, 1)
            pe.wait_ge(vec_loaded, 16 * len(vectors))
            nc.tensor.transpose(ps_cols[:, 0:NV], vec_rows[:, :], ident[0:NV, 0:NV]).then_inc(vec_t, 1)
            pe.wait_ge(ctx_normed, 1)
            for k in range(KB):
                if k >= 2:
                    pe.wait_ge(ctx_t_ready, k - 1)
                for b in range(B):
                    last = nc.tensor.transpose(ps[k % 2][:, b * KEYS:(b + 1) * KEYS], ctx_n[:, b, k * P:(k + 1) * P],
                                               ident[:, :])
                last.then_inc(ctx_turned, 1)
            pe.wait_ge(ctx_t_ready, KB)
            pe.wait_ge(wkv_loaded, 16)
            for m in range(KB):
                for k in range(KB):
                    last = nc.tensor.matmul(ps_k[m][:, 0:B * KEYS], wkv[:, k, m * P:(m + 1) * P], ctx_t[:, k, :],
                                            start=(k == 0), stop=(k == KB - 1))
                last.then_inc(k_done, 1)
            for b in range(B):
                for k in range(KB):
                    last = nc.tensor.matmul(ps_v[b][:, :], ctx_t[:, k, b * KEYS:(b + 1) * KEYS], wkv[:, k, D:2 * D],
                                            start=(k == 0), stop=(k == KB - 1))
                last.then_inc(v_done, 1)

        @block.vector
        def _(dve):
            done = [0]

            def link(ins):
                done[0] += 1
                ins.then_inc(dve_step, 1)
                dve.wait_ge(dve_step, done[0])

            nc.vector.memset(k_hi[:, :, :, :, :].bitcast(F32), 0.0)
            link(nc.vector.memset(k_lo[:, :, :, :, :].bitcast(F32), 0.0))
            dve.wait_ge(ctx_loaded, 16)
            for b in range(B):
                last = nc.vector.bn_stats(stats[:, b, :], ctx_sb[:, b, :])
            link(last)
            for b in range(B):
                last = nc.vector.bn_aggr(mean_var[:, b, :], stats[:, b, :])
            last.then_inc(ctx_stats, 1)
            dve.wait_ge(ctx_rstd, 1)
            for b in range(B):
                last = nc.vector.tensor_scalar(ctx_n[:, b, :], ctx_sb[:, b, :], mean_var[:, b, 0:1], rstd[:, b:b + 1],
                                               ALU.subtract, ALU.mult)
            last.then_inc(ctx_normed, 1)
            dve.wait_ge(vec_t, 1)
            nc.vector.tensor_copy(cols[:, :], ps_cols[:, 0:NV]).then_inc(cols_ready, 1)
            dve.wait_ge(mask_loaded, 16 * (1 + B))
            nc.vector.tensor_scalar(masked[:, :], mask_rows[:, :], 0.0, None, ALU.is_equal)
            link(nc.vector.tensor_scalar(valid[:, :], mask_rows[:, :], 0.0, None, ALU.not_equal))
            link(nc.vector.reduce_sum(n_valid[:, :], valid[:, :].rearrange("p (b k) -> p b k", b=B), AX.X))
            nc.vector.tensor_scalar(some_valid[:, :], n_valid[:, :], 1.0, None, ALU.min)
            link(nc.vector.tensor_scalar(divisor[:, :], n_valid[:, :], 1.0, None, ALU.max))
            link(nc.vector.reciprocal(inv_divisor[:, :], divisor[:, :]))
            link(nc.vector.tensor_scalar(fill_a[:, :], mask_col[:, :], 0.0, FILL, ALU.is_equal, ALU.mult))
            nc.vector.tensor_tensor(fill_col[:, :], fill_a[:, :], some_valid[:, :], ALU.mult)
            dve.wait_ge(tanh_ready, 2)
            dve.wait_ge(wp_loaded, 16)
            link(nc.vector.tensor_scalar(wp_raw[:, :, :], wp_raw[:, :, :], gates[:, 0:1], None, ALU.mult))
            link(nc.vector.tensor_copy(g("wp_hi")[:, :, :], wp_raw[:, :, :]))
            nc.vector.tensor_tensor(g("wp_lo")[:, :, :], wp_raw[:, :, :], g("wp_hi")[:, :, :].bitcast(F32), ALU.subtract)
            dve.wait_ge(bias_loaded, 32)
            nc.vector.tensor_scalar(bp_rows[:, :], bp_rows[:, :], gates[:, 0:1], None, ALU.mult)
            nc.vector.tensor_scalar(b2_rows[:, :], b2_rows[:, :], half_gate[:, :], None, ALU.mult)
            for m in range(KB):
                dve.wait_ge(k_done, m + 1)
                last = nc.vector.tensor_tensor(k_masked[:, m, :], ps_k[m][:, 0:B * KEYS], valid[:, :], ALU.mult)
            link(last)
            link(nc.vector.reduce_sum(k_sum[:, :, :], k_masked[:, :, :].rearrange("p m (b k) -> p m b k", b=B), AX.X))
            for b in range(B):
                last = nc.vector.tensor_scalar(k_mean[:, :, b], k_sum[:, :, b], inv_divisor[:, b:b + 1], None, ALU.mult)
            link(last)
            for m in range(KB):
                for b in range(B):
                    keys = slice(b * KEYS, (b + 1) * KEYS)
                    last = nc.vector.scalar_tensor_tensor(
                        out=k_full[:, m, b, :], in0=masked[:, keys], scalar=k_mean[:, m, b:b + 1],
                        in1=k_masked[:, m, keys], op0=ALU.mult, op1=ALU.add)
            link(last)
            for b in range(B):
                for j in range(HG):
                    at = slice(HEAD * j, HEAD * (j + 1))
                    last = nc.vector.tensor_copy(k_hi[at, b, :, j, :], k_full[at, :, b, :])
            link(last)
            for b in range(B):
                for j in range(HG):
                    at = slice(HEAD * j, HEAD * (j + 1))
                    nc.vector.tensor_tensor(k_lo[at, b, :, j, :], k_full[at, :, b, :], k_hi[at, b, :, j, :].bitcast(F32),
                                            ALU.subtract)
            for b in range(B):
                dve.wait_ge(v_done, b + 1)
                link(nc.vector.tensor_copy(v_parts[0][:, b, :], ps_v[b][:, :]))
                link(nc.vector.tensor_tensor(v_rest[:, b, :], ps_v[b][:, :], v_parts[0][:, b, :], ALU.subtract))
                link(nc.vector.tensor_copy(v_parts[1][:, b, :], v_rest[:, b, :]))
                nc.vector.tensor_tensor(v_parts[2][:, b, :], v_rest[:, b, :], v_parts[1][:, b, :], ALU.subtract)


def split_product(nc, out, stationary, moving, blocks=None):
    n = len(stationary)
    for k in blocks or range(n):
        (s_hi, s_lo), (m_hi, m_lo) = stationary[k], moving[k]
        nc.tensor.matmul(out, s_hi, m_hi, start=(k == 0), stop=False)
        nc.tensor.matmul(out, s_hi, m_lo, start=False, stop=False)
        last = nc.tensor.matmul(out, s_lo, m_hi, start=False, stop=(k == n - 1))
    return last


def attention(nc, env):
    g = env.get
    eps, pause = g("eps"), g("pause")
    (wq_hi, wq_lo, wp_hi, wp_lo, k_hi, k_lo, v_parts, fill_col, minus_row, ones16, bp_rows, max_row, ident, expo,
     gx_c, bx_c, x_chunks, x_tiles, x1_tiles) = (g(n) for n in (
         "wq_hi", "wq_lo", "wp_hi", "wp_lo", "k_hi", "k_lo", "v_parts", "fill_col", "minus_row", "ones16", "bp_rows",
         "max_row", "ident", "expo", "gx_c", "bx_c", "x_chunks", "x_tiles", "x1_tiles"))
    B, D, KB, TT, KEYS, NCHUNK, SCALE = (g(n) for n in ("B", "D", "KB", "TT", "KEYS", "NCHUNK", "SCALE"))
    UNITS = NCHUNK * KB
    PER = 2 * KB
    LOOPS = UNITS // PER
    AHEAD = KB + 2
    FIRST, LAST = -2 * KB, UNITS + 5

    with ExitStack() as scope:
        def sb(name, shape, dt):
            return scope.enter_context(nc.sbuf_tensor(name, shape, dt))

        def sem(name):
            return scope.enter_context(nc.semaphore(name))

        x_in = sb("x_in", [P, TT, D], F32)
        x_norm = sb("x_norm", [P, TT, D], F32)
        xt_f = [sb(f"xt_f{n}", [P, CHUNK], F32) for n in range(2)]
        xt_hi = [sb(f"xt_hi{n}", [P, KB, CHUNK], F32R) for n in range(2)]
        xt_lo = [sb(f"xt_lo{n}", [P, KB, CHUNK], F32R) for n in range(2)]
        q_f = [sb(f"q_f{n}", [P, CHUNK], F32) for n in range(2)]
        q_hi = [sb(f"q_hi{n}", [P, CHUNK], F32R) for n in range(4)]
        q_lo = [sb(f"q_lo{n}", [P, CHUNK], F32R) for n in range(4)]
        maxima = [sb(f"maxima{n}", [P, TT, HG], F32) for n in range(2)]
        p_f = [sb(f"p_f{n}", [P, CHUNK], F32) for n in range(HG)]
        p_hi = [sb(f"p_hi{n}", [P, CHUNK], F16) for n in range(HG)]
        p_lo = [sb(f"p_lo{n}", [P, CHUNK], F16) for n in range(HG)]
        inv_den = sb("inv_den", [P, CHUNK], F32)
        o_f = [sb(f"o_f{n}", [P, CHUNK], F32) for n in range(2)]
        o_hi = [sb(f"o_hi{n}", [P, KB, CHUNK], F32R) for n in range(2)]
        o_lo = [sb(f"o_lo{n}", [P, KB, CHUNK], F32R) for n in range(2)]
        x_res = [sb(f"x_res{n}", [P, D], F32) for n in range(2)]
        x1_out = [sb(f"x1_out{n}", [P, D], F32) for n in range(2)]
        stats = sb("x_stats", [P, TT, 6], F32)
        mean_var = sb("x_mean_var", [P, TT, 2], F32)
        ln_a, ln_r1, ln_b, ln_c, ln_r2, ln_r = (sb(n, [P, TT], F32) for n in
                                                ("ln_a", "ln_r1", "ln_b", "ln_c", "ln_r2", "ln_r"))

        def psum(name):
            return scope.enter_context(nc.psum_tensor(name, [P, 512], F32))

        ps_max = [psum("ps_max0"), psum("ps_max1")]
        ps_s = [psum("ps_s0"), psum("ps_s1")]
        ps_o, ps_den = psum("ps_o"), psum("ps_den")
        ps_qm = psum("ps_qm")
        ps_xp = psum("ps_xp")

        x_loaded = sem("x_loaded")
        res_loaded = [sem("res_loaded0"), sem("res_loaded1")]
        x1_stored = [sem("x1_stored0"), sem("x1_stored1")]
        (stats_some, stats_ready, ln_step, rstd_ready, norm_ready, xt_turned, xt_f_ready, xt_hi_ready, xt_lo_ready,
         q_done, q_f_ready, q_hi_ready, q_lo_ready, max_done, max_taken, max_turned, max_row_ready, s_done,
         p_f_ready, p_hi_ready, p_lo_dve, p_lo_pool, pv_done, den_inv, o_f_ready, o_hi_ready, o_lo_ready,
         proj_done, x1_ready, res_biased) = (sem(n) for n in (
             "stats_some", "stats_ready", "ln_step", "rstd_ready", "norm_ready", "xt_turned", "xt_f_ready",
             "xt_hi_ready", "xt_lo_ready", "q_done", "q_f_ready", "q_hi_ready", "q_lo_ready", "max_done",
             "max_taken", "max_turned", "max_row_ready", "s_done", "p_f_ready", "p_hi_ready", "p_lo_dve",
             "p_lo_pool", "pv_done", "den_inv", "o_f_ready", "o_hi_ready", "o_lo_ready", "proj_done", "x1_ready",
             "res_biased"))

        def real(i, k, n):
            return not isinstance(i, int) or 0 <= PER * i + k < n

        def every_step(eng, step):
            for k in range(FIRST, PER):
                step(0, k)
            with eng.Fori(1, LOOPS - 1) as i:
                for k in range(PER):
                    step(i, k)
            for k in range(LAST - PER * (LOOPS - 1)):
                step(LOOPS - 1, k)


        block = scope.enter_context(nc.Block())

        @block.sync
        def _(sp):
            def load_x(i, c):
                if real(i, KB * c, UNITS):
                    n = 2 * i + c
                    source = x_chunks[c % 2, i + c // 2, :, :, :]
                    sp.lower_val(source.offset * 4)
                    after(sp, norm_ready, TT * n)
                    sp.dma_start(x_in[:, :, :], source).then_inc(x_loaded, 16)

            def step(i, k):
                if k % KB == 0:
                    load_x(i, k // KB + 2)
                tile = k - 4
                if real(i, tile, UNITS):
                    c, t = tile // KB, tile % KB
                    source = x_tiles[c % 2, i + c // 2, t, :, :]
                    sp.lower_val(source.offset * 4)
                    after(sp, x1_ready, PER * i + tile - 1)
                    sp.dma_start(x_res[t % 2][:, :], source).then_inc(res_loaded[t % 2], 16)
                tile = k - 5
                if real(i, tile, UNITS):
                    c, t = tile // KB, tile % KB
                    target = x1_tiles[c % 2, i + c // 2, t, :, :]
                    sp.lower_val(target.offset * 4)
                    after(sp, x1_ready, PER * i + tile + 1)
                    sp.dma_start(target, x1_out[t % 2][:, :]).then_inc(x1_stored[t % 2], 16)

            every_step(sp, step)
            for s in x1_stored:
                sp.wait_ge(s, 16 * UNITS // 2)

        @block.tensor
        def _(pe):
            def queries(i, k, blocks):
                v, c, m = PER * i + k, (k // KB) % 2, k % KB
                if 0 in blocks:
                    after(pe, xt_hi_ready, KB * (2 * i + k // KB + 1))
                    after(pe, xt_lo_ready, KB * (2 * i + k // KB + 1))
                    after(pe, q_f_ready, v)
                    after(pe, max_row_ready, v - 1)
                block = slice(m * P, (m + 1) * P)
                last = split_product(nc, ps_qm[:, :], [(wq_hi[:, n, block], wq_lo[:, n, block]) for n in range(KB)],
                                     [(xt_hi[c][:, n, :], xt_lo[c][:, n, :]) for n in range(KB)], blocks)
                if KB - 1 in blocks:
                    last.then_inc(q_done, 1)

            def scores_for_max(i, k, tiles):
                v, b, m = PER * i + k, (k // KB) % 2, k % KB
                after(pe, q_hi_ready, v + 1)
                for t in tiles:
                    after(pe, max_taken, TT * v + t - 1)
                    nc.tensor.matmul(ps_max[t % 2][:, :], q_hi[k % 4][:, t * P:(t + 1) * P],
                                     k_hi[:, b, m, :, :].rearrange("p j n -> p (j n)"),
                                     start=True, stop=True).then_inc(max_done, 1)

            def turn_maxima(i, k):
                v = PER * i + k
                after(pe, max_taken, TT * (v + 1))
                after(pe, q_f_ready, v + 2 if real(i, k + 1, UNITS) else v + 1)
                after(pe, max_row_ready, v)
                for t in range(TT):
                    last = nc.tensor.transpose(ps_qm[0:HG, t * P:(t + 1) * P], maxima[k % 2][:, t, :], ident[:, :])
                last.then_inc(max_turned, 1)

            def scores(i, k, j):
                v, b, m = PER * i + k, (k // KB) % 2, k % KB
                if j == 0:
                    after(pe, q_lo_ready, v + 1)
                    after(pe, max_row_ready, v + 1)
                after(pe, p_hi_ready, HG * v + j - 1)
                to = ps_s[j % 2][:, :]
                nc.tensor.matmul(to, k_hi[:, b, m, j, :], q_hi[k % 4][:, :], start=True, stop=False)
                nc.tensor.matmul(to, k_hi[:, b, m, j, :], q_lo[k % 4][:, :], start=False, stop=False)
                nc.tensor.matmul(to, k_lo[:, b, m, j, :], q_hi[k % 4][:, :], start=False, stop=False)
                nc.tensor.matmul(to, minus_row[:, j, :], max_row[k % 2][:, :], start=False, stop=True).then_inc(s_done, 1)

            def weighted_values(i, k):
                v, b, m = PER * i + k, (k // KB) % 2, k % KB
                after(pe, p_hi_ready, HG * (v + 1))
                after(pe, p_lo_dve, (HG - 1) * (v + 1))
                after(pe, p_lo_pool, v + 1)
                after(pe, o_f_ready, v)
                terms = [(v_parts[0], p_hi), (v_parts[1], p_hi), (v_parts[2], p_hi), (v_parts[0], p_lo), (v_parts[1], p_lo)]
                for n, (part, probs) in enumerate(terms):
                    for j in range(HG):
                        h = HG * m + j
                        nc.tensor.matmul(ps_o[HEAD * j:HEAD * (j + 1), :], part[:, b, h * HEAD:(h + 1) * HEAD], probs[j][:, :],
                                         start=(n == 0), stop=(n == len(terms) - 1))
                for n, probs in enumerate((p_hi, p_lo)):
                    for j in range(HG):
                        last = nc.tensor.matmul(ps_den[HEAD * j:HEAD * (j + 1), :], ones16[:, :], probs[j][:, :],
                                                start=(n == 0), stop=(n == 1))
                last.then_inc(pv_done, 1)

            def turn_x(i, k):
                job, n = PER * i + k, k % KB
                after(pe, norm_ready, TT * (2 * i + k // KB + 1))
                after(pe, xt_f_ready, job)
                after(pe, x1_ready, job - AHEAD - 5)
                for t in range(TT):
                    last = nc.tensor.transpose(ps_xp[:, t * P:(t + 1) * P], x_norm[:, t, n * P:(n + 1) * P], ident[:, :])
                last.then_inc(xt_turned, 1)

            def project(i, k, blocks):
                tile, c, t = PER * i + k, (k // KB) % 2, k % KB
                chunk = 2 * i + k // KB
                if 0 in blocks:
                    after(pe, o_hi_ready, KB * (chunk + 1))
                    after(pe, o_lo_ready, KB * (chunk + 1))
                    after(pe, x1_ready, tile)
                    turned = tile + 5 + AHEAD + 1
                    after(pe, xt_f_ready, min(turned, UNITS) if isinstance(i, int) else turned)
                tokens = slice(t * P, (t + 1) * P)
                last = split_product(nc, ps_xp[:, :], [(o_hi[c][:, n, tokens], o_lo[c][:, n, tokens]) for n in range(KB)],
                                     [(wp_hi[:, n, :], wp_lo[:, n, :]) for n in range(KB)], blocks)
                if KB - 1 in blocks:
                    last.then_inc(proj_done, 1)

            def step(i, k):
                first, second = range(KB // 2), range(KB // 2, KB)
                if real(i, k + 1, UNITS):
                    scores_for_max(i, k + 1, (0, 1))
                if real(i, k + 2, UNITS):
                    queries(i, k + 2, first)
                if real(i, k + 1, UNITS):
                    scores_for_max(i, k + 1, (2, 3))
                if real(i, k + 2, UNITS):
                    queries(i, k + 2, second)
                if real(i, k + AHEAD, UNITS):
                    turn_x(i, k + AHEAD)
                if real(i, k - 1, UNITS):
                    weighted_values(i, k - 1)
                if real(i, k + 1, UNITS):
                    turn_maxima(i, k + 1)
                if real(i, k, UNITS):
                    scores(i, k, 0)
                    scores(i, k, 1)
                if real(i, k - 5, UNITS):
                    project(i, k - 5, first)
                if real(i, k, UNITS):
                    scores(i, k, 2)
                    scores(i, k, 3)
                if real(i, k - 5, UNITS):
                    project(i, k - 5, second)

            every_step(pe, step)

        @block.scalar
        def _(act):
            def take_queries(i, k):
                v = PER * i + k
                after(act, q_done, v + 1)
                after(act, q_hi_ready, v - 1)
                after(act, q_lo_ready, v - 1)
                nc.scalar.activation(q_f[k % 2][:, :], ps_qm[:, :], ACT.Identity, scale=SCALE).then_inc(q_f_ready, 1)

            def probabilities(i, k, j):
                v, b = PER * i + k, (k // KB) % 2
                after(act, s_done, HG * v + j + 1)
                if j == HG - 1:
                    after(act, p_lo_pool, v)
                else:
                    after(act, p_lo_dve, (HG - 1) * (v - 1) + j + 1)
                nc.scalar.activation(p_f[j][:, :], ps_s[j % 2][:, :], ACT.Exp, bias=fill_col[:, b:b + 1]).then_inc(p_f_ready, 1)
                after(act, pv_done, v)
                nc.scalar.activation(p_hi[j][:, :], ps_s[j % 2][:, :], ACT.Exp, bias=fill_col[:, b:b + 1]).then_inc(p_hi_ready, 1)

            def take_x(i, k):
                job, n = PER * i + k, k % KB
                after(act, xt_turned, job + 1)
                after(act, xt_hi_ready, job - 1)
                after(act, xt_lo_ready, job - 1)
                nc.scalar.activation(xt_f[n % 2][:, :], ps_xp[:, :], ACT.Identity, bias=bx_c[:, n:n + 1],
                                     scale=gx_c[:, n:n + 1]).then_inc(xt_f_ready, 1)

            def take_maxima(i, k):
                v = PER * i + k
                after(act, max_turned, v + 1)
                after(act, s_done, HG * (v - 1))
                nc.scalar.copy(max_row[k % 2][0:HG, :], ps_qm[0:HG, :]).then_inc(max_row_ready, 1)

            def outputs_hi(i, k):
                v, c, m = PER * i + k, (k // KB) % 2, k % KB
                after(act, o_f_ready, v + 1)
                after(act, proj_done, KB * (2 * i + k // KB - 1))
                nc.scalar.copy(o_hi[c][:, m, :], o_f[k % 2][:, :]).then_inc(o_hi_ready, 1)

            def step(i, k):
                if real(i, k + 2, UNITS):
                    take_queries(i, k + 2)
                if real(i, k + AHEAD, UNITS):
                    take_x(i, k + AHEAD)
                if real(i, k + 1, UNITS):
                    take_maxima(i, k + 1)
                if real(i, k, UNITS):
                    for j in range(HG):
                        probabilities(i, k, j)
                if real(i, k - 1, UNITS):
                    outputs_hi(i, k - 1)

            every_step(act, step)

        @block.vector
        def _(dve):
            def queries_hi(i, k):
                v = PER * i + k
                after(dve, q_f_ready, v + 1)
                after(dve, s_done, HG * (v - 3))
                nc.vector.tensor_copy(q_hi[k % 4][:, :], q_f[k % 2][:, :]).then_inc(q_hi_ready, 1)

            def take_max(i, k):
                v = PER * i + k
                after(dve, max_turned, v - 1)
                for t in range(TT):
                    after(dve, max_done, TT * v + t + 1)
                    nc.vector.reduce_max(maxima[k % 2][:, t, :], ps_max[t % 2][:, :].rearrange("p (j n) -> p j n", j=HG),
                                         AX.X).then_inc(max_taken, 1)

            def invert_sums(i, k):
                v = PER * i + k
                after(dve, pv_done, v + 1)
                after(dve, o_f_ready, v)
                nc.vector.reciprocal(inv_den[:, :], ps_den[:, :]).then_inc(den_inv, 1)

            def normalise(i, k):
                v = PER * i + k
                after(dve, o_hi_ready, v - 1)
                after(dve, o_lo_ready, v - 1)
                after(dve, den_inv, v + 1)
                nc.vector.tensor_tensor(o_f[k % 2][:, :], ps_o[:, :], inv_den[:, :], ALU.mult).then_inc(o_f_ready, 1)

            def probabilities_lo(i, k, j):
                v = PER * i + k
                after(dve, p_f_ready, HG * v + j + 1)
                after(dve, p_hi_ready, HG * v + j + 1)
                nc.vector.tensor_tensor(p_lo[j][:, :], p_f[j][:, :], p_hi[j][:, :], ALU.subtract).then_inc(p_lo_dve, 1)

            def x_hi(i, k):
                c, n, chunk = k // KB, k % KB, 2 * i + k // KB
                after(dve, xt_f_ready, PER * i + k + 1)
                after(dve, q_done, KB * (chunk - 1))
                nc.vector.tensor_copy(xt_hi[c % 2][:, n, :], xt_f[n % 2][:, :]).then_inc(xt_hi_ready, 1)

            def add_residual(i, k):
                tile = PER * i + k
                after(dve, proj_done, tile + 1)
                after(dve, res_biased, tile + 1)
                if real(i, k - 2, UNITS):
                    after(dve, x1_stored[k % 2], 8 * (tile - k % 2))
                nc.vector.tensor_tensor(x1_out[k % 2][:, :], ps_xp[:, :], x_res[k % 2][:, :], ALU.add).then_inc(x1_ready, 1)

            def row_stats(i, c):
                if not real(i, KB * c, UNITS):
                    return
                chunk = 2 * i + c
                after(dve, x_loaded, 16 * (chunk + 1))
                for t in range(TT):
                    nc.vector.bn_stats(stats[:, t, :], x_in[:, t, :]).then_inc(stats_some, 1)
                after(dve, rstd_ready, chunk)
                after(dve, stats_some, TT * (chunk + 1))
                nc.vector.memset(pause[:, :], 0.0)
                for t in range(TT):
                    last = nc.vector.bn_aggr(mean_var[:, t, :], stats[:, t, :])
                last.then_inc(stats_ready, 1)

            def normalise_rows(i, c):
                if not real(i, KB * c, UNITS):
                    return
                chunk = 2 * i + c
                after(dve, rstd_ready, chunk + 1)
                after(dve, stats_ready, chunk + 1)
                after(dve, xt_turned, KB * chunk)
                for t in range(TT):
                    nc.vector.tensor_scalar(x_norm[:, t, :], x_in[:, t, :], mean_var[:, t, 0:1], ln_r[:, t:t + 1],
                                            ALU.subtract, ALU.mult).then_inc(norm_ready, 1)

            def step(i, k):
                if real(i, k + 1, UNITS):
                    take_max(i, k + 1)
                if real(i, k + 2, UNITS):
                    queries_hi(i, k + 2)
                if real(i, k + AHEAD, UNITS):
                    x_hi(i, k + AHEAD)
                if k % KB == 0:
                    row_stats(i, k // KB + 2)
                if k % KB == 1:
                    normalise_rows(i, k // KB + 2)
                if real(i, k - 1, UNITS):
                    invert_sums(i, k - 1)
                if real(i, k, UNITS):
                    probabilities_lo(i, k, 0)
                    probabilities_lo(i, k, 1)
                if real(i, k - 1, UNITS):
                    normalise(i, k - 1)
                if real(i, k, UNITS):
                    probabilities_lo(i, k, 2)
                if real(i, k - 5, UNITS):
                    add_residual(i, k - 5)

            every_step(dve, step)

        @block.gpsimd
        def _(pool):
            def queries_lo(i, k):
                v = PER * i + k
                after(pool, q_hi_ready, v + 1)
                after(pool, s_done, HG * (v - 3))
                nc.gpsimd.tensor_tensor(q_lo[k % 4][:, :], q_f[k % 2][:, :], q_hi[k % 4][:, :].bitcast(F32),
                                        ALU.subtract).then_inc(q_lo_ready, 1)

            def bias_residual(i, k):
                tile = PER * i + k
                after(pool, res_loaded[k % 2], 8 * (tile - k % 2) + 16)
                nc.gpsimd.tensor_tensor(x_res[k % 2][:, :], x_res[k % 2][:, :], bp_rows[:, :], ALU.add).then_inc(res_biased, 1)

            def outputs_lo(i, k):
                v, c, m = PER * i + k, (k // KB) % 2, k % KB
                after(pool, o_hi_ready, v + 1)
                after(pool, proj_done, KB * (2 * i + k // KB - 1))
                nc.gpsimd.tensor_tensor(o_lo[c][:, m, :], o_f[k % 2][:, :], o_hi[c][:, m, :].bitcast(F32),
                                        ALU.subtract).then_inc(o_lo_ready, 1)

            def x_lo(i, k):
                c, n, chunk = k // KB, k % KB, 2 * i + k // KB
                after(pool, xt_hi_ready, PER * i + k + 1)
                after(pool, q_done, KB * (chunk - 1))
                nc.gpsimd.tensor_tensor(xt_lo[c % 2][:, n, :], xt_f[n % 2][:, :], xt_hi[c % 2][:, n, :].bitcast(F32),
                                        ALU.subtract).then_inc(xt_lo_ready, 1)

            def probabilities_lo(i, k, j):
                v = PER * i + k
                after(pool, p_f_ready, HG * v + j + 1)
                after(pool, p_hi_ready, HG * v + j + 1)
                nc.gpsimd.tensor_tensor(p_lo[j][:, :], p_f[j][:, :], p_hi[j][:, :], ALU.subtract).then_inc(p_lo_pool, 1)

            def row_scales(i, c):
                if not real(i, KB * c, UNITS):
                    return
                chunk = 2 * i + c
                after(pool, stats_ready, chunk + 1)
                after(pool, norm_ready, TT * chunk)
                var = mean_var[:, :, 1]
                nc.gpsimd.tensor_tensor(ln_a[:, :], var, eps[:, :], ALU.add).then_inc(ln_step, 1)
                after(pool, ln_step, 6 * chunk + 1)
                nc.gpsimd.tensor_tensor(ln_r1[:, :], ln_a[:, :], expo[:, 0, :], ALU.pow).then_inc(ln_step, 1)
                after(pool, ln_step, 6 * chunk + 2)
                nc.gpsimd.tensor_tensor(ln_b[:, :], var, ln_r1[:, :], ALU.mult).then_inc(ln_step, 1)
                after(pool, ln_step, 6 * chunk + 3)
                nc.gpsimd.tensor_tensor(ln_c[:, :], ln_b[:, :], ln_r1[:, :], ALU.mult).then_inc(ln_step, 1)
                after(pool, ln_step, 6 * chunk + 4)
                nc.gpsimd.tensor_tensor(ln_a[:, :], ln_c[:, :], eps[:, :], ALU.add).then_inc(ln_step, 1)
                after(pool, ln_step, 6 * chunk + 5)
                nc.gpsimd.tensor_tensor(ln_r2[:, :], ln_a[:, :], expo[:, 0, :], ALU.pow).then_inc(ln_step, 1)
                after(pool, ln_step, 6 * chunk + 6)
                nc.gpsimd.tensor_tensor(ln_r[:, :], ln_r1[:, :], ln_r2[:, :], ALU.mult).then_inc(rstd_ready, 1)

            def step(i, k):
                if real(i, k + 2, UNITS):
                    queries_lo(i, k + 2)
                if real(i, k + AHEAD, UNITS):
                    x_lo(i, k + AHEAD)
                if real(i, k - 5, UNITS):
                    bias_residual(i, k - 5)
                if k % KB == 0:
                    row_scales(i, k // KB + 2)
                if real(i, k, UNITS):
                    probabilities_lo(i, k, HG - 1)
                if real(i, k - 1, UNITS):
                    outputs_lo(i, k - 1)

            every_step(pool, step)


def feed_forward(nc, env):
    g = env.get
    eps, pause = g("eps"), g("pause")
    (gates, half_gate, expo, b2_rows, ident, lng_c, lnb_c, b1_c, x1_chunks, out_chunks, fc1_q, fc1_scales, fc2_q,
     fc2_scales) = (g(n) for n in (
         "gates", "half_gate", "expo", "b2_rows", "ident", "lng_c", "lnb_c", "b1_c", "x1_chunks", "out_chunks",
         "fc1_q", "fc1_scales", "fc2_q", "fc2_scales"))
    B, D, F, KB, FB, TT, NCHUNK = (g(n) for n in ("B", "D", "F", "KB", "FB", "TT", "NCHUNK"))
    LAG = 2
    PER = 2 * FB
    STEPS = NCHUNK * FB
    LOOPS = STEPS // PER

    with ExitStack() as scope:
        def sb(name, shape, dt):
            return scope.enter_context(nc.sbuf_tensor(name, shape, dt))

        def sem(name):
            return scope.enter_context(nc.semaphore(name))

        with ExitStack() as raw:
            s1_raw, q1_raw, s2_raw, q2_raw = (
                raw.enter_context(nc.sbuf_tensor(name, shape, dt)) for name, shape, dt in (
                    ("s1_raw", [P, KB, F], F32), ("q1_raw", [P, KB, F], I32),
                    ("s2_raw", [P, FB, D], F32), ("q2_raw", [P, FB, D], I32)))
        w1_hi, w1_lo = sb("w1_hi", [P, KB, F], F32R), sb("w1_lo", [P, KB, F], F32R)
        w2_hi, w2_lo = sb("w2_hi", [P, FB, D], F32R), sb("w2_lo", [P, FB, D], F32R)

        x1 = [sb(f"x1_{n}", [P, TT, D], F32) for n in range(2)]
        x1_norm = sb("x1_norm", [P, TT, D], F32)
        ht_f = [sb(f"ht_f{n}", [P, CHUNK], F32) for n in range(2)]
        ht_hi = [sb(f"ht_hi{n}", [P, KB, CHUNK], F32R) for n in range(2)]
        ht_lo = [sb(f"ht_lo{n}", [P, KB, CHUNK], F32R) for n in range(2)]
        y_f = [sb(f"y_f{n}", [P, CHUNK], F32) for n in range(2)]
        y_hi = [sb(f"y_hi{n}", [P, CHUNK], F32R) for n in range(4)]
        y_lo = [sb(f"y_lo{n}", [P, CHUNK], F32R) for n in range(4)]
        w_f = [sb(f"w_f{n}", [P, 2, D], F32) for n in range(2)]
        stats = sb("y_stats", [P, TT, 6], F32)
        mean_var = sb("y_mean_var", [P, TT, 2], F32)
        ln_a, ln_r1, ln_b, ln_c, ln_r2, ln_s2, ln_r, u_scale = (
            sb(n, [P, TT], F32) for n in ("fa", "fr1", "fb", "fc", "fr2", "fs2", "fr", "u_scale"))

        def psum(name):
            return scope.enter_context(nc.psum_tensor(name, [P, 512], F32))

        ps_y = [psum("ps_y0"), psum("ps_y1")]
        ps_h = [psum("ps_h0"), psum("ps_h1")]
        ps_z = [psum(f"ps_z{t}") for t in range(TT)]

        w_loaded = [[sem(f"w{w}_loaded{n}") for n in range(FB // 4)] for w in (1, 2)]
        x1_loaded = [sem("x1_loaded0"), sem("x1_loaded1")]
        out_stored = [sem("out_stored0"), sem("out_stored1")]
        (stats_some, stats_ready, ln_step, scales_ready, norm_ready, sum_ready, base_ready, h_turned, h_f_ready,
         h_hi_ready, h_lo_ready, y_done, y_f_ready, y_hi_ready, y_lo_ready, z_used, out_ready, w_ready, w_hi_ready,
         w1_ready, w2_ready) = (
            sem(n) for n in ("f_stats_some", "f_stats_ready", "f_ln_step", "f_scales_ready", "f_norm_ready",
                             "sum_ready", "base_ready", "h_turned", "h_f_ready", "h_hi_ready", "h_lo_ready", "y_done",
                             "y_f_ready", "y_hi_ready", "y_lo_ready", "z_used", "out_ready", "w_ready",
                             "w_hi_ready", "w1_ready", "w2_ready"))

        def every_step(eng, step):
            for k in range(-FB, PER):
                step(0, k)
            with eng.Fori(1, LOOPS - 1) as i:
                for k in range(PER):
                    step(i, k)
            for k in range(PER + LAG + 1):
                step(LOOPS - 1, k)

        def real(i, k):
            return not isinstance(i, int) or 0 <= PER * i + k < STEPS

        LOAD, STATS, SCALES, NORM, TURN, BASE = 3, 6, 7, 8, 10, 14
        EVACUATE = LAG

        PIECES = FB // 2
        w_steps = {}
        for n in range(PIECES):
            w_steps[2 * n - 3 if n else SCALES - FB] = (0, n)
            w_steps[2 * n] = (1, n)
        w_order = [w_steps[k] for k in sorted(w_steps)]

        def w_parts(w, n):
            cols = slice(2 * n * P, 2 * (n + 1) * P)
            blocks = slice(2 * n, 2 * (n + 1))
            if w == 0:
                parts = [a[:, :, cols] for a in (w1_hi, w1_lo, s1_raw, q1_raw)]
            else:
                parts = [a[:, blocks, :] for a in (w2_hi, w2_lo, s2_raw, q2_raw)]
            return (*parts, w_order.index((w, n)))

        def w_staged(w, at):
            if w == 0:
                return w_f[at % 2][:, :, :].rearrange("p a (b c) -> p (a b) c", c=2 * P)
            return w_f[at % 2][:, :, :]

        block = scope.enter_context(nc.Block())

        @block.sync
        def _(sp):
            def load_weights(n):
                cols, blocks, loaded = slice(4 * n * P, 4 * (n + 1) * P), slice(4 * n, 4 * (n + 1)), [w[n] for w in w_loaded]
                sp.dma_start(q1_raw[:, :, cols], fc1_q.rearrange("(g p) f -> p g f", p=P)[:, :, cols])\
                    .then_inc(loaded[0], 16)
                sp.dma_start(s1_raw[:, :, cols], fc1_scales[:, cols].partition_broadcast(P)).then_inc(loaded[0], 16)
                sp.dma_start(q2_raw[:, blocks, :], fc2_q.rearrange("(g p) d -> p g d", p=P)[:, blocks, :])\
                    .then_inc(loaded[1], 16)
                sp.dma_start(s2_raw[:, blocks, :], fc2_scales[blocks, :].partition_broadcast(P)).then_inc(loaded[1], 16)

            def step(i, k):
                c, f = k // FB, k % FB
                if isinstance(i, int) and i == 0 and k == LOAD + 1 - FB:
                    for n in range(FB // 4):
                        load_weights(n)
                if f == LOAD and real(i, FB * (c + 1)):
                    chunk = 2 * i + c + 1
                    source = x1_chunks[(c + 1) % 2, i + (c + 1) // 2, :, :, :]
                    sp.lower_val(source.offset * 4)
                    after(sp, out_stored[(c + 1) % 2], 16 * (i + (c + 1) // 2))
                    sp.dma_start(x1[(c + 1) % 2][:, :, :], source)\
                        .then_inc(x1_loaded[(c + 1) % 2], 16)
                if f == EVACUATE and real(i, FB * (c - 1)):
                    chunk = 2 * i + c - 1
                    target = out_chunks[(c - 1) % 2, i + (c - 1) // 2, :, :, :]
                    sp.lower_val(target.offset * 4)
                    after(sp, out_ready, TT * (chunk + 1))
                    sp.dma_start(target, x1[(c - 1) % 2][:, :, :]).then_inc(out_stored[(c - 1) % 2], 16)

            every_step(sp, step)
            for s in out_stored:
                sp.wait_ge(s, 16 * (NCHUNK // 2))

        @block.tensor
        def _(pe):
            def hidden(i, k):
                s, c, f = PER * i + k, (k // FB) % 2, k % FB
                if isinstance(i, int) and i == 0 and k < FB:
                    after(pe, w1_ready, k // 2 + 1)
                if f == 0:
                    after(pe, h_hi_ready, KB * (2 * i + k // FB + 1))
                    after(pe, h_lo_ready, KB * (2 * i + k // FB + 1))
                after(pe, y_f_ready, s - 1)
                block = slice(f * P, (f + 1) * P)
                split_product(nc, ps_y[f % 2][:, :], [(w1_hi[:, n, block], w1_lo[:, n, block]) for n in range(KB)],
                              [(ht_hi[c][:, n, :], ht_lo[c][:, n, :]) for n in range(KB)]).then_inc(y_done, 1)

            def sums(i, k):
                s, f = PER * i + k, k % FB
                if isinstance(i, int) and i == 0 and k < FB:
                    after(pe, w2_ready, k // 2 + 1)
                after(pe, y_hi_ready, s + 1)
                after(pe, y_lo_ready, s + 1)
                for t in range(TT):
                    if f == 0:
                        after(pe, out_ready, TT * (2 * i + k // FB - 1) + t + 1)
                    tokens = slice(t * P, (t + 1) * P)
                    hi, lo = y_hi[f % 4][:, tokens], y_lo[f % 4][:, tokens]
                    nc.tensor.matmul(ps_z[t][:, :], hi, w2_hi[:, f, :], start=(f == 0), stop=False)
                    nc.tensor.matmul(ps_z[t][:, :], hi, w2_lo[:, f, :], start=False, stop=False)
                    last = nc.tensor.matmul(ps_z[t][:, :], lo, w2_hi[:, f, :], start=False, stop=(f == FB - 1))
                last.then_inc(z_used, 1)

            def turn_h(i, c, n):
                if not real(i, FB * c):
                    return
                chunk = 2 * i + c
                after(pe, norm_ready, TT * (chunk + 1))
                after(pe, h_f_ready, KB * chunk + n - 1)
                for t in range(TT):
                    last = nc.tensor.transpose(ps_h[n % 2][:, t * P:(t + 1) * P], x1_norm[:, t, n * P:(n + 1) * P], ident[:, :])
                last.then_inc(h_turned, 1)

            def step(i, k):
                if real(i, k):
                    hidden(i, k)
                if TURN <= k % FB < TURN + KB:
                    turn_h(i, k // FB + 1, k % FB - TURN)
                if real(i, k - LAG):
                    sums(i, k - LAG)

            every_step(pe, step)

        @block.scalar
        def _(act):
            def weights_hi(w, n):
                hi, lo, scales, integers, at = w_parts(w, n)
                after(act, w_ready, at + 1)
                if w == 0:
                    nc.scalar.copy(hi, w_staged(w, at)).then_inc(w_hi_ready, 1)
                else:
                    nc.scalar.activation(hi, w_staged(w, at), ACT.Identity, scale=half_gate[:, :]).then_inc(w_hi_ready, 1)

            def step(i, k):
                if isinstance(i, int) and i == 0 and k in w_steps:
                    weights_hi(*w_steps[k])
                if real(i, k):
                    s, f = PER * i + k, k % FB
                    after(act, y_done, s + 1)
                    after(act, y_hi_ready, s - 1)
                    after(act, y_lo_ready, s - 1)
                    nc.scalar.activation(y_f[f % 2][:, :], ps_y[f % 2][:, :], ACT.Silu, bias=b1_c[:, f:f + 1]).then_inc(y_f_ready, 1)
                if TURN <= k % FB < TURN + KB and real(i, FB * (k // FB + 1)):
                    n = k % FB - TURN
                    job = KB * (2 * i + k // FB + 1) + n
                    after(act, h_turned, job + 1)
                    after(act, h_hi_ready, job - 1)
                    after(act, h_lo_ready, job - 1)
                    nc.scalar.activation(ht_f[n % 2][:, :], ps_h[n % 2][:, :], ACT.Identity, bias=lnb_c[:, n:n + 1],
                                         scale=lng_c[:, n:n + 1]).then_inc(h_f_ready, 1)

            every_step(act, step)

        @block.vector
        def _(dve):
            def split_hidden(i, k):
                s, f = PER * i + k, k % FB
                after(dve, y_f_ready, s + 1)
                after(dve, z_used, s - 3)
                nc.vector.tensor_copy(y_hi[f % 4][:, :], y_f[f % 2][:, :]).then_inc(y_hi_ready, 1)
                after(dve, y_hi_ready, s + 1)
                nc.vector.tensor_tensor(y_lo[f % 4][:, :], y_f[f % 2][:, :], y_hi[f % 4][:, :].bitcast(F32),
                                        ALU.subtract).then_inc(y_lo_ready, 1)

            def split_h(i, c, n):
                chunk = 2 * i + c
                after(dve, h_f_ready, KB * chunk + n + 1)
                after(dve, y_done, FB * (chunk - 1))
                nc.vector.tensor_copy(ht_hi[c % 2][:, n, :], ht_f[n % 2][:, :]).then_inc(h_hi_ready, 1)
                after(dve, h_hi_ready, KB * chunk + n + 1)
                nc.vector.tensor_tensor(ht_lo[c % 2][:, n, :], ht_f[n % 2][:, :], ht_hi[c % 2][:, n, :].bitcast(F32),
                                        ALU.subtract).then_inc(h_lo_ready, 1)

            def take_sums(i, c):
                chunk = 2 * i + c
                after(dve, z_used, FB * (chunk + 1))
                after(dve, base_ready, TT * (chunk + 1))
                for t in range(TT):
                    out_t = x1[c % 2][:, t, :]
                    nc.vector.tensor_tensor(out_t, ps_z[t][:, :], out_t, ALU.add).then_inc(out_ready, 1)

            def weights(w, n):
                hi, lo, scales, integers, at = w_parts(w, n)
                after(dve, w_loaded[w][n // 2], 32)
                after(dve, (w1_ready, w2_ready)[w_order[at - 2][0]], w_order[at - 2][1] + 1 if at >= 2 else 0)
                nc.vector.scalar_tensor_tensor(out=w_staged(w, at), in0=integers, scalar=-128.0, in1=scales,
                                               op0=ALU.add, op1=ALU.mult).then_inc(w_ready, 1)
                after(dve, w_hi_ready, at + 1)
                if w == 0:
                    nc.vector.tensor_tensor(lo, w_staged(w, at), hi.bitcast(F32), ALU.subtract).then_inc(w1_ready, 1)
                else:
                    nc.vector.scalar_tensor_tensor(out=lo, in0=w_staged(w, at), scalar=half_gate[:, :], in1=hi.bitcast(F32),
                                                   op0=ALU.mult, op1=ALU.subtract).then_inc(w2_ready, 1)

            def step(i, k):
                c, f = k // FB, k % FB
                if isinstance(i, int) and i == 0 and k in w_steps:
                    weights(*w_steps[k])
                if f == EVACUATE and real(i, FB * (c - 1)):
                    take_sums(i, c - 1)
                if real(i, k):
                    split_hidden(i, k)
                if not real(i, FB * (c + 1)):
                    return
                chunk, b = 2 * i + c + 1, (c + 1) % 2
                if f == STATS:
                    after(dve, x1_loaded[b], 16 * (i + (c + 1) // 2 + 1))
                    after(dve, stats_ready, chunk)
                    for t in range(TT):
                        nc.vector.bn_stats(stats[:, t, :], x1[b][:, t, :]).then_inc(stats_some, 1)
                    after(dve, scales_ready, chunk)
                    after(dve, stats_some, TT * (chunk + 1))
                    nc.vector.memset(pause[:, :], 0.0)
                    for t in range(TT):
                        last = nc.vector.bn_aggr(mean_var[:, t, :], stats[:, t, :])
                    last.then_inc(stats_ready, 1)
                if f == NORM:
                    after(dve, scales_ready, chunk + 1)
                    after(dve, h_turned, KB * chunk)
                    after(dve, sum_ready, TT * chunk)
                    for t in range(TT):
                        nc.vector.tensor_scalar(x1_norm[:, t, :], x1[b][:, t, :], mean_var[:, t, 0:1], ln_r[:, t:t + 1],
                                                ALU.subtract, ALU.mult).then_inc(norm_ready, 1)
                if TURN <= f < TURN + KB:
                    split_h(i, c + 1, f - TURN)
                if f == BASE:
                    for t in range(TT):
                        after(dve, norm_ready, TT * chunk + t + 1)
                        nc.vector.scalar_tensor_tensor(out=x1[b][:, t, :], in0=x1_norm[:, t, :], scalar=u_scale[:, t:t + 1],
                                                       in1=x1[b][:, t, :], op0=ALU.mult, op1=ALU.add).then_inc(sum_ready, 1)

            every_step(dve, step)

        @block.gpsimd
        def _(pool):
            def step(i, k):
                c, f = k // FB, k % FB
                if not real(i, FB * (c + 1)):
                    return
                chunk, b = 2 * i + c + 1, (c + 1) % 2
                if f == SCALES:
                    after(pool, stats_ready, chunk + 1)
                    after(pool, norm_ready, TT * chunk)
                    after(pool, sum_ready, TT * chunk)
                    var = mean_var[:, :, 1]
                    steps = 7 * chunk
                    nc.gpsimd.tensor_tensor(ln_a[:, :], var, eps[:, :], ALU.add).then_inc(ln_step, 1)
                    after(pool, ln_step, steps + 1)
                    nc.gpsimd.tensor_tensor(ln_r1[:, :], ln_a[:, :], expo[:, 0, :], ALU.pow).then_inc(ln_step, 1)
                    after(pool, ln_step, steps + 2)
                    nc.gpsimd.tensor_tensor(ln_b[:, :], var, ln_r1[:, :], ALU.mult).then_inc(ln_step, 1)
                    after(pool, ln_step, steps + 3)
                    nc.gpsimd.tensor_tensor(ln_c[:, :], ln_b[:, :], ln_r1[:, :], ALU.mult).then_inc(ln_step, 1)
                    after(pool, ln_step, steps + 4)
                    nc.gpsimd.tensor_tensor(ln_a[:, :], ln_c[:, :], eps[:, :], ALU.add).then_inc(ln_step, 1)
                    after(pool, ln_step, steps + 5)
                    nc.gpsimd.tensor_tensor(ln_r2[:, :], ln_a[:, :], expo[:, 0, :], ALU.pow).then_inc(ln_step, 1)
                    nc.gpsimd.tensor_tensor(ln_s2[:, :], ln_a[:, :], expo[:, 1, :], ALU.pow).then_inc(ln_step, 1)
                    after(pool, ln_step, steps + 7)
                    nc.gpsimd.tensor_tensor(u_scale[:, :], ln_s2[:, :], gates[:, 1:2].to_broadcast([P, TT]), ALU.mult)
                    nc.gpsimd.tensor_tensor(ln_r[:, :], ln_r1[:, :], ln_r2[:, :], ALU.mult).then_inc(scales_ready, 1)
                if f == BASE:
                    for t in range(TT):
                        after(pool, sum_ready, TT * chunk + t + 1)
                        nc.gpsimd.tensor_tensor(x1[b][:, t, :], x1[b][:, t, :], b2_rows[:, :], ALU.add).then_inc(base_ready, 1)

            every_step(pool, step)


_INS = ['x', 'ctx_1024', 'mask_BxS2_ik0', 'g_xattn', 'g_ffn', 'L0_xattn_w_q', 'L0_xattn_w_kv', 'L0_xattn_w_proj',
        'L0_xattn_b_proj', 'L0_xattn_g_x', 'L0_xattn_b_x', 'L0_xattn_g_kv', 'L0_xattn_b_kv', 'L0_ffn_ln_gamma',
        'L0_ffn_ln_beta', 'L0_ffn_fc1_q', 'L0_ffn_fc1_scales', 'L0_ffn_fc1_bias', 'L0_ffn_fc2_q', 'L0_ffn_fc2_scales',
        'L0_ffn_fc2_bias']


def kernel(**inputs):
    import concourse.bacc as bacc
    from concourse.bass_utils import run_bass_kernel_spmd

    nc = bacc.Bacc("TRN2", target_bir_lowering=False, num_devices=1, dynamic_dma_scratch_size=1024)
    arrays, args = {}, []
    for name in _INS:
        a = np.ascontiguousarray(inputs[name])
        arrays[f"in_{name}"] = a
        args.append(nc.dram_tensor(f"in_{name}", a.shape, mybir.dt.from_np(a.dtype), kind="ExternalInput").ap())
    out = nc.dram_tensor("out", arrays["in_x"].shape, F32, kind="ExternalOutput").ap()
    build(nc, *args, out)
    r = run_bass_kernel_spmd(nc, [arrays], core_ids=[0])
    return r.results[0]["out"]
```

```python
from contextlib import ExitStack

import numpy as np

import concourse.bass as bass
from concourse import mybir

F32 = mybir.dt.float32
F32R = mybir.dt.float32r
F16 = mybir.dt.float16
BF16 = mybir.dt.bfloat16
I32 = mybir.dt.int32
ALU = mybir.AluOpType
ACT = mybir.ActivationFunctionType
AX = mybir.AxisListType

P = 128
HEAD = 32
HG = P // HEAD
CHUNK = 512
EPS = 1e-5
FILL = -1e9


def after(eng, semaphore, count):
    if not isinstance(count, int) or count > 0:
        eng.wait_ge(semaphore, count)


def build(nc, x, ctx, mask, g_xattn, g_ffn, w_q, w_kv, w_proj, b_proj, g_x, b_x, g_kv, b_kv,
          ln_gamma, ln_beta, fc1_q, fc1_scales, fc1_bias, fc2_q, fc2_scales, fc2_bias, out):
    B, S, D = x.shape
    KEYS = ctx.shape[1]
    F = fc1_q.shape[1]
    KB = D // P
    FB = F // P
    TT = CHUNK // P
    NCHUNK = B * S // CHUNK
    SCALE = HEAD ** -0.5
    assert B == 2 and KEYS == P and KB == HG and FB % 4 == 0 and NCHUNK % 2 == 0

    rows = "b (c t p) d -> b c t p d"
    x_tiles = x.rearrange(rows, t=TT, p=P)
    out_chunks = out.rearrange("b (c t p) d -> b c p t d", t=TT, p=P)
    x1_dram = nc.dram_tensor("x1_dram", (B, S, D), F32, kind="Internal").ap()
    x1_tiles = x1_dram.rearrange(rows, t=TT, p=P)
    chunk_rows = "b (c t p) d -> b c p t d"
    x_chunks = x.rearrange(chunk_rows, t=TT, p=P)
    x1_chunks = x1_dram.rearrange(chunk_rows, t=TT, p=P)

    with ExitStack() as whole:
        def sb(name, shape, dt, scope=whole):
            return scope.enter_context(nc.sbuf_tensor(name, shape, dt))

        ident = sb("ident", [P, P], F32)
        cols = sb("cols", [P, 6 * KB + FB], F32)
        gx_c, bx_c, gkv_c, bkv_c, lng_c, lnb_c = (cols[:, KB * n:KB * n + KB] for n in range(6))
        b1_c = cols[:, 6 * KB:6 * KB + FB]
        gates = sb("gates", [P, 2], F32)
        half_gate = sb("half_gate", [P, 1], F32)
        expo = sb("expo", [P, 2, TT], F32)
        eps = sb("eps", [P, TT], F32)
        pause = sb("pause", [P, 1], F32)
        pool_pause, act_pause = sb("pool_pause", [P, 1], F32), sb("act_pause", [P, 1], F32)
        b2_rows = sb("b2_rows", [P, D], F32)

        x_in, x_norm = sb("x_in", [P, TT, D], F32), sb("x_norm", [P, TT, D], F32)
        xt_f = [sb(f"xt_f{n}", [P, CHUNK], F32) for n in range(2)]
        xt_hi = [sb(f"xt_hi{n}", [P, KB, CHUNK], F32R) for n in range(2)]
        xt_lo = [sb(f"xt_lo{n}", [P, KB, CHUNK], F32R) for n in range(2)]
        stats, mean_var = sb("x_stats", [P, TT, 6], F32), sb("x_mean_var", [P, TT, 2], F32)
        ln_a, ln_r1, ln_b, ln_c, ln_r2, ln_s2, ln_r, u_scale = (
            sb(n, [P, TT], F32) for n in ("ln_a", "ln_r1", "ln_b", "ln_c", "ln_r2", "ln_s2", "ln_r", "u_scale"))

        fill_col = sb("fill_col", [P, B], F32)
        ones16 = sb("ones16", [P, HEAD], BF16)
        maxima = [sb(f"maxima{n}", [P, TT, HG], F32) for n in range(2)]

        GROUP = 4
        w1_loaded, w2_loaded = ([whole.enter_context(nc.semaphore(f"w{w}_loaded{n}")) for n in range(FB // GROUP)]
                                for w in (1, 2))
        x1_stored = [whole.enter_context(nc.semaphore(f"x1_stored{n}")) for n in range(2)]
        with ExitStack() as raw:
            s1_raw, q1_raw, s2_raw, q2_raw = (
                raw.enter_context(nc.sbuf_tensor(name, shape, dt)) for name, shape, dt in (
                    ("s1_raw", [P, FB // GROUP, KB, GROUP * P], F32), ("q1_raw", [P, FB // GROUP, KB, GROUP * P], I32),
                    ("s2_raw", [P, FB, D], F32), ("q2_raw", [P, FB, D], I32)))

        with ExitStack() as later:
            def fb(name, shape, dt):
                return sb(name, shape, dt, later)

            w1_hi, w1_lo = (fb(n, [P, FB // GROUP, KB, GROUP * P], F32R) for n in ("w1_hi", "w1_lo"))
            w2_hi, w2_lo = fb("w2_hi", [P, FB, D], F32R), fb("w2_lo", [P, FB, D], F32R)
            x1_1 = fb("x1_1", [P, TT, D], F32)
            w_f = [fb(f"w_f{n}", [P, 2 * D], F32) for n in range(2)]
            y_f = [fb(f"y_f{n}", [P, CHUNK], F32) for n in range(2)]
            y_hi = [fb(f"y_hi{n}", [P, CHUNK], F32R) for n in range(4)]
            y_lo = [fb(f"y_lo{n}", [P, CHUNK], F32R) for n in range(4)]

        w_steps = {-2: (0, 0)}
        for n in range(FB // 2):
            w_steps[2 * n] = (1, n)
            if n > 0:
                w_steps[2 * n - 3] = (0, n)
        w_order = [w_steps[k] for k in sorted(w_steps)]
        w_ready, w_hi_ready, w1_ready, w2_ready = (
            whole.enter_context(nc.semaphore(n)) for n in ("w_ready", "w_hi_ready", "w1_ready", "w2_ready"))

        def w_parts(w, n):
            at = w_order.index((w, n))
            if w == 0:
                first = 2 * n % GROUP * P
                parts = [a[:, 2 * n // GROUP, :, first:first + 2 * P] for a in (w1_hi, w1_lo, s1_raw, q1_raw)]
                full = w_f[at % 2][:, :].rearrange("p (k c) -> p k c", k=KB)
            else:
                parts = [a[:, 2 * n:2 * (n + 1), :] for a in (w2_hi, w2_lo, s2_raw, q2_raw)]
                full = w_f[at % 2][:, :].rearrange("p (f d) -> p f d", f=2)
            return (*parts, full, at)

        def weights_hi(act, w, n):
            hi, lo, scales, integers, full, at = w_parts(w, n)
            after(act, w_ready, at + 1)
            if w == 0:
                nc.scalar.copy(hi, full).then_inc(w_hi_ready, 1)
            else:
                nc.scalar.activation(hi, full, ACT.Identity, scale=half_gate[:, :]).then_inc(w_hi_ready, 1)

        def weights(dve, w, n):
            hi, lo, scales, integers, full, at = w_parts(w, n)
            after(dve, (w1_loaded, w2_loaded)[w][2 * n // GROUP], 32)
            if at >= 2:
                before, m = w_order[at - 2]
                after(dve, (w1_ready, w2_ready)[before], m + 1)
            nc.vector.scalar_tensor_tensor(out=full, in0=integers, scalar=-128.0, in1=scales,
                                           op0=ALU.add, op1=ALU.mult).then_inc(w_ready, 1)
            after(dve, w_hi_ready, at + 1)
            if w == 0:
                nc.vector.tensor_tensor(lo, full, hi.bitcast(F32), ALU.subtract).then_inc(w1_ready, 1)
            else:
                nc.vector.scalar_tensor_tensor(out=lo, in0=full, scalar=half_gate[:, :], in1=hi.bitcast(F32),
                                               op0=ALU.mult, op1=ALU.subtract).then_inc(w2_ready, 1)

        def load_w1(eng, n):
            cols = slice(GROUP * P * n, GROUP * P * (n + 1))
            eng.dma_start(q1_raw[:, n, :, :], fc1_q.rearrange("(k p) f -> p k f", p=P)[:, :, cols]).then_inc(w1_loaded[n], 16)
            eng.dma_start(s1_raw[:, n, :, :], fc1_scales[:, cols].partition_broadcast(P)).then_inc(w1_loaded[n], 16)

        def load_w2(eng, n):
            blocks = slice(GROUP * n, GROUP * (n + 1))
            eng.dma_start(q2_raw[:, blocks, :], fc2_q.rearrange("(f p) d -> p f d", p=P)[:, blocks, :]).then_inc(w2_loaded[n], 16)
            eng.dma_start(s2_raw[:, blocks, :], fc2_scales[blocks, :].partition_broadcast(P)).then_inc(w2_loaded[n], 16)

        with ExitStack() as attn:
            def ab(name, shape, dt):
                return sb(name, shape, dt, attn)

            wq_hi = ab("wq_hi", [P, KB, D], F32R)
            wp_hi, wp_lo = ab("wp_hi", [P, KB, D], F32R), ab("wp_lo", [P, KB, D], F32R)
            v_parts = [ab(f"v{n}", [P, B, D], BF16) for n in range(3)]
            minus_row = ab("minus_row", [P, HG, KEYS], F32R)
            wq_lo = ab("wq_lo", [P, KB, D], F32R)
            k_hi, k_lo = (ab(n, [P, B, KB, HG, KEYS], F32R) for n in ("k_hi", "k_lo"))
            bp_rows = ab("bp_rows", [P, D], F32)
            max_row = [ab(f"max_row{n}", [P, CHUNK], F32R) for n in range(2)]

            attention(nc, locals())

        feed_forward(nc, locals())


def split_product(nc, out, stationary, moving, blocks=None):
    n = len(stationary)
    for k in blocks or range(n):
        (s_hi, s_lo), (m_hi, m_lo) = stationary[k], moving[k]
        nc.tensor.matmul(out, s_hi, m_hi, start=(k == 0), stop=False)
        nc.tensor.matmul(out, s_hi, m_lo, start=False, stop=False)
        last = nc.tensor.matmul(out, s_lo, m_hi, start=False, stop=(k == n - 1))
    return last


def attention(nc, env):
    g = env.get
    eps, pause, pool_pause, x1_stored = g("eps"), g("pause"), g("pool_pause"), g("x1_stored")
    (wq_hi, wq_lo, wp_hi, wp_lo, k_hi, k_lo, v_parts, fill_col, minus_row, ones16, bp_rows, max_row, ident, expo,
     gx_c, bx_c, gkv_c, bkv_c, x_chunks, x_tiles, x1_tiles, ctx, mask, cols, gates, half_gate, b2_rows) = (g(n) for n in (
         "wq_hi", "wq_lo", "wp_hi", "wp_lo", "k_hi", "k_lo", "v_parts", "fill_col", "minus_row", "ones16", "bp_rows",
         "max_row", "ident", "expo", "gx_c", "bx_c", "gkv_c", "bkv_c", "x_chunks", "x_tiles", "x1_tiles", "ctx", "mask",
         "cols", "gates", "half_gate", "b2_rows"))
    B, D, KB, FB, TT, KEYS, NCHUNK, SCALE = (g(n) for n in ("B", "D", "KB", "FB", "TT", "KEYS", "NCHUNK", "SCALE"))
    maxima = g("maxima")
    (x_in, x_norm, xt_f, xt_hi, xt_lo, stats, mean_var, ln_a, ln_r1, ln_b, ln_c, ln_r2, ln_s2, ln_r, u_scale, lng_c, lnb_c,
     x1_chunks) = (g(n) for n in ("x_in", "x_norm", "xt_f", "xt_hi", "xt_lo", "stats", "mean_var", "ln_a", "ln_r1", "ln_b",
                                  "ln_c", "ln_r2", "ln_s2", "ln_r", "u_scale", "lng_c", "lnb_c", "x1_chunks"))
    vectors = [g(n) for n in ("g_x", "b_x", "g_kv", "b_kv", "ln_gamma", "ln_beta", "fc1_bias")]
    NV = 6 * KB + FB
    UNITS = NCHUNK * KB
    PER = 2 * KB
    LOOPS = UNITS // PER
    AHEAD = KB + 2
    FIRST, LAST = -2 * KB, UNITS + 6

    with ExitStack() as scope:
        def sb(name, shape, dt):
            return scope.enter_context(nc.sbuf_tensor(name, shape, dt))

        def sem(name):
            return scope.enter_context(nc.semaphore(name))

        q_f = [sb(f"q_f{n}", [P, CHUNK], F32) for n in range(2)]
        q_hi = [sb(f"q_hi{n}", [P, CHUNK], F32R) for n in range(4)]
        q_lo = [sb(f"q_lo{n}", [P, CHUNK], F32R) for n in range(4)]

        with ExitStack() as early:
            def tmp(name, shape, dt):
                return early.enter_context(nc.sbuf_tensor(name, shape, dt))

            vec_rows = tmp("vec_rows", [NV, P], F32)
            ctx_sb = tmp("ctx_sb", [P, B, D], F32)
            ctx_t = tmp("ctx_t", [P, KB, B * KEYS], F32)
            mask_rows = tmp("mask_rows", [P, B * KEYS], I32)
            mask_col = tmp("mask_col", [P, B], I32)
            wkv = tmp("wkv", [P, KB, 2 * D], F32)
            wq_raw, wp_raw = tmp("wq_raw", [P, KB, D], F32), tmp("wp_raw", [P, KB, D], F32)
            valid, masked = tmp("valid", [P, B * KEYS], F32), tmp("masked", [P, B * KEYS], F32)
            n_valid, some_valid, divisor, inv_divisor, fill_a, var_eps, ctx_r = (
                tmp(n, [P, B], F32) for n in ("n_valid", "some_valid", "divisor", "inv_divisor", "fill_a",
                                              "c_var_eps", "c_rstd"))
            k_sum, k_mean = tmp("k_sum", [P, KB, B], F32), tmp("k_mean", [P, KB, B], F32)
            v_rest = tmp("v_rest", [P, B, D], F32)
            minus_f = tmp("minus_f", [P, HG, KEYS], F32)
            ctx_bn, ctx_mv = tmp("c_stats", [P, B, 6], F32), tmp("c_mean_var", [P, B, 2], F32)
            k_full = tmp("k_full", [P, KB, B * KEYS], F32)

        p_f = [sb(f"p_f{n}", [P, CHUNK], F32) for n in range(HG)]
        p_hi = [sb(f"p_hi{n}", [P, CHUNK], F16) for n in range(HG)]
        p_lo = [sb(f"p_lo{n}", [P, CHUNK], F16) for n in range(HG)]
        inv_den = sb("inv_den", [P, CHUNK], F32)
        o_f = [sb(f"o_f{n}", [P, CHUNK], F32) for n in range(2)]
        o_hi = [sb(f"o_hi{n}", [P, KB, CHUNK], F32R) for n in range(2)]
        o_lo = [sb(f"o_lo{n}", [P, KB, CHUNK], F32R) for n in range(2)]
        x_res = [sb(f"x_res{n}", [P, D], F32) for n in range(2)]
        x1_out = [sb(f"x1_out{n}", [P, D], F32) for n in range(2)]

        def psum(name):
            return scope.enter_context(nc.psum_tensor(name, [P, 512], F32))

        ps_max = [psum("ps_max0"), psum("ps_max1")]
        ps_s = [psum("ps_s0"), psum("ps_s1")]
        ps_o, ps_den = psum("ps_o"), psum("ps_den")
        ps_qm = psum("ps_qm")
        ps_xp = psum("ps_xp")

        ps_ctx, ps_cols = ps_max, ps_o
        ps_k, ps_v = [ps_s[0], ps_s[1], ps_den, ps_max[0]], [ps_o, ps_den]

        (vec_loaded, ctx_loaded, mask_loaded, gate_loaded, wk_loaded, wv_loaded, wq_loaded, wp_loaded, bias_loaded, ident_ready,
         pool_step, dve_step, vec_t, cols_ready, tanh_ready, ctx_stats, ctx_rstd, ctx_normed, ctx_turned, ctx_t_ready,
         k_done, k_taken, k_zeroed, v_done, wq_hi_ready, wq_lo_ready, wp_hi_ready, wp_lo_ready, bias_scaled,
         fill_ready, k_hi_ready, k_lo_ready, v_first, v_rest_ready, v_second, v_ready, wp_scaled, minus_ready, setup_over) = (sem(n) for n in (
             "vec_loaded", "ctx_loaded", "mask_loaded", "gate_loaded", "wk_loaded", "wv_loaded", "wq_loaded", "wp_loaded",
             "bias_loaded", "ident_ready", "pool_step", "dve_step", "vec_t", "cols_ready", "tanh_ready", "ctx_stats",
             "ctx_rstd", "ctx_normed", "ctx_turned", "ctx_t_ready", "k_done", "k_taken", "k_zeroed", "v_done",
             "wq_hi_ready", "wq_lo_ready", "wp_hi_ready", "wp_lo_ready", "bias_scaled", "fill_ready", "k_hi_ready",
             "k_lo_ready", "v_first", "v_rest_ready", "v_second", "v_ready", "wp_scaled", "minus_ready", "setup_over"))
        x_loaded = sem("x_loaded")
        res_loaded = [sem("res_loaded0"), sem("res_loaded1")]
        (stats_some, stats_ready, ln_step, rstd_ready, norm_ready, xt_turned, xt_f_ready, xt_hi_ready, xt_lo_ready,
         q_done, q_f_ready, q_hi_ready, q_lo_ready, max_done, max_taken, max_turned, max_row_ready, s_done,
         p_f_ready, p_hi_ready, p_lo_dve, p_lo_pool, pv_done, den_inv, o_f_ready, o_hi_ready, o_lo_ready,
         proj_done, x1_ready, res_biased) = (sem(n) for n in (
             "stats_some", "stats_ready", "ln_step", "rstd_ready", "norm_ready", "xt_turned", "xt_f_ready",
             "xt_hi_ready", "xt_lo_ready", "q_done", "q_f_ready", "q_hi_ready", "q_lo_ready", "max_done",
             "max_taken", "max_turned", "max_row_ready", "s_done", "p_f_ready", "p_hi_ready", "p_lo_dve",
             "p_lo_pool", "pv_done", "den_inv", "o_f_ready", "o_hi_ready", "o_lo_ready", "proj_done", "x1_ready",
             "res_biased"))

        def real(i, k, n):
            return not isinstance(i, int) or 0 <= PER * i + k < n

        def every_step(eng, step, setup):
            for k in range(FIRST, PER):
                if k in setup:
                    setup[k]()
                step(0, k)
            with eng.Fori(1, LOOPS - 1) as i:
                for k in range(PER):
                    step(i, k)
            for k in range(LAST - PER * (LOOPS - 1)):
                step(LOOPS - 1, k)

        def load_vectors(eng, which):
            for n in which:
                v, at = vectors[n], n * KB
                eng.dma_start(vec_rows[at:at + v.shape[0] // P, :], v.rearrange("(n p) -> n p", p=P)).then_inc(vec_loaded, 16)

        def proj_bank(i, k):
            return ps_qm if not real(i, k + KB, UNITS) and k % 2 else ps_xp


        block = scope.enter_context(nc.Block())

        @block.sync
        def _(sp):
            def load_x(i, c):
                if real(i, KB * c, UNITS + KB):
                    n = 2 * i + c
                    source = x_chunks[c % 2, i + c // 2, :, :, :] if real(i, KB * c, UNITS) else x1_chunks[0, 0, :, :, :]
                    if not real(i, KB * c, UNITS):
                        for stored in x1_stored:
                            sp.wait_ge(stored, 16 * TT // 2)
                    sp.lower_val(source.offset * 4)
                    after(sp, norm_ready, TT * n)
                    sp.dma_start(x_in[:, :, :], source).then_inc(x_loaded, 16)

            def step(i, k):
                if isinstance(i, int) and PER * i + k == UNITS - 2:
                    sp.wait_ge(q_done, UNITS)
                    g("load_w1")(sp, 0)
                if k % KB == 0:
                    load_x(i, k // KB + 2)
                tile = k - 4
                if real(i, tile, UNITS):
                    c, t = tile // KB, tile % KB
                    source = x_tiles[c % 2, i + c // 2, t, :, :]
                    sp.lower_val(source.offset * 4)
                    after(sp, x1_ready, PER * i + tile - 1)
                    sp.dma_start(x_res[t % 2][:, :], source).then_inc(res_loaded[t % 2], 16)
                if isinstance(i, int) and PER * i + k == UNITS:
                    sp.wait_ge(s_done, HG * UNITS)
                    sp.wait_ge(p_lo_dve, HG // 2 * UNITS)
                    sp.wait_ge(p_lo_pool, HG // 2 * UNITS)
                    g("load_w2")(sp, 0)
                tile = k - 6
                if real(i, tile, UNITS):
                    c, t = tile // KB, tile % KB
                    target = x1_tiles[c % 2, i + c // 2, t, :, :]
                    sp.lower_val(target.offset * 4)
                    after(sp, x1_ready, PER * i + tile + 1)
                    sp.dma_start(target, x1_out[t % 2][:, :]).then_inc(x1_stored[t % 2], 16)

            def load_context():
                sp.dma_start(ctx_sb[:, :, :], ctx.rearrange("b p d -> p b d")).then_inc(ctx_loaded, 16)
                load_vectors(sp, range(0, 5))

            def load_weights():
                w_kv = g("w_kv").rearrange("(k p) n -> p k n", p=P)
                sp.dma_start(wkv[:, :, 0:D], w_kv[:, :, 0:D]).then_inc(wk_loaded, 16)
                sp.dma_start(wq_raw[:, :, :], g("w_q").rearrange("(k p) n -> p k n", p=P)).then_inc(wq_loaded, 16)
                sp.dma_start(wkv[:, :, D:2 * D], w_kv[:, :, D:2 * D]).then_inc(wv_loaded, 16)
                sp.dma_start(wp_raw[:, :, :], g("w_proj").rearrange("(k p) n -> p k n", p=P)).then_inc(wp_loaded, 16)
                sp.dma_start(bp_rows[:, :], g("b_proj").partition_broadcast(P)).then_inc(bias_loaded, 16)
                sp.dma_start(b2_rows[:, :], g("fc2_bias").partition_broadcast(P)).then_inc(bias_loaded, 16)

            every_step(sp, step, {-8: load_context, -7: load_weights})

        @block.tensor
        def _(pe):
            def queries(i, k, blocks):
                v, c, m = PER * i + k, (k // KB) % 2, k % KB
                if 0 in blocks:
                    after(pe, xt_hi_ready, KB * (2 * i + k // KB + 1))
                    after(pe, xt_lo_ready, KB * (2 * i + k // KB + 1))
                    after(pe, q_f_ready, v)
                    after(pe, max_row_ready, v - 1)
                block = slice(m * P, (m + 1) * P)
                last = split_product(nc, ps_qm[:, :], [(wq_hi[:, n, block], wq_lo[:, n, block]) for n in range(KB)],
                                     [(xt_hi[c][:, n, :], xt_lo[c][:, n, :]) for n in range(KB)], blocks)
                if KB - 1 in blocks:
                    last.then_inc(q_done, 1)

            def scores_for_max(i, k, tiles):
                v, b, m = PER * i + k, (k // KB) % 2, k % KB
                after(pe, q_hi_ready, v + 1)
                for t in tiles:
                    after(pe, max_taken, TT * v + t - 1)
                    nc.tensor.matmul(ps_max[t % 2][:, :], q_hi[k % 4][:, t * P:(t + 1) * P],
                                     k_hi[:, b, m, :, :].rearrange("p j n -> p (j n)"),
                                     start=True, stop=True).then_inc(max_done, 1)

            def turn_maxima(i, k):
                v = PER * i + k
                after(pe, max_taken, TT * (v + 1))
                after(pe, q_f_ready, v + 2 if real(i, k + 1, UNITS) else v + 1)
                after(pe, max_row_ready, v)
                for t in range(TT):
                    last = nc.tensor.transpose(ps_qm[0:HG, t * P:(t + 1) * P], maxima[k % 2][:, t, :], ident[:, :])
                last.then_inc(max_turned, 1)

            def scores(i, k, j):
                v, b, m = PER * i + k, (k // KB) % 2, k % KB
                if j == 0:
                    after(pe, q_lo_ready, v + 1)
                    after(pe, max_row_ready, v + 1)
                after(pe, p_hi_ready, HG * v + j - 1)
                to = ps_s[j % 2][:, :]
                nc.tensor.matmul(to, k_hi[:, b, m, j, :], q_hi[k % 4][:, :], start=True, stop=False)
                nc.tensor.matmul(to, k_hi[:, b, m, j, :], q_lo[k % 4][:, :], start=False, stop=False)
                nc.tensor.matmul(to, k_lo[:, b, m, j, :], q_hi[k % 4][:, :], start=False, stop=False)
                nc.tensor.matmul(to, minus_row[:, j, :], max_row[k % 2][:, :], start=False, stop=True).then_inc(s_done, 1)

            def weighted_values(i, k):
                v, b, m = PER * i + k, (k // KB) % 2, k % KB
                after(pe, p_hi_ready, HG * (v + 1))
                after(pe, p_lo_dve, HG // 2 * (v + 1))
                after(pe, p_lo_pool, HG // 2 * (v + 1))
                after(pe, o_f_ready, v)
                terms = [(v_parts[0], p_hi), (v_parts[1], p_hi), (v_parts[2], p_hi), (v_parts[0], p_lo), (v_parts[1], p_lo)]
                for n, (part, probs) in enumerate(terms):
                    for j in range(HG):
                        h = HG * m + j
                        nc.tensor.matmul(ps_o[HEAD * j:HEAD * (j + 1), :], part[:, b, h * HEAD:(h + 1) * HEAD], probs[j][:, :],
                                         start=(n == 0), stop=(n == len(terms) - 1))
                for n, probs in enumerate((p_hi, p_lo)):
                    for j in range(HG):
                        last = nc.tensor.matmul(ps_den[HEAD * j:HEAD * (j + 1), :], ones16[:, :], probs[j][:, :],
                                                start=(n == 0), stop=(n == 1))
                last.then_inc(pv_done, 1)

            def turn_x(i, k):
                job, n = PER * i + k, k % KB
                after(pe, norm_ready, TT * (2 * i + k // KB + 1))
                after(pe, xt_f_ready, job)
                after(pe, x1_ready, job - AHEAD - 5)
                for t in range(TT):
                    last = nc.tensor.transpose(ps_xp[:, t * P:(t + 1) * P], x_norm[:, t, n * P:(n + 1) * P], ident[:, :])
                last.then_inc(xt_turned, 1)

            def project(i, k, blocks):
                tile, c, t = PER * i + k, (k // KB) % 2, k % KB
                chunk = 2 * i + k // KB
                after(pe, o_hi_ready, KB * chunk + max(blocks) + 1)
                after(pe, o_lo_ready, KB * chunk + max(blocks) + 1)
                if 0 in blocks:
                    after(pe, x1_ready, tile if real(i, k + KB - 1, UNITS) else tile - 1)
                    turned = tile + 5 + AHEAD + 1
                    after(pe, xt_f_ready, min(turned, UNITS + KB) if isinstance(i, int) else turned)
                tokens = slice(t * P, (t + 1) * P)
                last = split_product(nc, proj_bank(i, k)[:, :], [(o_hi[c][:, n, tokens], o_lo[c][:, n, tokens]) for n in range(KB)],
                                     [(wp_hi[:, n, :], wp_lo[:, n, :]) for n in range(KB)], blocks)
                if KB - 1 in blocks:
                    last.then_inc(proj_done, 1)

            def step(i, k):
                first, second = range(KB // 2), range(KB // 2, KB)
                if real(i, k + 1, UNITS):
                    scores_for_max(i, k + 1, (0, 1))
                if real(i, k + 2, UNITS):
                    queries(i, k + 2, first)
                if real(i, k + 1, UNITS):
                    scores_for_max(i, k + 1, (2, 3))
                if real(i, k + 2, UNITS):
                    queries(i, k + 2, second)
                if real(i, k + AHEAD, UNITS + KB):
                    turn_x(i, k + AHEAD)
                if real(i, k - 1, UNITS):
                    weighted_values(i, k - 1)
                if real(i, k + 1, UNITS):
                    turn_maxima(i, k + 1)
                if real(i, k, UNITS):
                    scores(i, k, 0)
                    scores(i, k, 1)
                if real(i, k - 5, UNITS) and not real(i, k - 5 + KB, UNITS):
                    if k % 2:
                        for blocks in (first, second):
                            project(i, k - 5, blocks)
                            project(i, k - 4, blocks)
                    return
                if real(i, k - 5, UNITS):
                    project(i, k - 5, first)
                if real(i, k, UNITS):
                    scores(i, k, 2)
                    scores(i, k, 3)
                if real(i, k - 5, UNITS):
                    project(i, k - 5, second)

            def turn_context():
                pe.wait_ge(ident_ready, 1)
                pe.wait_ge(vec_loaded, 16 * len(vectors))
                nc.tensor.transpose(ps_cols[:, 0:NV], vec_rows[:, :], ident[0:NV, 0:NV]).then_inc(vec_t, 1)
                pe.wait_ge(ctx_normed, 1)
                for k in range(KB):
                    if k >= 2:
                        pe.wait_ge(ctx_t_ready, k - 1)
                    for b in range(B):
                        last = nc.tensor.transpose(ps_ctx[k % 2][:, b * KEYS:(b + 1) * KEYS], ctx_sb[:, b, k * P:(k + 1) * P],
                                                   ident[:, :])
                    last.then_inc(ctx_turned, 1)
                pe.wait_ge(ctx_t_ready, KB)

            def keys(m):
                pe.wait_ge(wk_loaded, 16)
                for k in range(KB):
                    last = nc.tensor.matmul(ps_k[m][:, 0:B * KEYS], wkv[:, k, m * P:(m + 1) * P], ctx_t[:, k, :],
                                            start=(k == 0), stop=(k == KB - 1))
                last.then_inc(k_done, 1)

            def first_queries():
                values()
                pe.wait_ge(wq_hi_ready, 1)
                pe.wait_ge(wq_lo_ready, 2)

            def values():
                pe.wait_ge(wv_loaded, 16)
                pe.wait_ge(cols_ready, 1)
                for b in range(B):
                    if b == 1:
                        pe.wait_ge(k_taken, 3)
                    for k in range(KB):
                        last = nc.tensor.matmul(ps_v[b][:, :], ctx_t[:, k, b * KEYS:(b + 1) * KEYS], wkv[:, k, D:2 * D],
                                                start=(k == 0), stop=(k == KB - 1))
                    last.then_inc(v_done, 1)

            def first_maxima():
                pe.wait_ge(k_hi_ready, 1)

            def first_scores():
                pe.wait_ge(k_lo_ready, 1)
                pe.wait_ge(minus_ready, 1)

            def first_values():
                pe.wait_ge(v_ready, 1)

            def second_keys():
                pe.wait_ge(k_hi_ready, B)

            def second_keys_lo():
                pe.wait_ge(k_lo_ready, B)

            def first_projection():
                pe.wait_ge(wp_hi_ready, 1)
                pe.wait_ge(wp_lo_ready, 1)

            every_step(pe, step, {-8: turn_context, -6: lambda: [keys(m) for m in (0, 1)], -5: lambda: keys(2),
                                  -4: lambda: keys(3), -2: first_queries, -1: first_maxima, 0: first_scores, 1: first_values,
                                  3: second_keys, 4: second_keys_lo, 5: first_projection})

        @block.scalar
        def _(act):
            def take_queries(i, k):
                v = PER * i + k
                after(act, q_done, v + 1)
                after(act, s_done, HG * (v - 3))
                nc.scalar.activation(q_hi[k % 4][:, :], ps_qm[:, :], ACT.Identity, scale=SCALE).then_inc(q_hi_ready, 1)
                after(act, q_lo_ready, v - 1)
                nc.scalar.activation(q_f[k % 2][:, :], ps_qm[:, :], ACT.Identity, scale=SCALE).then_inc(q_f_ready, 1)

            def probabilities(i, k, j):
                v, b = PER * i + k, (k // KB) % 2
                if isinstance(i, int) and v == 0 and j == 0:
                    act.wait_ge(fill_ready, 1)
                    act.wait_ge(setup_over, 2)
                after(act, s_done, HG * v + j + 1)
                after(act, p_lo_dve if j < HG // 2 else p_lo_pool, HG // 2 * (v - 1) + j % (HG // 2) + 1)
                nc.scalar.activation(p_f[j][:, :], ps_s[j % 2][:, :], ACT.Exp, bias=fill_col[:, b:b + 1]).then_inc(p_f_ready, 1)
                after(act, pv_done, v)
                nc.scalar.activation(p_hi[j][:, :], ps_s[j % 2][:, :], ACT.Exp, bias=fill_col[:, b:b + 1]).then_inc(p_hi_ready, 1)

            def take_x(i, k):
                job, n = PER * i + k, k % KB
                gain, shift = (gx_c, bx_c) if real(i, k, UNITS) else (lng_c, lnb_c)
                after(act, xt_turned, job + 1)
                after(act, q_done, KB * (2 * i + k // KB - 1))
                nc.scalar.activation(xt_hi[k // KB % 2][:, n, :], ps_xp[:, :], ACT.Identity, bias=shift[:, n:n + 1],
                                     scale=gain[:, n:n + 1]).then_inc(xt_hi_ready, 1)
                after(act, xt_lo_ready, job - 1)
                nc.scalar.activation(xt_f[n % 2][:, :], ps_xp[:, :], ACT.Identity, bias=shift[:, n:n + 1],
                                     scale=gain[:, n:n + 1]).then_inc(xt_f_ready, 1)

            def take_maxima(i, k):
                v = PER * i + k
                after(act, max_turned, v + 1)
                after(act, s_done, HG * (v - 1))
                nc.scalar.copy(max_row[k % 2][0:HG, :], ps_qm[0:HG, :]).then_inc(max_row_ready, 1)

            def outputs_hi(i, k):
                v, c, m = PER * i + k, (k // KB) % 2, k % KB
                after(act, o_f_ready, v + 1)
                if m == 0:
                    after(act, proj_done, KB * (2 * i + k // KB - 1))
                nc.scalar.copy(o_hi[c][:, m, :], o_f[k % 2][:, :]).then_inc(o_hi_ready, 1)

            def step(i, k):
                if real(i, k + 2, UNITS):
                    take_queries(i, k + 2)
                if real(i, k + AHEAD, UNITS + KB):
                    take_x(i, k + AHEAD)
                if real(i, k + 1, UNITS):
                    take_maxima(i, k + 1)
                if real(i, k, UNITS):
                    for j in range(HG):
                        probabilities(i, k, j)
                if real(i, k - 1, UNITS):
                    outputs_hi(i, k - 1)
                if isinstance(i, int):
                    last_steps(PER * i + k)

            def small_loads():
                load_vectors(act, range(5, len(vectors)))
                act.dma_start(gates[:, 0:1], g("g_xattn").partition_broadcast(P)).then_inc(gate_loaded, 16)
                act.dma_start(gates[:, 1:2], g("g_ffn").partition_broadcast(P)).then_inc(gate_loaded, 16)
                act.dma_start(mask_rows[:, :], mask.rearrange("b k -> (b k)").partition_broadcast(P)).then_inc(mask_loaded, 16)
                for b in range(B):
                    act.dma_start(mask_col[:, b:b + 1], mask[b, :].rearrange("(k a) -> k a", a=1)).then_inc(mask_loaded, 16)
                act.wait_ge(gate_loaded, 32)
                nc.scalar.activation(gates[:, :], gates[:, :], ACT.Tanh).then_inc(tanh_ready, 1)
                act.wait_ge(tanh_ready, 1)
                nc.scalar.mul(half_gate[:, :], gates[:, 1:2], 0.5).then_inc(tanh_ready, 1)
                act.wait_ge(cols_ready, 1)
                for k in range(KB):
                    act.wait_ge(ctx_turned, k + 1)
                    nc.scalar.activation(ctx_t[:, k, :], ps_ctx[k % 2][:, 0:B * KEYS], ACT.Identity,
                                         bias=bkv_c[:, k:k + 1], scale=gkv_c[:, k:k + 1]).then_inc(ctx_t_ready, 1)

            def query_weights():
                act.wait_ge(wq_loaded, 16)
                nc.scalar.copy(wq_hi[:, :, :], wq_raw[:, :, :]).then_inc(wq_hi_ready, 1)

            def projection_weights():
                act.wait_ge(minus_ready, 1)
                act.wait_ge(wp_loaded, 16)
                nc.scalar.activation(wp_raw[:, :, :], wp_raw[:, :, :], ACT.Identity, scale=gates[:, 0:1]).then_inc(wp_scaled, 1)
                act.wait_ge(wp_scaled, 1)
                nc.scalar.copy(wp_hi[:, :, :], wp_raw[:, :, :]).then_inc(wp_hi_ready, 1)
                act.wait_ge(bias_loaded, 32)
                nc.scalar.activation(bp_rows[:, :], bp_rows[:, :], ACT.Identity, scale=gates[:, 0:1]).then_inc(bias_scaled, 1)
                nc.scalar.activation(b2_rows[:, :], b2_rows[:, :], ACT.Identity, scale=half_gate[:, :])

            def values_first_part():
                for b in range(B):
                    act.wait_ge(v_done, b + 1)
                    nc.scalar.copy(v_parts[0][:, b, :], ps_v[b][:, :]).then_inc(v_first, 1)

            def values_second_part():
                for b in range(B):
                    act.wait_ge(v_rest_ready, b + 1)
                    nc.scalar.copy(v_parts[1][:, b, :], v_rest[:, b, :]).then_inc(v_second, 1)

            def second_keys_hi():
                act.wait_ge(k_hi_ready, 1)
                for j in range(HG):
                    at = slice(HEAD * j, HEAD * (j + 1))
                    last = nc.scalar.copy(k_hi[at, 1, :, j, :], k_full[at, :, KEYS:2 * KEYS])
                last.then_inc(k_hi_ready, 1)

            def last_steps(u):
                if u in (UNITS + 1, UNITS + 3):
                    g("weights_hi")(act, 0, (u - UNITS) // 2)

            every_step(act, step, {-8: small_loads, -5: query_weights, -2: projection_weights, -1: values_first_part,
                                   0: values_second_part, 1: second_keys_hi})

        @block.vector
        def _(dve):
            def take_max(i, k, tiles):
                v = PER * i + k
                after(dve, max_turned, v - 1)
                for t in tiles:
                    after(dve, max_done, TT * v + t + 1)
                    nc.vector.reduce_max(maxima[k % 2][:, t, :], ps_max[t % 2][:, :].rearrange("p (j n) -> p j n", j=HG),
                                         AX.X).then_inc(max_taken, 1)

            def invert_sums(i, k):
                v = PER * i + k
                after(dve, pv_done, v + 1)
                after(dve, o_f_ready, v)
                nc.vector.reciprocal(inv_den[:, :], ps_den[:, :]).then_inc(den_inv, 1)

            def normalise(i, k):
                v = PER * i + k
                after(dve, o_hi_ready, v - 1)
                after(dve, o_lo_ready, v - 1)
                after(dve, den_inv, v + 1)
                nc.vector.tensor_tensor(o_f[k % 2][:, :], ps_o[:, :], inv_den[:, :], ALU.mult).then_inc(o_f_ready, 1)

            def probabilities_lo(i, k, j):
                v = PER * i + k
                if isinstance(i, int) and v == 0 and j == 0:
                    dve.wait_ge(setup_over, 2)
                after(dve, p_f_ready, HG * v + j + 1)
                after(dve, p_hi_ready, HG * v + j + 1)
                nc.vector.tensor_tensor(p_lo[j][:, :], p_f[j][:, :], p_hi[j][:, :], ALU.subtract).then_inc(p_lo_dve, 1)

            def add_residual(i, k):
                tile = PER * i + k
                after(dve, proj_done, tile + 1)
                after(dve, res_biased, tile + 1)
                if real(i, k - 2, UNITS):
                    after(dve, x1_stored[k % 2], 8 * (tile - k % 2))
                nc.vector.tensor_tensor(x1_out[k % 2][:, :], proj_bank(i, k)[:, :], x_res[k % 2][:, :], ALU.add).then_inc(x1_ready, 1)

            def row_stats(i, c):
                if not real(i, KB * c, UNITS + KB):
                    return
                chunk = 2 * i + c
                after(dve, x_loaded, 16 * (chunk + 1))
                for t in range(TT):
                    nc.vector.bn_stats(stats[:, t, :], x_in[:, t, :]).then_inc(stats_some, 1)
                after(dve, rstd_ready, chunk)
                after(dve, stats_some, TT * (chunk + 1))
                nc.vector.memset(pause[:, :], 0.0)
                for t in range(TT):
                    last = nc.vector.bn_aggr(mean_var[:, t, :], stats[:, t, :])
                last.then_inc(stats_ready, 1)

            def normalise_rows(i, c):
                if not real(i, KB * c, UNITS + KB):
                    return
                chunk = 2 * i + c
                after(dve, rstd_ready, chunk + 1)
                after(dve, stats_ready, chunk + 1)
                after(dve, xt_turned, KB * chunk)
                for t in range(TT):
                    nc.vector.tensor_scalar(x_norm[:, t, :], x_in[:, t, :], mean_var[:, t, 0:1], ln_r[:, t:t + 1],
                                            ALU.subtract, ALU.mult).then_inc(norm_ready, 1)

            def step(i, k):
                if real(i, k + 1, UNITS):
                    take_max(i, k + 1, (0, 1))
                if real(i, k - 6, UNITS):
                    add_residual(i, k - 6)
                if real(i, k + 1, UNITS):
                    take_max(i, k + 1, (2, 3))
                if k % KB == 0:
                    row_stats(i, k // KB + 2)
                if k % KB == 1:
                    normalise_rows(i, k // KB + 2)
                if real(i, k - 1, UNITS):
                    invert_sums(i, k - 1)
                if real(i, k, UNITS):
                    probabilities_lo(i, k, 0)
                    probabilities_lo(i, k, 1)
                if real(i, k - 1, UNITS):
                    normalise(i, k - 1)
                if isinstance(i, int):
                    last_steps(PER * i + k)

            done = [0]

            def link(ins):
                done[0] += 1
                ins.then_inc(dve_step, 1)
                dve.wait_ge(dve_step, done[0])

            def context_rows():
                nc.vector.memset(k_hi[:, :, :, :, :].bitcast(F32), 0.0)
                dve.wait_ge(ctx_loaded, 16)
                for b in range(B):
                    last = nc.vector.bn_stats(ctx_bn[:, b, :], ctx_sb[:, b, :])
                link(last)
                for b in range(B):
                    last = nc.vector.bn_aggr(ctx_mv[:, b, :], ctx_bn[:, b, :])
                last.then_inc(ctx_stats, 1)
                dve.wait_ge(ctx_rstd, 1)
                for b in range(B):
                    last = nc.vector.tensor_scalar(ctx_sb[:, b, :], ctx_sb[:, b, :], ctx_mv[:, b, 0:1], ctx_r[:, b:b + 1],
                                                   ALU.subtract, ALU.mult)
                last.then_inc(ctx_normed, 1)
                dve.wait_ge(vec_t, 1)
                nc.vector.tensor_copy(cols[:, :], ps_cols[:, 0:NV]).then_inc(cols_ready, 1)

            def masks():
                dve.wait_ge(mask_loaded, 16 * (1 + B))
                nc.vector.tensor_scalar(masked[:, :], mask_rows[:, :], 0.0, None, ALU.is_equal)
                link(nc.vector.tensor_scalar(valid[:, :], mask_rows[:, :], 0.0, None, ALU.not_equal))
                link(nc.vector.reduce_sum(n_valid[:, :], valid[:, :].rearrange("p (b k) -> p b k", b=B), AX.X))
                nc.vector.tensor_scalar(some_valid[:, :], n_valid[:, :], 1.0, None, ALU.min)
                link(nc.vector.tensor_scalar(divisor[:, :], n_valid[:, :], 1.0, None, ALU.max))
                link(nc.vector.reciprocal(inv_divisor[:, :], divisor[:, :]))
                link(nc.vector.tensor_scalar(fill_a[:, :], mask_col[:, :], 0.0, FILL, ALU.is_equal, ALU.mult))
                nc.vector.tensor_tensor(fill_col[:, :], fill_a[:, :], some_valid[:, :], ALU.mult).then_inc(fill_ready, 1)

            def key_parts():
                dve.wait_ge(wq_hi_ready, 1)
                half = slice(0, KB // 2)
                nc.vector.tensor_tensor(wq_lo[:, half, :], wq_raw[:, half, :], wq_hi[:, half, :].bitcast(F32),
                                        ALU.subtract).then_inc(wq_lo_ready, 1)
                for m in range(KB):
                    dve.wait_ge(k_done, m + 1)
                    last = nc.vector.tensor_tensor(k_full[:, m, :], ps_k[m][:, 0:B * KEYS], valid[:, :], ALU.mult)
                    last.then_inc(k_taken, 1)

            def key_means():
                dve.wait_ge(k_taken, KB)
                link(nc.vector.reduce_sum(k_sum[:, :, :], k_full[:, :, :].rearrange("p m (b k) -> p m b k", b=B), AX.X))
                for b in range(B):
                    last = nc.vector.tensor_scalar(k_mean[:, :, b], k_sum[:, :, b], inv_divisor[:, b:b + 1], None, ALU.mult)
                link(last)
                for m in range(KB):
                    for b in range(B):
                        keys = slice(b * KEYS, (b + 1) * KEYS)
                        last = nc.vector.scalar_tensor_tensor(
                            out=k_full[:, m, keys], in0=masked[:, keys], scalar=k_mean[:, m, b:b + 1],
                            in1=k_full[:, m, keys], op0=ALU.mult, op1=ALU.add)
                link(last)
                for j in range(HG):
                    at = slice(HEAD * j, HEAD * (j + 1))
                    last = nc.vector.tensor_copy(k_hi[at, 0, :, j, :], k_full[at, :, 0:KEYS])
                last.then_inc(k_hi_ready, 1)

            def keys_lo(b):
                dve.wait_ge(k_hi_ready, b + 1)
                dve.wait_ge(k_zeroed, 1)
                for j in range(HG):
                    at = slice(HEAD * j, HEAD * (j + 1))
                    last = nc.vector.tensor_tensor(k_lo[at, b, :, j, :], k_full[at, :, b * KEYS:(b + 1) * KEYS],
                                                   k_hi[at, b, :, j, :].bitcast(F32), ALU.subtract)
                last.then_inc(k_lo_ready, 1)

            def value_parts():
                for b in range(B):
                    dve.wait_ge(v_first, b + 1)
                    nc.vector.tensor_tensor(v_rest[:, b, :], ps_v[b][:, :], v_parts[0][:, b, :], ALU.subtract).then_inc(v_rest_ready, 1)
                for b in range(B):
                    dve.wait_ge(v_second, b + 1)
                    last = nc.vector.tensor_tensor(v_parts[2][:, b, :], v_rest[:, b, :], v_parts[1][:, b, :], ALU.subtract)
                last.then_inc(v_ready, 1)
                nc.vector.memset(pause[:, :], 0.0).then_inc(setup_over, 1)

            def last_steps(u):
                if u in (UNITS + 1, UNITS + 3):
                    dve.wait_ge(proj_done, UNITS - KB)
                    g("weights")(dve, 0, (u - UNITS) // 2)

            every_step(dve, step, {-8: context_rows, -7: masks, -4: lambda: [key_parts(), key_means()], -3: lambda: keys_lo(0),
                                   0: value_parts, 3: lambda: keys_lo(1)})

        @block.gpsimd
        def _(pool):
            def queries_lo(i, k):
                v = PER * i + k
                after(pool, q_f_ready, v + 1)
                after(pool, s_done, HG * (v - 3))
                nc.gpsimd.tensor_tensor(q_lo[k % 4][:, :], q_f[k % 2][:, :], q_hi[k % 4][:, :].bitcast(F32),
                                        ALU.subtract).then_inc(q_lo_ready, 1)

            def bias_residual(i, k):
                tile = PER * i + k
                after(pool, res_loaded[k % 2], 8 * (tile - k % 2) + 16)
                nc.gpsimd.tensor_tensor(x_res[k % 2][:, :], x_res[k % 2][:, :], bp_rows[:, :], ALU.add).then_inc(res_biased, 1)

            def outputs_lo(i, k):
                v, c, m = PER * i + k, (k // KB) % 2, k % KB
                after(pool, o_hi_ready, v + 1)
                if m == 0:
                    after(pool, proj_done, KB * (2 * i + k // KB - 1))
                nc.gpsimd.tensor_tensor(o_lo[c][:, m, :], o_f[k % 2][:, :], o_hi[c][:, m, :].bitcast(F32),
                                        ALU.subtract).then_inc(o_lo_ready, 1)

            def x_lo(i, k):
                c, n, chunk = k // KB, k % KB, 2 * i + k // KB
                after(pool, xt_f_ready, PER * i + k + 1)
                after(pool, q_done, KB * (chunk - 1))
                nc.gpsimd.tensor_tensor(xt_lo[c % 2][:, n, :], xt_f[n % 2][:, :], xt_hi[c % 2][:, n, :].bitcast(F32),
                                        ALU.subtract).then_inc(xt_lo_ready, 1)

            def probabilities_lo(i, k, j):
                v = PER * i + k
                if isinstance(i, int) and v == 0 and j == 2:
                    pool.wait_ge(setup_over, 2)
                after(pool, p_f_ready, HG * v + j + 1)
                after(pool, p_hi_ready, HG * v + j + 1)
                nc.gpsimd.tensor_tensor(p_lo[j][:, :], p_f[j][:, :], p_hi[j][:, :], ALU.subtract).then_inc(p_lo_pool, 1)

            def row_scales(i, c):
                if not real(i, KB * c, UNITS + KB):
                    return
                chunk = 2 * i + c
                after(pool, stats_ready, chunk + 1)
                after(pool, norm_ready, TT * chunk)
                var = mean_var[:, :, 1]
                nc.gpsimd.tensor_tensor(ln_a[:, :], var, eps[:, :], ALU.add).then_inc(ln_step, 1)
                after(pool, ln_step, 6 * chunk + 1)
                nc.gpsimd.tensor_tensor(ln_r1[:, :], ln_a[:, :], expo[:, 0, :], ALU.pow).then_inc(ln_step, 1)
                after(pool, ln_step, 6 * chunk + 2)
                nc.gpsimd.tensor_tensor(ln_b[:, :], var, ln_r1[:, :], ALU.mult).then_inc(ln_step, 1)
                after(pool, ln_step, 6 * chunk + 3)
                nc.gpsimd.tensor_tensor(ln_c[:, :], ln_b[:, :], ln_r1[:, :], ALU.mult).then_inc(ln_step, 1)
                after(pool, ln_step, 6 * chunk + 4)
                nc.gpsimd.tensor_tensor(ln_a[:, :], ln_c[:, :], eps[:, :], ALU.add).then_inc(ln_step, 1)
                after(pool, ln_step, 6 * chunk + 5)
                nc.gpsimd.tensor_tensor(ln_r2[:, :], ln_a[:, :], expo[:, 0, :], ALU.pow).then_inc(ln_step, 1)
                after(pool, ln_step, 6 * chunk + 6)
                nc.gpsimd.tensor_tensor(ln_r[:, :], ln_r1[:, :], ln_r2[:, :], ALU.mult).then_inc(rstd_ready, 1)
                if not real(i, KB * c, UNITS):
                    pool.wait_ge(tanh_ready, 2)
                    nc.gpsimd.tensor_tensor(ln_s2[:, :], ln_a[:, :], expo[:, 1, :], ALU.pow).then_inc(ln_step, 1)
                    after(pool, ln_step, 6 * chunk + 7)
                    nc.gpsimd.tensor_tensor(u_scale[:, :], ln_s2[:, :], gates[:, 1:2].to_broadcast([P, TT]), ALU.mult)

            def step(i, k):
                if real(i, k + 2, UNITS):
                    queries_lo(i, k + 2)
                if real(i, k + AHEAD, UNITS + KB):
                    x_lo(i, k + AHEAD)
                if real(i, k - 5, UNITS):
                    bias_residual(i, k - 5)
                if k % KB == 0 and k != -KB:
                    row_scales(i, k // KB + 2)
                if real(i, k, UNITS):
                    probabilities_lo(i, k, 2)
                    probabilities_lo(i, k, 3)
                if real(i, k - 1, UNITS):
                    outputs_lo(i, k - 1)

            done = [0]

            def link(ins):
                done[0] += 1
                ins.then_inc(pool_step, 1)
                pool.wait_ge(pool_step, done[0])

            def constants():
                link(nc.gpsimd.memset(ident[:, :], 0.0))
                nc.gpsimd.affine_select(out=ident[:, :], in_=ident[:, :], compare_op=ALU.not_equal, fill=1.0, base=0,
                                        pattern=[[-1, P]], channel_multiplier=1).then_inc(ident_ready, 1)
                nc.gpsimd.memset(ones16[:, :], 1.0)
                nc.gpsimd.memset(expo[:, 1, :], 0.5)
                nc.gpsimd.memset(eps[:, :], EPS)
                link(nc.gpsimd.memset(expo[:, 0, :], -0.5))
                nc.gpsimd.memset(k_lo[:, :, :, :, :].bitcast(F32), 0.0).then_inc(k_zeroed, 1)
                pool.wait_ge(ctx_stats, 1)
                link(nc.gpsimd.tensor_scalar(var_eps[:, :], ctx_mv[:, :, 1], EPS, None, ALU.add))
                nc.gpsimd.tensor_tensor(ctx_r[:, :], var_eps[:, :], expo[:, 0, 0:B], ALU.pow).then_inc(ctx_rstd, 1)

            def maxima_constants():
                nc.gpsimd.memset(max_row[0][:, :].bitcast(F32), 0.0)
                nc.gpsimd.memset(max_row[1][:, :].bitcast(F32), 0.0)
                link(nc.gpsimd.memset(minus_f[:, :, :], 0.0))
                link(nc.gpsimd.affine_select(out=minus_f[:, :, :], in_=minus_f[:, :, :], compare_op=ALU.not_equal,
                                             fill=-1.0, base=0, pattern=[[-1, HG], [0, KEYS]], channel_multiplier=1))
                nc.gpsimd.tensor_copy(minus_row[:, :, :], minus_f[:, :, :]).then_inc(minus_ready, 1)

            def query_weights_lo():
                pool.wait_ge(wq_hi_ready, 1)
                for k in range(KB // 2, KB):
                    last = nc.gpsimd.tensor_tensor(wq_lo[:, k, :], wq_raw[:, k, :], wq_hi[:, k, :].bitcast(F32), ALU.subtract)
                last.then_inc(wq_lo_ready, 1)

            def projection_weights_lo():
                row_scales(0, 1)
                pool.wait_ge(wp_hi_ready, 1)
                for k in range(KB):
                    last = nc.gpsimd.tensor_tensor(wp_lo[:, k, :], wp_raw[:, k, :], wp_hi[:, k, :].bitcast(F32), ALU.subtract)
                last.then_inc(wp_lo_ready, 1)
                nc.gpsimd.memset(pool_pause[:, :], 0.0).then_inc(setup_over, 1)

            def first_outputs():
                pool.wait_ge(bias_scaled, 1)
                pool.wait_ge(k_lo_ready, B)

            every_step(pool, step, {-8: constants, -6: maxima_constants, -4: query_weights_lo, -2: projection_weights_lo,
                              4: first_outputs})


def feed_forward(nc, env):
    g = env.get
    eps, pause, act_pause = g("eps"), g("pause"), g("act_pause")
    (gates, half_gate, expo, b2_rows, ident, lng_c, lnb_c, b1_c, x1_chunks, out_chunks, fc2_q, fc2_scales, s1_raw, q1_raw,
     s2_raw, q2_raw, load_w1, load_w2, w1_loaded, w2_loaded) = (g(n) for n in (
         "gates", "half_gate", "expo", "b2_rows", "ident", "lng_c", "lnb_c", "b1_c", "x1_chunks", "out_chunks",
         "fc2_q", "fc2_scales", "s1_raw", "q1_raw", "s2_raw", "q2_raw", "load_w1", "load_w2", "w1_loaded", "w2_loaded"))
    x1_norm, ht_f, ht_hi, ht_lo = (g(n) for n in ("x_norm", "xt_f", "xt_hi", "xt_lo"))
    (w1_hi, w1_lo, w2_hi, w2_lo, y_f, y_hi, y_lo, w_steps, weights, weights_hi, w1_ready, w2_ready) = (g(n) for n in (
        "w1_hi", "w1_lo", "w2_hi", "w2_lo", "y_f", "y_hi", "y_lo", "w_steps", "weights", "weights_hi", "w1_ready",
        "w2_ready"))
    x1 = [g("x_in"), g("x1_1")]
    stats, mean_var, ln_a, ln_r1, ln_b, ln_c, ln_r2, ln_s2, ln_r, u_scale = (
        g(n) for n in ("stats", "mean_var", "ln_a", "ln_r1", "ln_b", "ln_c", "ln_r2", "ln_s2", "ln_r", "u_scale"))
    D, KB, FB, TT, NCHUNK, GROUP = (g(n) for n in ("D", "KB", "FB", "TT", "NCHUNK", "GROUP"))
    LAG = 2
    PER = 2 * FB
    STEPS = NCHUNK * FB
    LOOPS = STEPS // PER

    with ExitStack() as scope:
        def sem(name):
            return scope.enter_context(nc.semaphore(name))

        def psum(name):
            return scope.enter_context(nc.psum_tensor(name, [P, 512], F32))

        ps_y = [psum("ps_y0"), psum("ps_y1")]
        ps_h = [psum("ps_h0"), psum("ps_h1")]
        ps_z = [psum(f"ps_z{t}") for t in range(TT)]

        x1_loaded = [sem("x1_loaded0"), sem("x1_loaded1")]
        out_stored, last_stored = [sem("out_stored0"), sem("out_stored1")], sem("last_stored")
        (stats_some, stats_ready, ln_step, scales_ready, norm_ready, sum_ready, base_ready, h_turned, h_f_ready,
         h_hi_ready, h_lo_ready, y_done, y_f_ready, y_hi_ready, y_lo_ready, z_done, z_used, out_ready) = (
            sem(n) for n in ("f_stats_some", "f_stats_ready", "f_ln_step", "f_scales_ready", "f_norm_ready",
                             "sum_ready", "base_ready", "h_turned", "h_f_ready", "h_hi_ready", "h_lo_ready", "y_done",
                             "y_f_ready", "y_hi_ready", "y_lo_ready", "z_done", "z_used", "out_ready"))

        def every_step(eng, step):
            for k in range(-2, PER):
                step(0, k)
            with eng.Fori(1, LOOPS - 1) as i:
                for k in range(PER):
                    step(i, k)
            for k in range(PER + LAG + 1):
                step(LOOPS - 1, k)

        def real(i, k):
            return not isinstance(i, int) or 0 <= PER * i + k < STEPS

        LOAD, STATS, SCALES, NORM, TURN, BASE = 3, 6, 7, 8, 10, 14
        EVACUATE = LAG

        block = scope.enter_context(nc.Block())

        @block.sync
        def _(sp):
            def step(i, k):
                c, f = k // FB, k % FB
                if isinstance(i, int) and i == 0 and k in (-2, LOAD + 1):
                    half = FB // GROUP // 2
                    for n in range(half) if k == -2 else range(half, 2 * half):
                        if n > 0:
                            load_w1(sp, n)
                            load_w2(sp, n)
                if f == LOAD and real(i, FB * (c + 1)):
                    chunk = 2 * i + c + 1
                    if isinstance(i, int) and i == 0 and c == 0:
                        for stored in g("x1_stored"):
                            sp.wait_ge(stored, 16 * TT * NCHUNK // 2)
                    source = x1_chunks[(c + 1) % 2, i + (c + 1) // 2, :, :, :]
                    sp.lower_val(source.offset * 4)
                    after(sp, out_stored[(c + 1) % 2], 16 * (i + (c + 1) // 2))
                    sp.dma_start(x1[(c + 1) % 2][:, :, :], source)\
                        .then_inc(x1_loaded[(c + 1) % 2], 16)
                if f == EVACUATE and real(i, FB * (c - 1)):
                    chunk = 2 * i + c - 1
                    if not real(i, FB * c):
                        for t in range(TT):
                            sp.wait_ge(out_ready, TT * chunk + t + 1)
                            sp.dma_start(out_chunks[(c - 1) % 2, i + (c - 1) // 2, :, t, :], x1[(c - 1) % 2][:, t, :])\
                                .then_inc(last_stored, 16)
                        return
                    target = out_chunks[(c - 1) % 2, i + (c - 1) // 2, :, :, :]
                    sp.lower_val(target.offset * 4)
                    after(sp, out_ready, TT * (chunk + 1))
                    sp.dma_start(target, x1[(c - 1) % 2][:, :, :]).then_inc(out_stored[(c - 1) % 2], 16)

            every_step(sp, step)
            sp.wait_ge(out_stored[0], 16 * (NCHUNK // 2))
            sp.wait_ge(out_stored[1], 16 * (NCHUNK // 2 - 1))
            sp.wait_ge(last_stored, 16 * TT)

        @block.tensor
        def _(pe):
            def hidden(i, k):
                s, c, f = PER * i + k, (k // FB) % 2, k % FB
                if isinstance(i, int) and i == 0 and k < FB:
                    after(pe, w1_ready, k // 2 + 1)
                if f == 0:
                    after(pe, h_hi_ready, KB * (2 * i + k // FB))
                    after(pe, h_lo_ready, KB * (2 * i + k // FB))
                after(pe, y_f_ready, s - 1)
                cols = slice(f % GROUP * P, (f % GROUP + 1) * P)
                split_product(nc, ps_y[f % 2][:, :], [(w1_hi[:, f // GROUP, n, cols], w1_lo[:, f // GROUP, n, cols]) for n in range(KB)],
                              [(ht_hi[c][:, n, :], ht_lo[c][:, n, :]) for n in range(KB)]).then_inc(y_done, 1)

            def sums(i, k):
                s, f = PER * i + k, k % FB
                if isinstance(i, int) and i == 0 and k < FB:
                    after(pe, w2_ready, k // 2 + 1)
                after(pe, y_hi_ready, s + 1)
                after(pe, y_lo_ready, s + 1)
                for t in range(TT):
                    if f == 0:
                        after(pe, out_ready, TT * (2 * i + k // FB - 1) + t + 1)
                    tokens = slice(t * P, (t + 1) * P)
                    hi, lo = y_hi[f % 4][:, tokens], y_lo[f % 4][:, tokens]
                    nc.tensor.matmul(ps_z[t][:, :], hi, w2_hi[:, f, :], start=(f == 0), stop=False)
                    nc.tensor.matmul(ps_z[t][:, :], hi, w2_lo[:, f, :], start=False, stop=False)
                    last = nc.tensor.matmul(ps_z[t][:, :], lo, w2_hi[:, f, :], start=False, stop=(f == FB - 1))
                    if f == FB - 1 and t < TT - 1:
                        last.then_inc(z_done, 1)
                last.then_inc(z_used, 1)

            def turn_h(i, c, n):
                if not real(i, FB * c):
                    return
                chunk = 2 * i + c
                after(pe, norm_ready, TT * chunk)
                after(pe, h_f_ready, KB * (chunk - 1) + n - 1)
                for t in range(TT):
                    last = nc.tensor.transpose(ps_h[n % 2][:, t * P:(t + 1) * P], x1_norm[:, t, n * P:(n + 1) * P], ident[:, :])
                last.then_inc(h_turned, 1)

            def step(i, k):
                if real(i, k):
                    hidden(i, k)
                if TURN <= k % FB < TURN + KB:
                    turn_h(i, k // FB + 1, k % FB - TURN)
                if real(i, k - LAG):
                    sums(i, k - LAG)

            every_step(pe, step)

        @block.scalar
        def _(act):
            def step(i, k):
                if real(i, k):
                    s, f = PER * i + k, k % FB
                    after(act, y_done, s + 1)
                    after(act, y_hi_ready, s - 1)
                    after(act, y_lo_ready, s - 1)
                    nc.scalar.activation(y_f[f % 2][:, :], ps_y[f % 2][:, :], ACT.Silu, bias=b1_c[:, f:f + 1]).then_inc(y_f_ready, 1)
                if isinstance(i, int) and i == 0 and k in w_steps and k >= 0:
                    weights_hi(act, *w_steps[k])
                if TURN <= k % FB < TURN + KB and real(i, FB * (k // FB + 1)):
                    n = k % FB - TURN
                    job = KB * (2 * i + k // FB) + n
                    after(act, h_turned, job + 1)
                    after(act, h_hi_ready, job - 1)
                    after(act, h_lo_ready, job - 1)
                    nc.scalar.activation(ht_f[n % 2][:, :], ps_h[n % 2][:, :], ACT.Identity, bias=lnb_c[:, n:n + 1],
                                         scale=lng_c[:, n:n + 1]).then_inc(h_f_ready, 1)

            nc.scalar.activation(act_pause[:, :], half_gate[:, :], ACT.Silu)
            every_step(act, step)

        @block.vector
        def _(dve):
            def split_hidden(i, k):
                s, f = PER * i + k, k % FB
                if isinstance(i, int) and s == 0:
                    for stored in g("x1_stored"):
                        dve.wait_ge(stored, 16 * TT * NCHUNK // 2)
                after(dve, y_f_ready, s + 1)
                after(dve, z_used, s - 3)
                nc.vector.tensor_copy(y_hi[f % 4][:, :], y_f[f % 2][:, :]).then_inc(y_hi_ready, 1)
                after(dve, y_hi_ready, s + 1)
                nc.vector.tensor_tensor(y_lo[f % 4][:, :], y_f[f % 2][:, :], y_hi[f % 4][:, :].bitcast(F32),
                                        ALU.subtract).then_inc(y_lo_ready, 1)

            def split_h(i, c, n):
                chunk = 2 * i + c
                after(dve, h_f_ready, KB * (chunk - 1) + n + 1)
                after(dve, y_done, FB * (chunk - 1))
                nc.vector.tensor_copy(ht_hi[c % 2][:, n, :], ht_f[n % 2][:, :]).then_inc(h_hi_ready, 1)
                after(dve, h_hi_ready, KB * (chunk - 1) + n + 1)
                nc.vector.tensor_tensor(ht_lo[c % 2][:, n, :], ht_f[n % 2][:, :], ht_hi[c % 2][:, n, :].bitcast(F32),
                                        ALU.subtract).then_inc(h_lo_ready, 1)

            def take_sums(i, c):
                chunk = 2 * i + c
                after(dve, base_ready, TT * (chunk + 1))
                for t in range(TT):
                    if t < TT - 1:
                        after(dve, z_done, (TT - 1) * chunk + t + 1)
                    else:
                        after(dve, z_used, FB * (chunk + 1))
                    out_t = x1[c % 2][:, t, :]
                    nc.vector.tensor_tensor(out_t, ps_z[t][:, :], out_t, ALU.add).then_inc(out_ready, 1)

            def step(i, k):
                c, f = k // FB, k % FB
                if f == EVACUATE and real(i, FB * (c - 1)):
                    take_sums(i, c - 1)
                if real(i, k):
                    split_hidden(i, k)
                if isinstance(i, int) and i == 0 and k in w_steps and k >= 0:
                    weights(dve, *w_steps[k])
                if not real(i, FB * (c + 1)):
                    return
                chunk, b = 2 * i + c + 1, (c + 1) % 2
                if f == STATS:
                    after(dve, x1_loaded[b], 16 * (i + (c + 1) // 2 + b))
                    after(dve, stats_ready, chunk - 1)
                    for t in range(TT):
                        nc.vector.bn_stats(stats[:, t, :], x1[b][:, t, :]).then_inc(stats_some, 1)
                    after(dve, scales_ready, chunk - 1)
                    after(dve, stats_some, TT * chunk)
                    nc.vector.memset(pause[:, :], 0.0)
                    for t in range(TT):
                        last = nc.vector.bn_aggr(mean_var[:, t, :], stats[:, t, :])
                    last.then_inc(stats_ready, 1)
                if f == NORM:
                    after(dve, scales_ready, chunk)
                    after(dve, h_turned, KB * (chunk - 1))
                    after(dve, sum_ready, TT * chunk)
                    for t in range(TT):
                        nc.vector.tensor_scalar(x1_norm[:, t, :], x1[b][:, t, :], mean_var[:, t, 0:1], ln_r[:, t:t + 1],
                                                ALU.subtract, ALU.mult).then_inc(norm_ready, 1)
                if TURN <= f < TURN + KB:
                    split_h(i, c + 1, f - TURN)
                if f == BASE:
                    for t in range(TT):
                        after(dve, norm_ready, TT * (chunk - 1) + t + 1)
                        nc.vector.scalar_tensor_tensor(out=x1[b][:, t, :], in0=x1_norm[:, t, :], scalar=u_scale[:, t:t + 1],
                                                       in1=x1[b][:, t, :], op0=ALU.mult, op1=ALU.add).then_inc(sum_ready, 1)

            every_step(dve, step)

        @block.gpsimd
        def _(pool):
            def step(i, k):
                c, f = k // FB, k % FB
                if not real(i, FB * (c + 1)):
                    return
                chunk, b = 2 * i + c + 1, (c + 1) % 2
                if f == SCALES:
                    after(pool, stats_ready, chunk)
                    after(pool, norm_ready, TT * (chunk - 1))
                    after(pool, sum_ready, TT * chunk)
                    var = mean_var[:, :, 1]
                    steps = 7 * (chunk - 1)
                    nc.gpsimd.tensor_tensor(ln_a[:, :], var, eps[:, :], ALU.add).then_inc(ln_step, 1)
                    after(pool, ln_step, steps + 1)
                    nc.gpsimd.tensor_tensor(ln_r1[:, :], ln_a[:, :], expo[:, 0, :], ALU.pow).then_inc(ln_step, 1)
                    after(pool, ln_step, steps + 2)
                    nc.gpsimd.tensor_tensor(ln_b[:, :], var, ln_r1[:, :], ALU.mult).then_inc(ln_step, 1)
                    after(pool, ln_step, steps + 3)
                    nc.gpsimd.tensor_tensor(ln_c[:, :], ln_b[:, :], ln_r1[:, :], ALU.mult).then_inc(ln_step, 1)
                    after(pool, ln_step, steps + 4)
                    nc.gpsimd.tensor_tensor(ln_a[:, :], ln_c[:, :], eps[:, :], ALU.add).then_inc(ln_step, 1)
                    after(pool, ln_step, steps + 5)
                    nc.gpsimd.tensor_tensor(ln_r2[:, :], ln_a[:, :], expo[:, 0, :], ALU.pow).then_inc(ln_step, 1)
                    nc.gpsimd.tensor_tensor(ln_s2[:, :], ln_a[:, :], expo[:, 1, :], ALU.pow).then_inc(ln_step, 1)
                    after(pool, ln_step, steps + 7)
                    nc.gpsimd.tensor_tensor(u_scale[:, :], ln_s2[:, :], gates[:, 1:2].to_broadcast([P, TT]), ALU.mult)
                    nc.gpsimd.tensor_tensor(ln_r[:, :], ln_r1[:, :], ln_r2[:, :], ALU.mult).then_inc(scales_ready, 1)
                if f == BASE:
                    for t in range(TT):
                        after(pool, sum_ready, TT * chunk + t + 1)
                        nc.gpsimd.tensor_tensor(x1[b][:, t, :], x1[b][:, t, :], b2_rows[:, :], ALU.add).then_inc(base_ready, 1)

            every_step(pool, step)


_INS = ['x', 'ctx_1024', 'mask_BxS2_ik0', 'g_xattn', 'g_ffn', 'L0_xattn_w_q', 'L0_xattn_w_kv', 'L0_xattn_w_proj',
        'L0_xattn_b_proj', 'L0_xattn_g_x', 'L0_xattn_b_x', 'L0_xattn_g_kv', 'L0_xattn_b_kv', 'L0_ffn_ln_gamma',
        'L0_ffn_ln_beta', 'L0_ffn_fc1_q', 'L0_ffn_fc1_scales', 'L0_ffn_fc1_bias', 'L0_ffn_fc2_q', 'L0_ffn_fc2_scales',
        'L0_ffn_fc2_bias']


def kernel(**inputs):
    import concourse.bacc as bacc
    from concourse.bass_utils import run_bass_kernel_spmd

    nc = bacc.Bacc("TRN2", target_bir_lowering=False, num_devices=1, dynamic_dma_scratch_size=1024)
    arrays, args = {}, []
    for name in _INS:
        a = np.ascontiguousarray(inputs[name])
        arrays[f"in_{name}"] = a
        args.append(nc.dram_tensor(f"in_{name}", a.shape, mybir.dt.from_np(a.dtype), kind="ExternalInput").ap())
    out = nc.dram_tensor("out", arrays["in_x"].shape, F32, kind="ExternalOutput").ap()
    build(nc, *args, out)
    r = run_bass_kernel_spmd(nc, [arrays], core_ids=[0])
    return r.results[0]["out"]
```
